# Optimizing a Trainium2 kernel written in Bass

```python
import numpy as np
import jax
import jax.numpy as jnp

def _softmax(x, axis=-1):
    return jax.nn.softmax(x, axis=axis)

def _gelu(x):
    return jax.nn.gelu(x, approximate=True)

def _silu(x):
    return jax.nn.silu(x)

def _sigmoid(x):
    return jax.nn.sigmoid(x)

def _layernorm(x, axis=-1, eps=1e-05):
    m = jnp.mean(x, axis=axis, keepdims=True)
    v = jnp.var(x, axis=axis, keepdims=True)
    return (x - m) / jnp.sqrt(v + eps)

def _scatter_add(tgt, idx, src, axis=0):
    return tgt.at[idx].add(src)

def _segment_sum(src, seg, n):
    return jax.ops.segment_sum(src, seg, n)
kernel_name = 'mk_sandwich_d1_jaxref_r4_6f48b5'

def setup_inputs(seed: int=0):
    np.random.seed(seed)
    _w = jnp.asarray

    def _L0_attn_setup():
        import jax, jax.numpy as jnp
        import numpy as np
        D_MODEL, D_HIDDEN = (256, 512)
        B, L = (4, 1024)

        def _lin(x, w, b=None):
            y = jnp.einsum('bld,od->blo', x, w)
            return y if b is None else y + b

        def _depthwise_conv(x, conv_w, conv_b):
            lhs = jnp.transpose(x, (0, 2, 1))
            y = jax.lax.conv_general_dilated(lhs, conv_w, window_strides=(1,), padding=[(1, 1)], dimension_numbers=('NCH', 'OIH', 'NCH'), feature_group_count=D_MODEL)
            y = y + conv_b[None, :, None]
            return jnp.transpose(y, (0, 2, 1))
        key = jax.random.key(seed)
        ks = jax.random.split(key, 16)
        r = lambda k, shape, s: s * jax.random.normal(k, shape, dtype=jnp.float32)
        inp = {'x': r(ks[0], (B, L, D_MODEL), 1.0), 'w1': r(ks[1], (D_MODEL, D_MODEL), 0.02), 'w2': r(ks[2], (D_MODEL, D_MODEL), 0.02), 'w3': r(ks[3], (D_MODEL, D_MODEL), 0.02), 'conv_w': r(ks[4], (D_MODEL, 1, 3), 0.1), 'conv_b': r(ks[5], (D_MODEL,), 0.02), 'A_w': r(ks[6], (D_HIDDEN, D_MODEL), 0.001), 'A_b': jnp.ones((D_HIDDEN,), jnp.float32), 'B_w': r(ks[7], (D_HIDDEN, D_MODEL), 0.02), 'B_b': jnp.zeros((D_HIDDEN,), jnp.float32), 'C_w': r(ks[8], (D_MODEL, D_HIDDEN), 0.02), 'C_b': jnp.zeros((D_MODEL,), jnp.float32), 'D_w': r(ks[9], (D_MODEL, D_MODEL), 0.02), 'D_b': jnp.zeros((D_MODEL,), jnp.float32), 'dl_w': r(ks[10], (D_HIDDEN, D_MODEL), 0.001), 'dl_b': -5.0 * jnp.ones((D_HIDDEN,), jnp.float32)}
        return inp
    _L0_attn_in = _L0_attn_setup()

    def _L0_ffn_setup():
        import jax, jax.numpy as jnp
        import numpy as np
        B, S, D, F, E, K = (4, 512, 256, 1024, 8, 2)
        FS = 256
        LN_EPS = 1e-05

        def _swiglu(x, gu_w, dn_w):
            gate, up = jnp.split(x @ gu_w, 2, axis=-1)
            gate = jnp.clip(gate, -10.0, 10.0)
            return jax.nn.silu(gate) * up @ dn_w
        key = jax.random.key(seed)
        ks = jax.random.split(key, 6)
        s = 0.02
        return {'x': jax.random.normal(ks[0], (B, S, D), jnp.float32), 'ln_gamma': jnp.ones((D,), jnp.float32), 'ln_beta': jnp.zeros((D,), jnp.float32), 'router_w': jax.random.normal(ks[1], (D, E), jnp.float32) * s, 'gate_up_w': jax.random.normal(ks[2], (E, D, 2 * F), jnp.float32) * s, 'down_w': jax.random.normal(ks[3], (E, F, D), jnp.float32) * s, 'shared_gate_up_w': jax.random.normal(ks[4], (D, 2 * FS), jnp.float32) * s, 'shared_down_w': jax.random.normal(ks[5], (FS, D), jnp.float32) * s}
    _L0_ffn_in = _L0_ffn_setup()
    _d = {'L0_attn_x': _L0_attn_in['x'], 'L0_attn_w1': _L0_attn_in['w1'], 'L0_attn_w2': _L0_attn_in['w2'], 'L0_attn_w3': _L0_attn_in['w3'], 'L0_attn_conv_w': _L0_attn_in['conv_w'], 'L0_attn_conv_b': _L0_attn_in['conv_b'], 'L0_attn_A_w': _L0_attn_in['A_w'], 'L0_attn_A_b': _L0_attn_in['A_b'], 'L0_attn_B_w': _L0_attn_in['B_w'], 'L0_attn_B_b': _L0_attn_in['B_b'], 'L0_attn_C_w': _L0_attn_in['C_w'], 'L0_attn_C_b': _L0_attn_in['C_b'], 'L0_attn_D_w': _L0_attn_in['D_w'], 'L0_attn_D_b': _L0_attn_in['D_b'], 'L0_attn_dl_w': _L0_attn_in['dl_w'], 'L0_attn_dl_b': _L0_attn_in['dl_b'], 'L0_ffn_ln_gamma': _L0_ffn_in['ln_gamma'], 'L0_ffn_ln_beta': _L0_ffn_in['ln_beta'], 'L0_ffn_router_w': _L0_ffn_in['router_w'], 'L0_ffn_gate_up_w': _L0_ffn_in['gate_up_w'], 'L0_ffn_down_w': _L0_ffn_in['down_w'], 'L0_ffn_shared_gate_up_w': _L0_ffn_in['shared_gate_up_w'], 'L0_ffn_shared_down_w': _L0_ffn_in['shared_down_w']}
    _x0 = _d['L0_attn_x']
    _d['L0_attn_x'] = jax.random.normal(jax.random.fold_in(jax.random.key(seed), 1), (4, 1024, 256), dtype=_x0.dtype)
    del _x0
    return _d

def reference(L0_attn_x, L0_attn_w1, L0_attn_w2, L0_attn_w3, L0_attn_conv_w, L0_attn_conv_b, L0_attn_A_w, L0_attn_A_b, L0_attn_B_w, L0_attn_B_b, L0_attn_C_w, L0_attn_C_b, L0_attn_D_w, L0_attn_D_b, L0_attn_dl_w, L0_attn_dl_b, L0_ffn_ln_gamma, L0_ffn_ln_beta, L0_ffn_router_w, L0_ffn_gate_up_w, L0_ffn_down_w, L0_ffn_shared_gate_up_w, L0_ffn_shared_down_w):

    def _L0_attn_ref(x, w1, w2, w3, conv_w, conv_b, A_w, A_b, B_w, B_b, C_w, C_b, D_w, D_b, dl_w, dl_b):
        import jax, jax.numpy as jnp
        import numpy as np
        D_MODEL, D_HIDDEN = (256, 512)
        B, L = (4, 1024)

        def _lin(x, w, b=None):
            y = jnp.einsum('bld,od->blo', x, w)
            return y if b is None else y + b

        def _depthwise_conv(x, conv_w, conv_b):
            lhs = jnp.transpose(x, (0, 2, 1))
            y = jax.lax.conv_general_dilated(lhs, conv_w, window_strides=(1,), padding=[(1, 1)], dimension_numbers=('NCH', 'OIH', 'NCH'), feature_group_count=D_MODEL)
            y = y + conv_b[None, :, None]
            return jnp.transpose(y, (0, 2, 1))
        x = _lin(x, w1)
        x = _depthwise_conv(x, conv_w, conv_b)
        x = jax.nn.silu(x)
        x_delta = jax.nn.softplus(_lin(x, dl_w, dl_b))
        A_t = _lin(x, A_w, A_b)
        A_bar = jnp.exp(-x_delta * A_t)
        B_x = _lin(x, B_w, B_b)
        A_cum = jnp.cumprod(A_bar, axis=1)
        h = jnp.cumsum(B_x * A_cum, axis=1)
        ssm_out = _lin(h, C_w, C_b) + _lin(x, D_w, D_b)
        x_res = jax.nn.silu(_lin(ssm_out, w2))
        z = ssm_out * x_res
        out = ssm_out + _lin(z, w3)
        return out

    def _L0_ffn_ref(x, ln_gamma, ln_beta, router_w, gate_up_w, down_w, shared_gate_up_w, shared_down_w):
        import jax, jax.numpy as jnp
        import numpy as np
        B, S, D, F, E, K = (4, 512, 256, 1024, 8, 2)
        FS = 256
        LN_EPS = 1e-05

        def _swiglu(x, gu_w, dn_w):
            gate, up = jnp.split(x @ gu_w, 2, axis=-1)
            gate = jnp.clip(gate, -10.0, 10.0)
            return jax.nn.silu(gate) * up @ dn_w
        b, s, d = x.shape
        xf = x.reshape(-1, d)
        mu = jnp.mean(xf, axis=-1, keepdims=True)
        var = jnp.var(xf, axis=-1, keepdims=True)
        xn = (xf - mu) * jax.lax.rsqrt(var + LN_EPS) * ln_gamma + ln_beta
        logits = xn @ router_w
        probs = jax.nn.softmax(logits, axis=-1)
        topv, topi = jax.lax.top_k(probs, K)
        topv = topv / jnp.sum(topv, axis=-1, keepdims=True)
        comb = jnp.sum(jax.nn.one_hot(topi, E, dtype=xn.dtype) * topv[..., None], axis=1)
        out = jnp.zeros_like(xf)
        for e in range(E):
            out = out + comb[:, e:e + 1] * _swiglu(xn, gate_up_w[e], down_w[e])
        out = out + _swiglu(xn, shared_gate_up_w, shared_down_w)
        return out.reshape(b, s, d)
    x = L0_attn_x
    x = x + _layernorm(_L0_attn_ref(_layernorm(x, axis=-1), L0_attn_w1, L0_attn_w2, L0_attn_w3, L0_attn_conv_w, L0_attn_conv_b, L0_attn_A_w, L0_attn_A_b, L0_attn_B_w, L0_attn_B_b, L0_attn_C_w, L0_attn_C_b, L0_attn_D_w, L0_attn_D_b, L0_attn_dl_w, L0_attn_dl_b), axis=-1)
    x = x + _layernorm(_L0_ffn_ref(_layernorm(x, axis=-1), L0_ffn_ln_gamma, L0_ffn_ln_beta, L0_ffn_router_w, L0_ffn_gate_up_w, L0_ffn_down_w, L0_ffn_shared_gate_up_w, L0_ffn_shared_down_w), axis=-1)
    return x

_drawn_inputs = setup_inputs


def setup_inputs(seed=0):
    import zlib

    import numpy as np

    out = dict(_drawn_inputs(seed))
    spreads = {'L0_attn_A_b': (1.0, 0.2),
     'L0_attn_B_b': (0.0, 0.1),
     'L0_attn_C_b': (0.0, 0.1),
     'L0_attn_D_b': (0.0, 0.1),
     'L0_attn_dl_b': (-5.0, 0.2),
     'L0_ffn_ln_gamma': (1.0, 0.2),
     'L0_ffn_ln_beta': (0.0, 0.1)}
    factors = {'L0_attn_A_w': 52.368, 'L0_attn_D_w': 4.325, 'L0_attn_dl_w': 55.353}
    for name, (base, spread) in spreads.items():
        noise = np.random.default_rng([zlib.crc32(name.encode()), seed]).standard_normal(out[name].shape)
        drawn = base * np.exp(spread * noise) if base else spread * noise
        out[name] = jnp.asarray(drawn.astype(out[name].dtype))
    for name, factor in factors.items():
        out[name] = (out[name] * factor).astype(out[name].dtype)
    return out
```

```python
import concourse.bass as bass
from concourse import mybir
from contextlib import ExitStack

F32 = mybir.dt.float32
F32R = mybir.dt.float32r
I32 = mybir.dt.int32
ALU = mybir.AluOpType
ACT = mybir.ActivationFunctionType
AX = mybir.AxisListType

P = 128
B, L, D, H = 4, 1024, 256, 512
E, F, FS, K = 8, 1024, 256, 2
T = B * L
DC, HC, FC, SC = D // P, H // P, F // P, FS // P
HALF = 512
HT = HALF // P
LT = L // P
TT = T // P
EPS = 1e-5
CLIP = 10.0
EXP_CAP = 1e9

W1_AT, DL_AT, A_AT, B_AT = 0, DC * D, DC * (D + H), DC * (D + 2 * H)
C_AT = DC * (D + 3 * H)
DD_AT = C_AT + HC * D
W2_AT, W3_AT = DD_AT + DC * D, DD_AT + 2 * DC * D
W_COLS = W3_AT + DC * D
SGU_AT, SDN_AT = 0, DC * 2 * FS
RT_AT = SDN_AT + SC * D
S_COLS = RT_AT + DC * E
V_CW, V_CB = 0, 3 * DC
V_AB = V_CB + DC
V_BB, V_DLB = V_AB + HC, V_AB + 2 * HC
V_CDB = V_DLB + HC
V_G, V_BE = V_CDB + 2 * DC, V_CDB + 3 * DC
V_COLS = V_BE + DC


def split_weights(nc, weights, shared, consts, w_hi, w_lo, s_hi, s_lo, vec, ident, ident_r, zeros, ones, neg_half, eps):
    with ExitStack() as ctx:
        raw = ctx.enter_context(nc.sbuf_tensor("raw_w", [P, W_COLS], F32))
        raw_s = ctx.enter_context(nc.sbuf_tensor("raw_s", [P, S_COLS], F32))
        loaded = [ctx.enter_context(nc.semaphore(f"prep_loaded{i}")) for i in range(len(weights) + len(shared))]
        vec_loaded = ctx.enter_context(nc.semaphore("vec_loaded"))
        hi_ready = ctx.enter_context(nc.semaphore("prep_hi"))
        lo_ready = ctx.enter_context(nc.semaphore("prep_lo"))
        made = ctx.enter_context(nc.semaphore("consts_made"))
        block = ctx.enter_context(nc.Block())
        parts = []
        for at, src, chunks in weights:
            parts.append((raw, w_hi, w_lo, at, src, chunks))
        for at, src, chunks in shared:
            parts.append((raw_s, s_hi, s_lo, at, src, chunks))

        @block.sync
        def _(sp):
            for n, (r, hi, lo, at, src, chunks) in enumerate(parts):
                width = src.shape[1]
                sp.dma_start(r[:, at:at + chunks * width].rearrange("p (c n) -> p c n", c=chunks),
                             src.rearrange("(c p) n -> p c n", p=P)).then_inc(loaded[n], 16)
            sp.dma_start(vec[:, :], consts).then_inc(vec_loaded, 16)
            sp.wait_ge(vec_loaded, 16)

        @block.scalar
        def _(act):
            for n, (r, hi, lo, at, src, chunks) in enumerate(parts):
                cols = chunks * src.shape[1]
                act.wait_ge(loaded[n], 16)
                nc.scalar.activation(hi[:, at:at + cols], r[:, at:at + cols], ACT.Copy).then_inc(hi_ready, 1)
            act.wait_ge(made, 3)
            nc.scalar.activation(ident_r[:, :], ident[:, :], ACT.Copy)

        @block.vector
        def _(dve):
            nc.vector.memset(zeros[:, :], 0.0)
            nc.vector.memset(ones[:, :], 1.0)
            nc.vector.memset(neg_half[:, :], -0.5)
            nc.vector.memset(eps[:, :], EPS)
            for n, (r, hi, lo, at, src, chunks) in enumerate(parts):
                cols = chunks * src.shape[1]
                dve.wait_ge(hi_ready, n + 1)
                nc.vector.tensor_tensor(lo[:, at:at + cols], r[:, at:at + cols], hi[:, at:at + cols],
                                        ALU.subtract).then_inc(lo_ready, 1)
            dve.wait_ge(lo_ready, len(parts))

        @block.gpsimd
        def _(pool):
            nc.gpsimd.memset(ident[:, :], 0.0).then_inc(made, 1)
            pool.wait_ge(made, 1)
            nc.gpsimd.affine_select(out=ident[:, :], in_=ident[:, :], compare_op=ALU.not_equal, fill=1.0,
                                    base=0, pattern=[[-1, P]], channel_multiplier=1).then_inc(made, 2)


def mixer(nc, x, xs_dram, cleared, x1_dram, n_dram, ys_dram, logits, w_hi, w_lo, s_hi, s_lo, vec, ident, ident_r, zeros, ones, neg_half, eps):
    with ExitStack() as ctx:
        def sb(name, shape, dt=F32):
            return ctx.enter_context(nc.sbuf_tensor(name, shape, dt))

        def sem(name):
            return ctx.enter_context(nc.semaphore(name))

        x_in = sb("x_in", [P, LT, D])
        xt_hi = sb("xt_hi", [P, DC, L], F32R)
        xt_lo = sb("xt_lo", [P, DC, L], F32R)
        u = sb("u", [P, DC, L + 2])
        cv = sb("cv", [P, DC, L])
        xs_hi = sb("xs_hi", [P, DC, L], F32R)
        xs_lo = sb("xs_lo", [P, DC, L], F32R)
        delta = sb("delta", [P, 2, HALF])
        decay = sb("decay", [P, 2, HALF])
        a_cum = sb("a_cum", [P, HALF])
        bx = sb("bx", [P, HALF])
        h = sb("h", [P, 2, HALF])
        carry_a = sb("carry_a", [P, HC])
        carry_h = sb("carry_h", [P, HC])
        h_hi = sb("h_hi", [P, HC, HALF], F32R)
        h_lo = sb("h_lo", [P, HC, HALF], F32R)
        s = sb("s", [P, DC, HALF])
        s_out_hi = sb("s_out_hi", [P, DC, HALF], F32R)
        s_out_lo = sb("s_out_lo", [P, DC, HALF], F32R)
        g = sb("g", [P, DC, HALF])
        z_hi = sb("z_hi", [P, DC, HALF], F32R)
        z_lo = sb("z_lo", [P, DC, HALF], F32R)
        xr = sb("xr", [P, HT, D])
        xnt_hi = sb("xnt_hi", [P, DC, HALF], F32R)
        xnt_lo = sb("xnt_lo", [P, DC, HALF], F32R)
        y_n = sb("y_n", [P, HT, D])
        n2 = sb("n2", [P, HT, D])
        cdb = sb("cdb", [P, DC])
        st = sb("st", [P, LT, 6])
        mv = sb("mv", [P, LT, 2])
        ve = sb("ve", [P, LT])
        rs = sb("rs", [P, LT])
        st2 = sb("st2", [P, 2 * HT, 6])
        mv2 = sb("mv2", [P, 2 * HT, 2])
        ve2 = sb("ve2", [P, HT])
        rs2 = sb("rs2", [P, HT])
        ve3 = sb("ve3", [P, HT])
        rs3 = sb("rs3", [P, HT])
        ve4 = sb("ve4", [P, HT])
        rs4 = sb("rs4", [P, HT])
        banks = [ctx.enter_context(nc.psum_tensor(f"bank{i}", [P, HALF], F32)) for i in range(8)]

        x_loaded = sem("x_loaded")
        xr_loaded = sem("xr_loaded")
        x1_stored, n_stored, ys_stored = sem("x1_stored"), sem("n_stored"), sem("ys_stored")
        stats_seen, sp_seen = sem("stats_seen"), sem("sp_seen")
        a_order, d_order, start_made = sem("a_order"), sem("d_order"), sem("start_made")
        pool_a, pool_d = sem("pool_a"), sem("pool_d")
        mv_ready, rs_ready, xn_ready = sem("mv_ready"), sem("rs_ready"), sem("xn_ready")
        t1_done, xt_hi_ready, xt_lo_ready = sem("t1_done"), sem("xt_hi_ready"), sem("xt_lo_ready")
        u_done, u_copied, cv0_ready, cv_ready = sem("u_done"), sem("u_copied"), sem("cv0_ready"), sem("cv_ready")
        silu_ready, xs_hi_ready, xs_lo_ready = sem("silu_ready"), sem("xs_hi_ready"), sem("xs_lo_ready")
        dl_done, a_done, b_done = sem("dl_done"), sem("a_done"), sem("b_done")
        exp_ready, capped, ln_ready = sem("exp_ready"), sem("capped"), sem("ln_ready")
        delta_ready, da_ready, abar_ready = sem("delta_ready"), sem("da_ready"), sem("abar_ready")
        acum_ready, bx_ready, h_ready = sem("acum_ready"), sem("bx_ready"), sem("h_ready")
        carried, h_hi_ready, h_lo_ready = sem("carried"), sem("h_hi_ready"), sem("h_lo_ready")
        s_done, s_ready, s_hi_ready, s_lo_ready = sem("s_done"), sem("s_ready"), sem("s_hi_ready"), sem("s_lo_ready")
        g_done, g_ready, z_ready = sem("g_done"), sem("g_ready"), sem("z_ready")
        z_hi_ready, z_lo_ready, w3_done = sem("z_hi_ready"), sem("z_lo_ready"), sem("w3_done")
        mv2_ready, rs2_ready, yn_ready = sem("mv2_ready"), sem("rs2_ready"), sem("yn_ready")
        x1_ready, mv3_ready, rs4_ready, n2_ready = sem("x1_ready"), sem("mv3_ready"), sem("rs4_ready"), sem("n2_ready")
        t2_done, xn_hi_ready, xn_f_ready, xn_lo_ready = sem("t2_done"), sem("xn_hi_ready"), sem("xn_f_ready"), sem("xn_lo_ready")
        router_done, logits_ready = sem("router_done"), sem("logits_ready")
        gate_done, up_done, clipped, sg_ready = sem("gate_done"), sem("up_done"), sem("clipped"), sem("sg_ready")
        hs_ready, hs_hi_ready, hs_lo_ready = sem("hs_ready"), sem("hs_hi_ready"), sem("hs_lo_ready")
        sd_done, ys_ready = sem("sd_done"), sem("ys_ready")
        block = ctx.enter_context(nc.Block())

        UNITS = [(half, j) for half in range(2) for j in range(HC)]
        NU = len(UNITS)
        HH = ((h_hi, h_lo), (xt_hi[:, :, :].rearrange("p c (a l) -> p (c a) l", l=HALF),
                             xt_lo[:, :, :].rearrange("p c (a l) -> p (c a) l", l=HALF)))
        S_BANKS = ((6, 7), (4, 5))
        U_BANKS = (0, 1, 2, 3)

        BESIDE_A = [([(1, 1)], []), ([], [(0, 9), (0, 10)]), ([], [(0, 11), (0, 12)]), ([], [(0, 13), (0, 14)]),
                    ([], [(1, 2), (1, 3)]), ([], [(1, 4), (1, 5)])]
        BESIDE_C = [[(1, 6)], [(1, 7)], [(1, 8)], [(1, 9), (1, 10)], [(1, 11), (1, 12)], [(1, 13), (1, 14)],
                    [(0, 1), (0, 2)], [(0, 3), (0, 4)], [(0, 5), (0, 6)], [(0, 7), (0, 8)]]

        def run(eng, a_stage, c_step, d_stage):
            def turn(b, first):
                for a in range(6):
                    if not first:
                        for half, d in BESIDE_A[a][0]:
                            d_stage(b * 2 - 2 + half, half, d)
                    a_stage(b, a)
                    if not first:
                        for half, d in BESIDE_A[a][1]:
                            d_stage(b * 2 - 2 + half, half, d)
                for n in range(NU + 2):
                    c_step(b, n)
                    for half, d in BESIDE_C[n]:
                        if half == 0:
                            d_stage(b * 2, 0, d)
                        elif not first:
                            d_stage(b * 2 - 1, 1, d)

            turn(0, True)
            with eng.Fori(1, B) as b:
                turn(b, False)
            for half, d in [(1, 1)] + [(0, i) for i in range(9, 15)] + [(1, i) for i in range(2, 15)]:
                d_stage(2 * B - 2 + half, half, d)

        def W(hi_lo, at, c, width, lo=0, n=P):
            return hi_lo[:, at + c * width + lo:at + c * width + lo + n]

        @block.sync
        def _(sp):
            def load_x(b):
                sp.dma_start(x_in[:, :, :], x[b, :, :].rearrange("(t p) d -> p t d", p=P)).then_inc(x_loaded, 16)

            def clear(b):
                for j in range(CLEARS):
                    sp.dma_start(xs_dram.rearrange("(b n) d -> b (n d)", b=B).rearrange(
                        "b (j p m) -> b j p m", j=CLEARS, p=P)[b, j, :, :], zeros[:, 0:CLEAR_N]).then_inc(cleared, 16)

            def passed(semaphore, value):
                sp.wait_ge(semaphore, value)
                sp.sem_inc(sp_seen, 1)

            def half_dmas(b, half):
                k = b * 2 + half
                rows = slice(half * HALF, (half + 1) * HALF)
                passed(x1_stored, k * 16 + 16)
                passed(n2_ready, k + 1)
                sp.dma_start(xr[:, :, :], x[b, rows, :].rearrange("(t p) d -> p t d", p=P)).then_inc(xr_loaded, 16)
                passed(x1_ready, k + 1)
                sp.dma_start(x1_dram[b, rows, :].rearrange("(t p) d -> p t d", p=P), xr[:, :, :]).then_inc(x1_stored, 16)
                passed(n2_ready, k + 2)
                sp.dma_start(n_dram[b, rows, :].rearrange("(t p) d -> p t d", p=P), n2[:, :, :]).then_inc(n_stored, 16)
                passed(ys_ready, 2 * k + 4)
                sp.dma_start(ys_dram[b, rows, :].rearrange("(t p) d -> p t d", p=P), y_n[:, :, :]).then_inc(ys_stored, 16)

            load_x(0)
            clear(0)
            with sp.Fori(1, B) as b:
                passed(t1_done, b * 4)
                load_x(b)
                clear(b)
                for half in range(2):
                    half_dmas(b - 1, half)
            for half in range(2):
                half_dmas(B - 1, half)
            sp.wait_ge(x1_stored, 16 + 32 * B)
            sp.wait_ge(n_stored, 16 + 32 * B)
            sp.wait_ge(ys_stored, 16 + 32 * B)

        @block.tensor
        def _(pe):
            def product(out, hi, lo, x_hi, x_lo, first, last):
                nc.tensor.matmul(out, hi, x_hi, start=first, stop=False)
                nc.tensor.matmul(out, hi, x_lo, start=False, stop=False)
                return nc.tensor.matmul(out, lo, x_hi, start=False, stop=last)

            def product_t(out, x_hi, x_lo, hi, lo, first, last):
                nc.tensor.matmul(out, x_hi, hi, start=first, stop=False)
                nc.tensor.matmul(out, x_hi, lo, start=False, stop=False)
                return nc.tensor.matmul(out, x_lo, hi, start=False, stop=last)

            def a_stage(b, a):
                if a == 1:
                    pe.wait_ge(xn_ready, b + 1)
                    pe.wait_ge(bx_ready, b * NU + 2)
                    for n in range(4):
                        half, c = n // 2, n % 2
                        for t in range(HT):
                            i = nc.tensor.transpose(banks[n][:, t * P:(t + 1) * P],
                                                    x_in[:, half * HT + t, c * P:(c + 1) * P], ident[:, :])
                        i.then_inc(t1_done, 1)
                if a == 2:
                    for n in range(4):
                        half, o = n // 2, n % 2
                        cols = slice(half * HALF, (half + 1) * HALF)
                        pe.wait_ge(xt_lo_ready, b * 4 + 2 * half + 2)
                        for c in range(DC):
                            i = product(banks[U_BANKS[n]][:, :], W(w_hi, W1_AT, c, D, o * P), W(w_lo, W1_AT, c, D, o * P),
                                        xt_hi[:, c, cols], xt_lo[:, c, cols], c == 0, c == DC - 1)
                        i.then_inc(u_done, 1)

            def dl_a(b, n):
                half, j = UNITS[n]
                cols = slice(half * HALF, (half + 1) * HALF)
                for at, bank, done, free in ((DL_AT, n % 2, dl_done, delta_ready), (A_AT, 2 + n % 2, a_done, da_ready)):
                    pe.wait_ge(free, b * NU + n + 1)
                    for c in range(DC):
                        i = product(banks[bank][:, :], W(w_hi, at, c, H, j * P), W(w_lo, at, c, H, j * P),
                                    xs_hi[:, c, cols], xs_lo[:, c, cols], c == 0, c == DC - 1)
                    i.then_inc(done, 1)

            def b_unit(b, n):
                half, j = UNITS[n]
                cols = slice(half * HALF, (half + 1) * HALF)
                pe.wait_ge(bx_ready, b * NU + n + 1)
                if n == 0 and not (isinstance(b, int) and b == 0):
                    pe.wait_ge(s_hi_ready, b * 4)
                for c in range(DC):
                    i = product(banks[4 + n % 2][:, :], W(w_hi, B_AT, c, H, j * P), W(w_lo, B_AT, c, H, j * P),
                                xs_hi[:, c, cols], xs_lo[:, c, cols], c == 0, c == DC - 1)
                i.then_inc(b_done, 1)

            def c_step(b, n):
                if n == 0:
                    pe.wait_ge(u_copied, b * 4 + 4)
                    pe.wait_ge(xs_lo_ready, b + 1)
                if n < NU:
                    dl_a(b, n)
                if 1 <= n <= NU:
                    b_unit(b, n - 1)

            def gate_up(k, f):
                for bank, lo, done in ((6, f * P, gate_done), (7, FS + f * P, up_done)):
                    for c in range(DC):
                        i = product(banks[bank][:, :], W(s_hi, SGU_AT, c, 2 * FS, lo),
                                    W(s_lo, SGU_AT, c, 2 * FS, lo), xnt_hi[:, c, :], xnt_lo[:, c, :],
                                    c == 0, c == DC - 1)
                    i.then_inc(done, 1)

            def d_stage(k, half, d):
                if d == 1:
                    cols = slice(half * HALF, (half + 1) * HALF)
                    if half == 0:
                        pe.wait_ge(ys_ready, k * 2 + 2)
                    else:
                        pe.wait_ge(bx_ready, (k - 1) * (NU // 2) + NU + 2)
                    for o in range(DC):
                        out = banks[S_BANKS[half][o]][:, :]
                        for c in range(DC):
                            product(out, W(w_hi, DD_AT, c, D, o * P), W(w_lo, DD_AT, c, D, o * P),
                                    xs_hi[:, c, cols], xs_lo[:, c, cols], c == 0, False)
                        if o == 0:
                            pe.wait_ge(h_lo_ready, k * HC + HC + 2)
                        for c in range(HC):
                            i = product(out, W(w_hi, C_AT, c, D, o * P), W(w_lo, C_AT, c, D, o * P),
                                        HH[half][0][:, c, :], HH[half][1][:, c, :], False, c == HC - 1)
                        i.then_inc(s_done, 1)
                if d == 2:
                    pe.wait_ge(s_lo_ready, k + 1)
                    pe.wait_ge(s_hi_ready, 2 * k + 2)
                    pe.wait_ge(ys_ready, k * 2 + 2)
                    for o in range(DC):
                        for c in range(DC):
                            i = product(banks[6 + o][:, :], W(w_hi, W2_AT, c, D, o * P), W(w_lo, W2_AT, c, D, o * P),
                                        s_out_hi[:, c, :], s_out_lo[:, c, :], c == 0, c == DC - 1)
                        i.then_inc(g_done, 1)
                if d == 4:
                    pe.wait_ge(g_ready, 2 * k + 2)
                    pe.wait_ge(z_lo_ready, k + 1)
                    for t in range(HT):
                        at = (t % 2) * D
                        out = banks[6 + t // 2][:, at:at + D]
                        toks = slice(t * P, (t + 1) * P)
                        for c in range(DC):
                            w3 = slice(W3_AT + c * D, W3_AT + (c + 1) * D)
                            product_t(out, z_hi[:, c, toks], z_lo[:, c, toks], w_hi[:, w3], w_lo[:, w3], c == 0, False)
                        for c in range(DC):
                            part = banks[6 + t // 2][:, at + c * P:at + (c + 1) * P]
                            nc.tensor.matmul(part, s_out_hi[:, c, toks], ident_r[:, :], start=False, stop=False)
                            i = nc.tensor.matmul(part, s_out_lo[:, c, toks], ident_r[:, :], start=False, stop=c == DC - 1)
                        i.then_inc(w3_done, 1)
                if d == 7:
                    pe.wait_ge(n2_ready, k + 2)
                    for c in range(DC):
                        for t in range(HT):
                            i = nc.tensor.transpose(banks[6 + c][:, t * P:(t + 1) * P], n2[:, t, c * P:(c + 1) * P],
                                                    ident[:, :])
                        i.then_inc(t2_done, 1)
                if d == 8:
                    pe.wait_ge(xn_lo_ready, 2 * k + 2)
                    for t in range(HT):
                        toks = slice(t * P, (t + 1) * P)
                        for c in range(DC):
                            rt = slice(RT_AT + c * E, RT_AT + (c + 1) * E)
                            i = product_t(banks[6][:, t * E:(t + 1) * E], xnt_hi[:, c, toks], xnt_lo[:, c, toks],
                                          s_hi[:, rt], s_lo[:, rt], c == 0, c == DC - 1)
                    i.then_inc(router_done, 1)
                if d == 9:
                    pe.wait_ge(logits_ready, k + 1)
                    gate_up(k, 0)
                if d == 11:
                    pe.wait_ge(hs_ready, 2 * k + 1)
                    gate_up(k, 1)
                if d == 13:
                    pe.wait_ge(hs_lo_ready, 2 * k + 2)
                    for t in range(HT):
                        toks = slice(t * P, (t + 1) * P)
                        for f in range(SC):
                            dn = slice(SDN_AT + f * D, SDN_AT + (f + 1) * D)
                            i = product_t(banks[6 + t // 2][:, (t % 2) * D:(t % 2 + 1) * D], z_hi[:, f, toks],
                                          z_lo[:, f, toks], s_hi[:, dn], s_lo[:, dn], f == 0, f == SC - 1)
                        i.then_inc(sd_done, 1)

            run(pe, a_stage, c_step, d_stage)

        @block.scalar
        def _(act):
            def a_stage(b, a):
                if a == 1:
                    act.wait_ge(s_done, b * 4 + 2)
                    for n in range(4):
                        half, c = n // 2, n % 2
                        act.wait_ge(t1_done, b * 4 + n + 1)
                        nc.scalar.activation(xt_hi[:, c, half * HALF:(half + 1) * HALF], banks[n][:, :],
                                             ACT.Copy).then_inc(xt_hi_ready, 1)
                if a == 2:
                    act.wait_ge(cv_ready, b * 2 + 2)
                    for n in range(4):
                        half, o = n // 2, n % 2
                        act.wait_ge(u_done, b * 4 + n + 1)
                        nc.scalar.activation(u[:, o, 1 + half * HALF:1 + (half + 1) * HALF],
                                             banks[U_BANKS[n]][:, :], ACT.Copy).then_inc(u_copied, 1)
                if a == 3:
                    for o in range(DC):
                        act.wait_ge(u_copied, b * 4 + 3 + o)
                        nc.scalar.activation(cv[:, o, :], u[:, o, 1:L + 1], ACT.Identity,
                                             bias=vec[:, V_CB + o:V_CB + o + 1],
                                             scale=vec[:, V_CW + 3 * o + 1:V_CW + 3 * o + 2]).then_inc(cv0_ready, 1)
                if a == 4:
                    for o in range(DC):
                        act.wait_ge(cv_ready, b * 2 + o + 3)
                        nc.scalar.activation(cv[:, o, :], cv[:, o, :], ACT.Silu).then_inc(silu_ready, 1)
                    for o in range(DC):
                        act.wait_ge(silu_ready, b * 2 + o + 1)
                        nc.scalar.activation(xs_hi[:, o, :], cv[:, o, :], ACT.Copy).then_inc(xs_hi_ready, 1)

            def c_step(b, n):
                if n == 0 or any(d in (2, 9, 11) for _, d in BESIDE_C[n - 1]):
                    act.preload_act_table_set("natural_log_exp_and_others")
                if n < NU:
                    half, j = UNITS[n]
                    act.wait_ge(dl_done, b * NU + n + 1)
                    act.wait_ge(da_ready, b * NU + n + 1)
                    nc.scalar.activation(delta[:, n % 2, :], banks[n % 2][:, :], ACT.Exp,
                                         bias=vec[:, V_DLB + j:V_DLB + j + 1]).then_inc(exp_ready, 1)
                if 1 <= n <= NU:
                    act.wait_ge(da_ready, b * NU + n - 1 + 3)
                    nc.scalar.activation(decay[:, (n - 1) % 2, :], decay[:, (n - 1) % 2, :], ACT.Exp,
                                         scale=-1.0).then_inc(abar_ready, 1)
                if n < NU:
                    act.wait_ge(capped, b * NU + n + 1)
                    nc.scalar.activation(delta[:, n % 2, :], delta[:, n % 2, :], ACT.Ln, bias=1.0).then_inc(ln_ready, 1)
                if n >= 2:
                    half, j = UNITS[n - 2]
                    act.wait_ge(h_ready, b * NU + n - 2 + 1)
                    nc.scalar.activation(HH[half][0][:, j, :], h[:, n % 2, :], ACT.Copy).then_inc(h_hi_ready, 1)

            def d_stage(k, half, d):
                if d == 1:
                    act.wait_ge(w3_done, k * 4 + 4)
                    for o in range(DC):
                        act.wait_ge(s_done, 2 * k + o + 3)
                        bank = banks[S_BANKS[half][o]]
                        nc.scalar.activation(s[:, o, :], bank[:, :], ACT.Identity, bias=cdb[:, o:o + 1]).then_inc(s_ready, 1)
                        nc.scalar.activation(s_out_hi[:, o, :], bank[:, :], ACT.Identity,
                                             bias=cdb[:, o:o + 1]).then_inc(s_hi_ready, 1)
                if d == 2:
                    for o in range(DC):
                        act.wait_ge(g_done, 2 * k + o + 1)
                        nc.scalar.activation(g[:, o, :], banks[6 + o][:, :], ACT.Silu).then_inc(g_ready, 1)
                if d == 3:
                    act.wait_ge(z_ready, k + 1)
                    nc.scalar.activation(z_hi[:, :, :], g[:, :, :], ACT.Copy).then_inc(z_hi_ready, 1)
                if d == 7:
                    for c in range(DC):
                        act.wait_ge(t2_done, 2 * k + c + 1)
                        nc.scalar.activation(xnt_hi[:, c, :], banks[6 + c][:, :], ACT.Identity,
                                             bias=vec[:, V_BE + c:V_BE + c + 1],
                                             scale=vec[:, V_G + c:V_G + c + 1]).then_inc(xn_hi_ready, 1)
                if d in (9, 11):
                    f = (d - 9) // 2
                    act.wait_ge(clipped, 2 * k + f + 1)
                    nc.scalar.activation(g[:, f, :], g[:, f, :], ACT.Silu).then_inc(sg_ready, 1)
                if d in (10, 12):
                    f = (d - 10) // 2
                    act.wait_ge(hs_ready, 2 * k + f + 1)
                    nc.scalar.activation(z_hi[:, f, :], g[:, f, :], ACT.Copy).then_inc(hs_hi_ready, 1)
                if d == 14:
                    for t in range(2):
                        act.wait_ge(sd_done, k * 4 + 2 * t + 2)
                        nc.scalar.activation(y_n[:, 2 * t:2 * t + 2, :].rearrange("p t d -> p (t d)"),
                                             banks[6 + t][:, :], ACT.Copy).then_inc(ys_ready, 1)

            act.sem_inc(ys_ready, 2)
            run(act, a_stage, c_step, d_stage)

        @block.vector
        def _(dve):
            def moments(source, stats, out, n, order, count, ready):
                for t in range(n):
                    i = nc.vector.bn_stats(stats[:, t, :], source(t))
                i.then_inc(order, 1)
                dve.wait_ge(order, count)
                dve.sem_inc(stats_seen, 1)
                for t in range(n):
                    i = nc.vector.bn_aggr(out[:, t, :], stats[:, t, :])
                i.then_inc(ready, 1)

            def a_stage(b, a):
                if a == 0:
                    dve.wait_ge(x_loaded, b * 16 + 16)
                    moments(lambda t: x_in[:, t, :], st, mv, LT, a_order, b * 3 + 1, mv_ready)
                    dve.wait_ge(mv_ready, b + 1)
                    dve.wait_ge(rs_ready, b + 1)
                    for t in range(LT):
                        i = nc.vector.tensor_scalar(x_in[:, t, :], x_in[:, t, :], mv[:, t, 0:1], rs[:, t:t + 1],
                                                    ALU.subtract, ALU.mult)
                    i.then_inc(xn_ready, 1)
                if a == 1:
                    for n in range(4):
                        half, c = n // 2, n % 2
                        dve.wait_ge(xt_hi_ready, b * 4 + n + 1)
                        cols = slice(half * HALF, (half + 1) * HALF)
                        nc.vector.tensor_tensor(xt_lo[:, c, cols], banks[n][:, :], xt_hi[:, c, cols],
                                                ALU.subtract).then_inc(xt_lo_ready, 1)
                if a == 3:
                    for o in range(DC):
                        dve.wait_ge(cv0_ready, b * 2 + o + 1)
                        nc.vector.scalar_tensor_tensor(out=cv[:, o, :], in0=u[:, o, 0:L],
                                                       scalar=vec[:, V_CW + 3 * o:V_CW + 3 * o + 1],
                                                       in1=cv[:, o, :], op0=ALU.mult, op1=ALU.add).then_inc(a_order, 1)
                        dve.wait_ge(a_order, b * 3 + 2 + o)
                        nc.vector.scalar_tensor_tensor(out=cv[:, o, :], in0=u[:, o, 2:L + 2],
                                                       scalar=vec[:, V_CW + 3 * o + 2:V_CW + 3 * o + 3],
                                                       in1=cv[:, o, :], op0=ALU.mult, op1=ALU.add).then_inc(cv_ready, 1)
                if a == 5:
                    dve.wait_ge(xs_hi_ready, b * 2 + 2)
                    nc.vector.tensor_tensor(xs_lo[:, :, :], cv[:, :, :], xs_hi[:, :, :], ALU.subtract).then_inc(xs_lo_ready, 1)

            def c_step(b, n):
                if n < NU:
                    dve.wait_ge(exp_ready, b * NU + n + 1)
                    nc.vector.tensor_scalar(delta[:, n % 2, :], delta[:, n % 2, :], EXP_CAP, None, ALU.min).then_inc(capped, 1)
                if 1 <= n <= NU:
                    m = n - 1
                    half, j = UNITS[m]
                    dve.wait_ge(ln_ready, b * NU + m + 1)
                    nc.vector.scalar_tensor_tensor(out=delta[:, m % 2, :], in0=banks[m % 2][:, :],
                                                   scalar=vec[:, V_DLB + j:V_DLB + j + 1], in1=delta[:, m % 2, :],
                                                   op0=ALU.add, op1=ALU.max).then_inc(delta_ready, 1)
                    dve.wait_ge(delta_ready, b * NU + m + 3)
                    dve.wait_ge(a_done, b * NU + m + 1)
                    nc.vector.scalar_tensor_tensor(out=decay[:, m % 2, :], in0=banks[2 + m % 2][:, :],
                                                   scalar=vec[:, V_AB + j:V_AB + j + 1], in1=delta[:, m % 2, :],
                                                   op0=ALU.add, op1=ALU.mult).then_inc(da_ready, 1)
                if n >= 2:
                    m = n - 2
                    half, j = UNITS[m]
                    dve.wait_ge(abar_ready, b * NU + m + 1)
                    first = half == 0
                    if 1 <= m < HC:
                        dve.wait_ge(carried, b * 2 * HC + 2 * m - 1)
                    if m == HC:
                        dve.wait_ge(carried, b * 2 * HC + 2 * HC)
                    nc.vector.tensor_tensor_scan(a_cum[:, :], decay[:, m % 2, :], zeros[:, 0:HALF],
                                                 1.0 if first else carry_a[:, j:j + 1], ALU.mult, ALU.add).then_inc(acum_ready, 1)
                    dve.wait_ge(acum_ready, b * NU + m + 1)
                    dve.wait_ge(b_done, b * NU + m + 1)
                    nc.vector.scalar_tensor_tensor(out=bx[:, :], in0=banks[4 + m % 2][:, :],
                                                   scalar=vec[:, V_BB + j:V_BB + j + 1], in1=a_cum[:, :],
                                                   op0=ALU.add, op1=ALU.mult).then_inc(bx_ready, 1)
                    dve.wait_ge(bx_ready, b * NU + m + 3)
                    dve.wait_ge(h_lo_ready, b * NU + m + 1)
                    nc.vector.tensor_tensor_scan(h[:, m % 2, :], ones[:, 0:HALF], bx[:, :],
                                                 0.0 if first else carry_h[:, j:j + 1], ALU.mult, ALU.add).then_inc(h_ready, 1)

            def d_stage(k, half, d):
                if d == 2:
                    dve.wait_ge(s_hi_ready, 2 * k + 2)
                    nc.vector.tensor_tensor(s_out_lo[:, :, :], s[:, :, :], s_out_hi[:, :, :], ALU.subtract).then_inc(s_lo_ready, 1)
                if d == 3:
                    dve.wait_ge(g_ready, 2 * k + 2)
                    nc.vector.tensor_tensor(g[:, :, :], s[:, :, :], g[:, :, :], ALU.mult).then_inc(z_ready, 1)
                if d == 4:
                    dve.wait_ge(z_hi_ready, k + 1)
                    nc.vector.tensor_tensor(z_lo[:, :, :], g[:, :, :], z_hi[:, :, :], ALU.subtract).then_inc(z_lo_ready, 1)
                out = lambda t: banks[6 + t // 2][:, (t % 2) * D:(t % 2 + 1) * D]
                if d == 5:
                    dve.wait_ge(w3_done, k * 4 + 8)
                    moments(out, st2, mv2, HT, d_order, k * 2 + 1, mv2_ready)
                if d == 6:
                    dve.wait_ge(rs2_ready, k + 1)
                    dve.wait_ge(ys_stored, k * 16 + 16)
                    for t in range(HT):
                        i = nc.vector.tensor_scalar(y_n[:, t, :], out(t), mv2[:, t, 0:1], rs2[:, t:t + 1],
                                                    ALU.subtract, ALU.mult)
                    i.then_inc(yn_ready, 1)
                    dve.wait_ge(yn_ready, k + 1)
                    dve.wait_ge(xr_loaded, k * 16 + 16)
                    nc.vector.tensor_tensor(xr[:, :, :], xr[:, :, :], y_n[:, :, :], ALU.add).then_inc(x1_ready, 1)
                    dve.wait_ge(x1_ready, k + 1)
                    moments(lambda t: xr[:, t, :], st2[:, HT:, :], mv2[:, HT:, :], HT, d_order, k * 2 + 2, mv3_ready)
                if d == 7:
                    dve.wait_ge(rs4_ready, k + 1)
                    dve.wait_ge(n_stored, k * 16 + 16)
                    for t in range(HT):
                        i = nc.vector.tensor_scalar(n2[:, t, :], xr[:, t, :], mv2[:, HT + t, 0:1], rs4[:, t:t + 1],
                                                    ALU.subtract, ALU.mult)
                    i.then_inc(n2_ready, 1)
                if d == 8:
                    for c in range(DC):
                        dve.wait_ge(xn_hi_ready, 2 * k + c + 1)
                        nc.vector.tensor_scalar(g[:, c, :], banks[6 + c][:, :], vec[:, V_G + c:V_G + c + 1],
                                                vec[:, V_BE + c:V_BE + c + 1], ALU.mult, ALU.add).then_inc(xn_f_ready, 1)
                        dve.wait_ge(xn_f_ready, 2 * k + c + 1)
                        nc.vector.tensor_tensor(xnt_lo[:, c, :], g[:, c, :], xnt_hi[:, c, :],
                                                ALU.subtract).then_inc(xn_lo_ready, 1)
                if d == 9:
                    dve.wait_ge(router_done, k + 1)
                    nc.vector.tensor_copy(logits[:, bass.ds(k * HT * E, HT * E)], banks[6][:, 0:HT * E]).then_inc(logits_ready, 1)
                if d in (9, 11):
                    f = (d - 9) // 2
                    dve.wait_ge(gate_done, 2 * k + f + 1)
                    nc.vector.tensor_scalar(g[:, f, :], banks[6][:, :], CLIP, -CLIP, ALU.min, ALU.max).then_inc(clipped, 1)
                if d in (10, 12):
                    f = (d - 10) // 2
                    dve.wait_ge(sg_ready, 2 * k + f + 1)
                    dve.wait_ge(up_done, 2 * k + f + 1)
                    nc.vector.tensor_tensor(g[:, f, :], banks[7][:, :], g[:, f, :], ALU.mult).then_inc(hs_ready, 1)
                if d in (11, 13):
                    f = (d - 11) // 2
                    dve.wait_ge(hs_hi_ready, 2 * k + f + 1)
                    nc.vector.tensor_tensor(z_lo[:, f, :], g[:, f, :], z_hi[:, f, :], ALU.subtract).then_inc(hs_lo_ready, 1)

            for pad in (0, L + 1):
                nc.vector.memset(u[:, :, pad:pad + 1], 0.0)
            nc.vector.tensor_tensor(cdb[:, :], vec[:, V_CDB:V_CDB + DC], vec[:, V_CDB + DC:V_CDB + 2 * DC],
                                    ALU.add).then_inc(start_made, 1)
            dve.wait_ge(start_made, 1)
            dve.sem_inc(delta_ready, 2)
            dve.sem_inc(da_ready, 2)
            dve.sem_inc(bx_ready, 2)
            dve.sem_inc(cv_ready, 2)
            dve.sem_inc(n2_ready, 1)
            run(dve, a_stage, c_step, d_stage)

        @block.gpsimd
        def _(pool):
            def chain(order, first, steps):
                for n, (out, x0, x1, op) in enumerate(steps):
                    i = nc.gpsimd.tensor_tensor(out, x0, x1, op)
                    if n < len(steps) - 1:
                        i.then_inc(order, 1)
                        pool.wait_ge(order, first + n + 1)
                return i

            def a_stage(b, a):
                if a == 0:
                    pool.wait_ge(mv_ready, b + 1)
                    chain(pool_a, b, [(ve[:, :], mv[:, :, 1], eps[:, 0:LT], ALU.add),
                                      (rs[:, :], ve[:, :], neg_half[:, 0:LT], ALU.pow)]).then_inc(rs_ready, 1)

            def c_step(b, n):
                if n >= 2:
                    m = n - 2
                    half, j = UNITS[m]
                    if half == 0:
                        pool.wait_ge(acum_ready, b * NU + m + 1)
                        nc.gpsimd.tensor_tensor(carry_a[:, j:j + 1], a_cum[:, HALF - 1:HALF], ones[:, 0:1],
                                                ALU.mult).then_inc(carried, 1)
                        pool.wait_ge(h_ready, b * NU + m + 1)
                        nc.gpsimd.tensor_tensor(carry_h[:, j:j + 1], h[:, m % 2, HALF - 1:HALF], ones[:, 0:1],
                                                ALU.mult).then_inc(carried, 1)
                    pool.wait_ge(h_hi_ready, b * NU + m + 1)
                    nc.gpsimd.tensor_tensor(HH[half][1][:, j, :], h[:, m % 2, :], HH[half][0][:, j, :],
                                            ALU.subtract).then_inc(h_lo_ready, 1)

            def d_stage(k, half, d):
                if d == 5:
                    pool.wait_ge(mv2_ready, k + 1)
                    chain(pool_d, k * 7, [(ve2[:, :], mv2[:, 0:HT, 1], eps[:, 0:HT], ALU.add),
                                          (rs2[:, :], ve2[:, :], neg_half[:, 0:HT], ALU.pow)]).then_inc(rs2_ready, 1)
                if d == 6:
                    var = mv2[:, HT:2 * HT, 1]
                    pool.wait_ge(mv3_ready, k + 1)
                    chain(pool_d, k * 7 + 1, [(ve3[:, :], var, eps[:, 0:HT], ALU.add),
                                              (rs3[:, :], ve3[:, :], neg_half[:, 0:HT], ALU.pow),
                                              (ve4[:, :], var, rs3[:, :], ALU.mult),
                                              (ve4[:, :], ve4[:, :], rs3[:, :], ALU.mult),
                                              (ve4[:, :], ve4[:, :], eps[:, 0:HT], ALU.add),
                                              (ve4[:, :], ve4[:, :], neg_half[:, 0:HT], ALU.pow),
                                              (rs4[:, :], ve4[:, :], rs3[:, :], ALU.mult)]).then_inc(rs4_ready, 1)

            pool.sem_inc(h_lo_ready, 2)
            pool.sem_inc(s_done, 2)
            pool.sem_inc(w3_done, 4)
            pool.sem_inc(x1_stored, 16)
            pool.sem_inc(n_stored, 16)
            pool.sem_inc(ys_stored, 16)
            run(pool, a_stage, c_step, d_stage)



G = 384
GT = G // P
NG = (T * K + E * (G - 1)) // G
SLOTS = (NG + 1) * G
CW = 4 * P + D
MAXG = T // G + 1
CLEAR_N = 640
CLEARS = SLOTS * D // (B * P * CLEAR_N)
TC = 4
NC = TT // TC
assert CLEARS * B * P * CLEAR_N == SLOTS * D


def token_rows(dram):
    return dram.rearrange("b l d -> (b l) d").rearrange("(c t p) d -> c p t d", t=TC, p=P)


def route(nc, logits, n_dram, xs_dram, slot, weight, group_expert, cleared):
    with ExitStack() as ctx:
        def sb(name, shape, dt=F32):
            return ctx.enter_context(nc.sbuf_tensor(name, shape, dt))

        def sem(name):
            return ctx.enter_context(nc.semaphore(name))

        top = sb("top", [P, TT])
        p = sb("p", [P, TT, E])
        total = sb("total", [P, TT])
        desc = sb("desc", [P, TT, E])
        score = sb("score", [P, TT, E])
        best = sb("best", [P, TT])
        pick = [sb(f"pick{k}", [P, TT, E]) for k in range(K)]
        val = [sb(f"val{k}", [P, TT]) for k in range(K)]
        both = sb("both", [P, E, TT])
        ones = sb("r_ones", [P, E * TT])
        run_sum = sb("run_sum", [P, E, TT])
        count = sb("count", [P, E])
        before = sb("before", [P, P])
        all_ones = sb("all_ones", [P, P])
        offset = sb("offset", [P, E])
        n_all = sb("n_all", [P, E])
        limits = sb("limits", [P, E, MAXG])
        over = sb("over", [P, E, MAXG])
        groups = sb("groups", [P, E])
        group_end = sb("group_end", [P, E])
        base = sb("base", [P, E])
        slot_f = sb("slot_f", [P, TT, K])
        group_no = sb("group_no", [P, NG + 1, E - 1])
        past = sb("past", [P, NG + 1, E - 1])
        expert_f = sb("expert_f", [P, NG + 1])
        rows = sb("rows", [P, 2, TC, D])
        ps = ctx.enter_context(nc.psum_tensor("ps_route", [P, 512], F32))
        steps, exp_ready, shifted = sem("route_steps"), sem("r_exp"), sem("r_shifted")
        counted, summed, masks, slots_ready = sem("counted"), sem("summed"), sem("masks"), sem("slots_ready")
        loaded = [sem(f"rows_loaded{i}") for i in range(2)]
        before_set = sem("before_set")
        scattered = [sem(f"scattered{i}") for i in range(2)]
        block = ctx.enter_context(nc.Block())

        @block.sync
        def _(sp):
            for c in range(NC):
                if c >= 2:
                    sp.wait_ge(scattered[c % 2], c // 2 * 16 * TC * K)
                sp.dma_start(rows[:, c % 2, :, :], token_rows(n_dram)[c, :, :, :]).then_inc(loaded[c % 2], 16)

        @block.tensor
        def _(pe):
            pe.wait_ge(masks, 2)
            pe.wait_ge(counted, 1)
            nc.tensor.matmul(ps[:, 0:E], before[:, :], count[:, :], start=True, stop=True)
            nc.tensor.matmul(ps[:, E:2 * E], all_ones[:, :], count[:, :], start=True, stop=True).then_inc(summed, 1)

        @block.scalar
        def _(act):
            act.wait_ge(shifted, 1)
            nc.scalar.activation(p[:, :, :], p[:, :, :], ACT.Exp).then_inc(exp_ready, 1)

        @block.vector
        def _(dve):
            n = [0]

            def link(i):
                n[0] += 1
                i.then_inc(steps, 1)
                dve.wait_ge(steps, n[0])

            def wide(v):
                return v[:, :].unsqueeze(2).to_broadcast([P, TT, E])

            for e in range(E):
                nc.vector.memset(desc[:, :, e:e + 1], float(E - e))
            for j in range(MAXG):
                nc.vector.memset(limits[:, :, j:j + 1], float(j * G))
            for g in range(NG + 1):
                nc.vector.memset(group_no[:, g:g + 1, :], float(g))
            link(nc.vector.memset(ones[:, :], 1.0))
            nc.vector.memset(all_ones[:, :], 1.0).then_inc(masks, 1)
            l = logits[:, :].rearrange("p (t e) -> p t e", e=E)
            link(nc.vector.tensor_reduce(top[:, :], l, AX.X, ALU.max))
            nc.vector.tensor_tensor(p[:, :, :], l, wide(top), ALU.subtract).then_inc(shifted, 1)
            dve.wait_ge(exp_ready, 1)
            link(nc.vector.tensor_reduce(total[:, :], p[:, :, :], AX.X, ALU.add))
            link(nc.vector.reciprocal(total[:, :], total[:, :]))
            link(nc.vector.tensor_tensor(p[:, :, :], p[:, :, :], wide(total), ALU.mult))
            for k in range(K):
                link(nc.vector.tensor_reduce(val[k][:, :], p[:, :, :], AX.X, ALU.max))
                link(nc.vector.tensor_tensor(score[:, :, :], p[:, :, :], wide(val[k]), ALU.is_equal))
                link(nc.vector.tensor_tensor(score[:, :, :], score[:, :, :], desc[:, :, :], ALU.mult))
                link(nc.vector.tensor_reduce(best[:, :], score[:, :, :], AX.X, ALU.max))
                link(nc.vector.tensor_tensor(pick[k][:, :, :], score[:, :, :], wide(best), ALU.is_equal))
                if k == 0:
                    link(nc.vector.scalar_tensor_tensor(out=p[:, :, :], in0=pick[k][:, :, :], scalar=-2.0,
                                                        in1=p[:, :, :], op0=ALU.mult, op1=ALU.add))
            link(nc.vector.tensor_tensor(total[:, :], val[0][:, :], val[1][:, :], ALU.add))
            link(nc.vector.reciprocal(total[:, :], total[:, :]))
            for k in range(K):
                nc.vector.tensor_tensor(weight[:, :, k], val[k][:, :], total[:, :], ALU.mult)
            link(nc.vector.tensor_tensor(both[:, :, :].rearrange("p e t -> p t e"), pick[0][:, :, :], pick[1][:, :, :], ALU.add))
            link(nc.vector.tensor_tensor_scan(run_sum[:, :, :].rearrange("p e t -> p (e t)"), ones[:, :],
                                              both[:, :, :].rearrange("p e t -> p (e t)"), 0.0, ALU.mult, ALU.add))
            nc.vector.tensor_reduce(count[:, :], both[:, :, :], AX.X, ALU.add).then_inc(counted, 1)
            dve.wait_ge(summed, 1)
            link(nc.vector.tensor_copy(n_all[:, :], ps[:, E:2 * E]))
            link(nc.vector.tensor_tensor(over[:, :, :], n_all[:, :].unsqueeze(2).to_broadcast([P, E, MAXG]),
                                         limits[:, :, :], ALU.is_gt))
            link(nc.vector.tensor_reduce(groups[:, :], over[:, :, :], AX.X, ALU.add))
            link(nc.vector.tensor_tensor_scan(group_end[:, :], ones[:, 0:E], groups[:, :], 0.0, ALU.mult, ALU.add))
            link(nc.vector.tensor_tensor(base[:, :], group_end[:, :], groups[:, :], ALU.subtract))
            link(nc.vector.scalar_tensor_tensor(out=offset[:, :], in0=base[:, :], scalar=float(G), in1=ps[:, 0:E],
                                                op0=ALU.mult, op1=ALU.add))
            link(nc.vector.tensor_tensor(offset[:, :], offset[:, :], count[:, :], ALU.add))
            link(nc.vector.tensor_tensor(offset[:, :], offset[:, :], run_sum[:, :, TT - 1], ALU.subtract))
            link(nc.vector.tensor_scalar(offset[:, :], offset[:, :], -1.0, None, ALU.add))
            link(nc.vector.tensor_tensor(run_sum[:, :, :], run_sum[:, :, :],
                                         offset[:, :].unsqueeze(2).to_broadcast([P, E, TT]), ALU.add))
            for k in range(K):
                link(nc.vector.tensor_tensor(score[:, :, :], pick[k][:, :, :],
                                             run_sum[:, :, :].rearrange("p e t -> p t e"), ALU.mult))
                link(nc.vector.tensor_reduce(slot_f[:, :, k:k + 1], score[:, :, :], AX.X, ALU.add))
            nc.vector.tensor_copy(slot[:, :, :], slot_f[:, :, :]).then_inc(slots_ready, 1)
            link(nc.vector.tensor_tensor(past[:, :, :], group_no[:, :, :],
                                         group_end[:, 0:E - 1].unsqueeze(1).to_broadcast([P, NG + 1, E - 1]), ALU.is_ge))
            link(nc.vector.tensor_reduce(expert_f[:, :], past[:, :, :], AX.X, ALU.add))
            nc.vector.tensor_copy(group_expert[:, :], expert_f[:, :])

        @block.gpsimd
        def _(pool):
            nc.gpsimd.memset(before[:, :], 1.0).then_inc(before_set, 1)
            pool.wait_ge(before_set, 1)
            nc.gpsimd.affine_select(out=before[:, :], in_=before[:, :], compare_op=ALU.is_gt, fill=0.0,
                                    base=0, pattern=[[1, P]], channel_multiplier=-1).then_inc(masks, 1)
            pool.wait_ge(cleared, 16 * B * CLEARS)
            pool.wait_ge(slots_ready, 1)
            for c in range(NC):
                pool.wait_ge(loaded[c % 2], (c // 2 + 1) * 16)
                for t in range(TC):
                    for k in range(K):
                        nc.gpsimd.indirect_dma_start(
                            out=xs_dram, out_offset=bass.IndirectOffsetOnAxis(ap=slot[:, c * TC + t, k:k + 1], axis=0),
                            in_=rows[:, c % 2, t, :], in_offset=None).then_inc(scattered[c % 2], 16)
            for par in range(2):
                pool.wait_ge(scattered[par], NC // 2 * 16 * TC * K)


def experts(nc, w_e, xs_dram, y_dram, group_expert, vec, ident):
    with ExitStack() as ctx:
        def sb(name, shape, dt=F32):
            return ctx.enter_context(nc.sbuf_tensor(name, shape, dt))

        def sem(name):
            return ctx.enter_context(nc.semaphore(name))

        RAW, RING, AHEAD, LAG = 4, FC, 5, 2
        raw = sb("raw", [P, RAW, CW])
        e_hi = sb("e_hi", [P, RING, CW], F32R)
        e_lo = sb("e_lo", [P, RING, CW], F32R)
        rows = sb("x_rows", [P, 2, GT, D])
        xg_hi = sb("xg_hi", [P, 2, DC, G], F32R)
        xg_lo = sb("xg_lo", [P, 2, DC, G], F32R)
        xg_f = sb("xg_f", [P, DC, G])
        gate = sb("gate", [P, 2, G])
        hg_hi = sb("hg_hi", [P, 4, G], F32R)
        hg_lo = sb("hg_lo", [P, 4, G], F32R)
        y = sb("y", [P, 2, GT, D])
        gate_ps = [ctx.enter_context(nc.psum_tensor(f"gate_ps{i}", [P, 512], F32)) for i in range(2)]
        up_ps = [ctx.enter_context(nc.psum_tensor(f"up_ps{i}", [P, 512], F32)) for i in range(2)]
        x_ps = ctx.enter_context(nc.psum_tensor("x_ps", [P, 512], F32))
        down_ps = [ctx.enter_context(nc.psum_tensor(f"down_ps{i}", [P, 512], F32)) for i in range(GT)]
        loaded = [sem(f"chunk_loaded{i}") for i in range(RAW)]
        hi_ready, lo_ready = sem("chunk_hi"), sem("chunk_lo")
        rows_loaded = [sem(f"x_rows_loaded{i}") for i in range(2)]
        x_turned, x_hi_ready, x_f_ready, x_lo_ready = sem("x_turned"), sem("x_hi_ready"), sem("x_f_ready"), sem("x_lo_ready")
        gate_done, up_done, down_done = sem("e_gate_done"), sem("e_up_done"), sem("e_down_done")
        clipped, silu_ready, h_ready = sem("e_clipped"), sem("e_silu"), sem("e_h_ready")
        h_hi_ready, h_lo_ready, y_ready = sem("e_h_hi"), sem("e_h_lo"), sem("e_y_ready")
        y_stored = [sem(f"y_stored{i}") for i in range(2)]
        block = ctx.enter_context(nc.Block())

        def groups(eng, turn):
            turn(0, 0)
            with eng.Fori(0, (NG - 1) // 2) as i:
                for k in range(2):
                    turn(i * 2 + 1 + k, 1 - k)

        assert NG % 2 == 1

        @block.sync
        def _(sp):
            def load_rows(g, par):
                sp.dma_start(rows[:, par, :, :], xs_dram.rearrange("(g t p) d -> g p t d", t=GT, p=P)[g, :, :, :]
                             ).then_inc(rows_loaded[par], 16)

            def load_chunk(g, f, e):
                sp.wait_ge(lo_ready, g * FC + f + 1)
                sp.dma_start(raw[:, f % RAW, :], w_e[e, f, :, :]).then_inc(loaded[f % RAW], 16)

            def store_y(g, par):
                sp.wait_ge(y_ready, g + 2 + 1)
                sp.dma_start(y_dram.rearrange("(g t p) d -> g p t d", t=GT, p=P)[g, :, :, :], y[:, par, :, :]
                             ).then_inc(y_stored[par], 16)

            def expert_of(g):
                return sp.value_load(group_expert[0:1, bass.ds(g, 1)], min_val=0, max_val=E - 1)

            def turn(g, par):
                e = expert_of(g)
                for f in range(FC):
                    load_chunk(g, f, e)
                    if f == 0:
                        if not (isinstance(g, int) and g == 0):
                            sp.wait_ge(x_turned, g * DC)
                        load_rows(g + 1, 1 - par)

            load_rows(0, 0)
            turn(0, 0)
            turn(1, 1)
            turn(2, 0)
            with sp.Fori(0, (NG - 3) // 2) as i:
                for k in range(2):
                    g = i * 2 + 3 + k
                    store_y(g - 3, 0 if k == 0 else 1)
                    turn(g, 1 - k)
            e = expert_of(NG)
            for f in range(AHEAD):
                load_chunk(NG, f, e)
            for g in range(NG - 3, NG):
                store_y(g, g % 2)
            sp.wait_ge(y_stored[0], 16 + 16 * ((NG + 1) // 2))
            sp.wait_ge(y_stored[1], 16 + 16 * (NG // 2))

        @block.tensor
        def _(pe):
            def turn_rows(g, par, c):
                if c == 0:
                    pe.wait_ge(rows_loaded[par], (g_half(g, par)) * 16 + 16)
                pe.wait_ge(x_f_ready, g * DC + c + 1)
                for t in range(GT):
                    i = nc.tensor.transpose(x_ps[:, t * P:(t + 1) * P], rows[:, par, t, c * P:(c + 1) * P], ident[:, :])
                i.then_inc(x_turned, 1)

            def gate_up(g, par, f):
                pe.wait_ge(lo_ready, g * FC + f + 1 + RAW)
                if f == 0:
                    pe.wait_ge(x_lo_ready, g * DC + DC)
                pe.wait_ge(h_ready, g * FC + f + 1)
                for ps, at, done in ((gate_ps, 0, gate_done), (up_ps, 2 * P, up_done)):
                    out = ps[f % 2][:, 0:G]
                    for c in range(DC):
                        cols = slice(at + c * P, at + (c + 1) * P)
                        nc.tensor.matmul(out, e_hi[:, f, cols], xg_hi[:, par, c, :], start=c == 0, stop=False)
                        nc.tensor.matmul(out, e_hi[:, f, cols], xg_lo[:, par, c, :], start=False, stop=False)
                        i = nc.tensor.matmul(out, e_lo[:, f, cols], xg_hi[:, par, c, :], start=False, stop=c == DC - 1)
                    i.then_inc(done, 1)

            def down(g, f):
                pe.wait_ge(h_lo_ready, g * FC + f + 1)
                if f == 0:
                    pe.wait_ge(y_ready, g + 2)
                for t in range(GT):
                    toks = slice(t * P, (t + 1) * P)
                    out = down_ps[t][:, 0:D]
                    nc.tensor.matmul(out, hg_hi[:, f % 4, toks], e_hi[:, f, 4 * P:CW], start=f == 0, stop=False)
                    nc.tensor.matmul(out, hg_hi[:, f % 4, toks], e_lo[:, f, 4 * P:CW], start=False, stop=False)
                    i = nc.tensor.matmul(out, hg_lo[:, f % 4, toks], e_hi[:, f, 4 * P:CW], start=False, stop=f == FC - 1)
                i.then_inc(down_done, 1)

            def turn(g, par):
                for f in range(FC):
                    gate_up(g, par, f)
                    if f >= LAG:
                        down(g, f - LAG)
                    elif not (isinstance(g, int) and g == 0):
                        down(g - 1, FC + f - LAG)
                    if f in (2, 4):
                        turn_rows(g + 1, 1 - par, (f - 2) // 2)

            for c in range(DC):
                turn_rows(0, 0, c)
            groups(pe, turn)
            for f in range(FC - LAG, FC):
                down(NG - 1, f)

        @block.scalar
        def _(act):
            def split(g, f):
                act.wait_ge(loaded[f % RAW], (g * (FC // RAW) + f // RAW) * 16 + 16)
                act.wait_ge(down_done, g * FC + f + 1)
                nc.scalar.activation(e_hi[:, f, :], raw[:, f % RAW, :], ACT.Copy).then_inc(hi_ready, 1)

            def rows_hi(g, par, c):
                act.wait_ge(x_turned, g * DC + c + 1)
                nc.scalar.activation(xg_hi[:, par, c, :], x_ps[:, 0:G], ACT.Identity,
                                     bias=vec[:, V_BE + c:V_BE + c + 1],
                                     scale=vec[:, V_G + c:V_G + c + 1]).then_inc(x_hi_ready, 1)

            def turn(g, par):
                for f in range(FC):
                    act.wait_ge(clipped, g * FC + f + 1)
                    nc.scalar.activation(gate[:, f % 2, :], gate[:, f % 2, :], ACT.Silu).then_inc(silu_ready, 1)
                    ahead = f + AHEAD
                    split(g + ahead // FC, ahead % FC)
                    if f in (3, 5):
                        rows_hi(g + 1, 1 - par, (f - 3) // 2)
                    act.wait_ge(h_ready, g * FC + f + 1 + 2)
                    nc.scalar.activation(hg_hi[:, f % 4, :], gate[:, f % 2, :], ACT.Copy).then_inc(h_hi_ready, 1)

            act.sem_inc(down_done, FC)
            for c in range(DC):
                rows_hi(0, 0, c)
            for f in range(AHEAD):
                split(0, f)
            groups(act, turn)

        @block.vector
        def _(dve):
            def rows_lo(g, par, c):
                dve.wait_ge(x_hi_ready, g * DC + c + 1)
                nc.vector.tensor_scalar(xg_f[:, c, :], x_ps[:, 0:G], vec[:, V_G + c:V_G + c + 1],
                                        vec[:, V_BE + c:V_BE + c + 1], ALU.mult, ALU.add).then_inc(x_f_ready, 1)
                dve.wait_ge(x_f_ready, g * DC + c + 2)
                nc.vector.tensor_tensor(xg_lo[:, par, c, :], xg_f[:, c, :], xg_hi[:, par, c, :],
                                        ALU.subtract).then_inc(x_lo_ready, 1)

            def copy_y(g, par):
                dve.wait_ge(down_done, (g + 1) * FC + FC)
                dve.wait_ge(y_stored[par], (g_half(g, par)) * 16 + 16)
                for t in range(GT):
                    i = nc.vector.tensor_copy(y[:, par, t, :], down_ps[t][:, 0:D])
                i.then_inc(y_ready, 1)

            def turn(g, par):
                for f in range(FC):
                    if f == LAG and not (isinstance(g, int) and g == 0):
                        copy_y(g - 1, 1 - par)
                    dve.wait_ge(gate_done, g * FC + f + 1)
                    nc.vector.tensor_scalar(gate[:, f % 2, :], gate_ps[f % 2][:, 0:G], CLIP, -CLIP,
                                            ALU.min, ALU.max).then_inc(clipped, 1)
                    dve.wait_ge(silu_ready, g * FC + f + 1)
                    dve.wait_ge(up_done, g * FC + f + 1)
                    nc.vector.tensor_tensor(gate[:, f % 2, :], up_ps[f % 2][:, 0:G], gate[:, f % 2, :],
                                            ALU.mult).then_inc(h_ready, 1)
                    if f in (3, 5):
                        rows_lo(g + 1, 1 - par, (f - 3) // 2)
                    dve.wait_ge(h_hi_ready, g * FC + f + 1)
                    nc.vector.tensor_tensor(hg_lo[:, f % 4, :], gate[:, f % 2, :], hg_hi[:, f % 4, :],
                                            ALU.subtract).then_inc(h_lo_ready, 1)

            dve.sem_inc(x_f_ready, 1)
            dve.sem_inc(h_ready, 2)
            dve.sem_inc(y_ready, 2)
            for par in range(2):
                dve.sem_inc(y_stored[par], 16)
            for c in range(DC):
                rows_lo(0, 0, c)
            groups(dve, turn)
            copy_y(NG - 1, 0)

        @block.gpsimd
        def _(pool):
            def split(g, f):
                pool.wait_ge(hi_ready, g * FC + f + 1)
                nc.gpsimd.tensor_tensor(e_lo[:, f, :], raw[:, f % RAW, :], e_hi[:, f, :], ALU.subtract).then_inc(lo_ready, 1)

            pool.sem_inc(lo_ready, RAW)
            for f in range(AHEAD):
                split(0, f)

            def turn(g, par):
                for f in range(FC):
                    ahead = f + AHEAD
                    split(g + ahead // FC, ahead % FC)

            groups(pool, turn)


def g_half(g, par):
    if isinstance(g, int):
        return g // 2
    return (g - par) // 2


def combine(nc, y_dram, ys_dram, x1_dram, out, slot, weight, neg_half, eps):
    with ExitStack() as ctx:
        def sb(name, shape, dt=F32):
            return ctx.enter_context(nc.sbuf_tensor(name, shape, dt))

        def sem(name):
            return ctx.enter_context(nc.semaphore(name))

        x1 = sb("c_x1", [P, 2, TC, D])
        ys = sb("c_ys", [P, 2, TC, D])
        ye = sb("c_ye", [P, 2, TC, K, D])
        st = sb("c_st", [P, TC, 6])
        mv = sb("c_mv", [P, TC, 2])
        ve = sb("c_ve", [P, TC])
        rs = sb("c_rs", [P, TC])
        tokens_loaded = [sem(f"tokens_loaded{i}") for i in range(2)]
        gathered = [sem(f"gathered{i}") for i in range(2)]
        stored = [sem(f"out_stored{i}") for i in range(2)]
        mixed, order, seen = sem("c_mixed"), sem("c_order"), sem("c_seen")
        moments_ready, rs_ready, ve_ready = sem("c_moments"), sem("c_rs_ready"), sem("c_ve_ready")
        normed, out_ready = sem("c_normed"), sem("c_out_ready")
        block = ctx.enter_context(nc.Block())

        @block.sync
        def _(sp):
            for par in range(2):
                sp.sem_inc(stored[par], 16)
            sp.sem_inc(out_ready, 2)
            with sp.Fori(0, NC // 2) as i:
                for par in range(2):
                    sp.wait_ge(stored[par], i * 16 + 16)
                    sp.dma_start(x1[:, par, :, :], token_rows(x1_dram)[i * 2 + par, :, :, :]).then_inc(tokens_loaded[par], 16)
                    sp.wait_ge(out_ready, i * 2 + par + 1)
                    sp.dma_start(ys[:, par, :, :], token_rows(ys_dram)[i * 2 + par, :, :, :]).then_inc(tokens_loaded[par], 16)
                for par in range(2):
                    sp.wait_ge(out_ready, i * 2 + par + 3)
                    sp.dma_start(token_rows(out)[i * 2 + par, :, :, :], x1[:, par, :, :]).then_inc(stored[par], 16)
            for par in range(2):
                sp.wait_ge(stored[par], 16 + 16 * (NC // 2))

        @block.gpsimd
        def _(pool):
            def roots(c):
                pool.wait_ge(moments_ready, c + 1)
                nc.gpsimd.tensor_tensor(ve[:, :], mv[:, :, 1], eps[:, 0:TC], ALU.add).then_inc(ve_ready, 1)
                pool.wait_ge(ve_ready, c + 1)
                nc.gpsimd.tensor_tensor(rs[:, :], ve[:, :], neg_half[:, 0:TC], ALU.pow).then_inc(rs_ready, 1)

            for c in range(NC):
                if c >= 2:
                    pool.wait_ge(mixed, c - 1)
                for t in range(TC):
                    for k in range(K):
                        nc.gpsimd.indirect_dma_start(
                            out=ye[:, c % 2, t, k, :], out_offset=None, in_=y_dram,
                            in_offset=bass.IndirectOffsetOnAxis(ap=slot[:, c * TC + t, k:k + 1], axis=0)
                        ).then_inc(gathered[c % 2], 16)
                if c >= 1:
                    roots(c - 1)
            roots(NC - 1)

        @block.vector
        def _(dve):
            with dve.Fori(0, NC // 2) as i:
                for par in range(2):
                    c = i * 2 + par
                    dve.wait_ge(tokens_loaded[par], i * 32 + 32)
                    dve.wait_ge(gathered[par], i * 16 * TC * K + 16 * TC * K)
                    for k in range(K):
                        for t in range(TC):
                            j = nc.vector.scalar_tensor_tensor(out=ys[:, par, t, :], in0=ye[:, par, t, k, :],
                                                               scalar=weight[:, bass.ds(c * TC + t, 1), k:k + 1].rearrange("p t k -> p (t k)"),
                                                               in1=ys[:, par, t, :], op0=ALU.mult, op1=ALU.add)
                        if k < K - 1:
                            j.then_inc(order, 1)
                            dve.wait_ge(order, c * 2 + 1)
                    j.then_inc(mixed, 1)
                    dve.wait_ge(mixed, c + 1)
                    for t in range(TC):
                        j = nc.vector.bn_stats(st[:, t, :], ys[:, par, t, :])
                    j.then_inc(order, 1)
                    dve.wait_ge(order, c * 2 + 2)
                    dve.sem_inc(seen, 1)
                    for t in range(TC):
                        j = nc.vector.bn_aggr(mv[:, t, :], st[:, t, :])
                    j.then_inc(moments_ready, 1)
                    dve.wait_ge(moments_ready, c + 1)
                    dve.wait_ge(rs_ready, c + 1)
                    for t in range(TC):
                        j = nc.vector.tensor_scalar(ys[:, par, t, :], ys[:, par, t, :], mv[:, t, 0:1], rs[:, t:t + 1],
                                                    ALU.subtract, ALU.mult)
                    j.then_inc(normed, 1)
                    dve.wait_ge(normed, c + 1)
                    nc.vector.tensor_tensor(x1[:, par, :, :], x1[:, par, :, :], ys[:, par, :, :], ALU.add).then_inc(out_ready, 1)


def program(nc, d, out):
    scratch = lambda name, shape: nc.dram_tensor(name, shape, F32, kind="Internal").ap()
    x1_dram = scratch("x1_scratch", (B, L, D))
    n_dram = scratch("n_scratch", (B, L, D))
    ys_dram = scratch("ys_scratch", (B, L, D))
    xs_dram = scratch("xs_scratch", (SLOTS, D))
    y_dram = scratch("y_scratch", (NG * G, D))
    with ExitStack() as ctx:
        def sb(name, shape, dt=F32):
            return ctx.enter_context(nc.sbuf_tensor(name, shape, dt))

        cleared = ctx.enter_context(nc.semaphore("cleared"))
        vec = sb("vec", [P, V_COLS])
        slot = sb("slot", [P, TT, K], I32)
        weight = sb("weight", [P, TT, K])
        group_expert = sb("group_expert", [P, NG + 1], I32)
        logits = sb("logits", [P, TT * E])
        ident = sb("ident", [P, P])
        neg_half = sb("neg_half", [P, LT])
        eps = sb("eps", [P, LT])
        with ExitStack() as first:
            def sb1(name, shape, dt=F32):
                return first.enter_context(nc.sbuf_tensor(name, shape, dt))

            w_hi, w_lo = sb1("w_hi", [P, W_COLS], F32R), sb1("w_lo", [P, W_COLS], F32R)
            s_hi, s_lo = sb1("s_hi", [P, S_COLS], F32R), sb1("s_lo", [P, S_COLS], F32R)
            ident_r = sb1("ident_r", [P, P], F32R)
            zeros, ones = sb1("zeros", [P, CLEAR_N]), sb1("ones", [P, HALF])
            split_weights(nc, [(W1_AT, d["w1_t"], DC), (DL_AT, d["dl_w_t"], DC), (A_AT, d["A_w_t"], DC),
                               (B_AT, d["B_w_t"], DC), (C_AT, d["C_w_t"], HC), (DD_AT, d["D_w_t"], DC),
                               (W2_AT, d["w2_t"], DC), (W3_AT, d["w3_t"], DC)],
                          [(SGU_AT, d["sgu"], DC), (SDN_AT, d["sdn"], SC), (RT_AT, d["router"], DC)],
                          d["vecs"], w_hi, w_lo, s_hi, s_lo, vec, ident, ident_r, zeros, ones, neg_half, eps)
            mixer(nc, d["x"], xs_dram, cleared, x1_dram, n_dram, ys_dram, logits, w_hi, w_lo, s_hi, s_lo, vec, ident, ident_r,
                  zeros, ones, neg_half, eps)
        route(nc, logits, n_dram, xs_dram, slot, weight, group_expert, cleared)
        experts(nc, d["w_e"], xs_dram, y_dram, group_expert, vec, ident)
        combine(nc, y_dram, ys_dram, x1_dram, out, slot, weight, neg_half, eps)

def kernel(**inputs):
    import numpy as np
    import concourse.bacc as bacc
    from concourse.bass_utils import run_bass_kernel_spmd as run

    a = {k.replace("L0_attn_", "").replace("L0_ffn_", "f_"): np.asarray(v) for k, v in inputs.items()}
    cols = lambda v: v.reshape(-1, P).T
    vecs = np.concatenate([a["conv_w"].reshape(DC, P, 3).transpose(1, 0, 2).reshape(P, DC * 3)] +
                          [cols(a[k]) for k in ("conv_b", "A_b", "B_b", "dl_b", "C_b", "D_b", "f_ln_gamma", "f_ln_beta")], axis=1)
    arrays = {"x": a["x"], "vecs": vecs, "sgu": a["f_shared_gate_up_w"], "sdn": a["f_shared_down_w"],
              "router": a["f_router_w"]}
    gu = a["f_gate_up_w"].reshape(E, DC, P, 2, FC, P).transpose(0, 4, 2, 3, 1, 5).reshape(E, FC, P, 4 * P)
    arrays["w_e"] = np.concatenate([gu, a["f_down_w"].reshape(E, FC, P, D)], axis=3)
    for k in ("w1", "w2", "w3", "A_w", "B_w", "C_w", "D_w", "dl_w"):
        arrays[k + "_t"] = a[k].T
    arrays = {k: np.ascontiguousarray(v) for k, v in arrays.items()}
    nc = bacc.Bacc("TRN2", target_bir_lowering=False, num_devices=1)
    d = {k: nc.dram_tensor(k, v.shape, mybir.dt.from_np(v.dtype), kind="ExternalInput").ap() for k, v in arrays.items()}
    out = nc.dram_tensor("out", (B, L, D), F32, kind="ExternalOutput").ap()
    program(nc, d, out)
    return run(nc, [arrays], core_ids=[0]).results[0]["out"]
```

```python
import concourse.bass as bass
from concourse import mybir
from contextlib import ExitStack

F32 = mybir.dt.float32
F32R = mybir.dt.float32r
I32 = mybir.dt.int32
ALU = mybir.AluOpType
ACT = mybir.ActivationFunctionType
AX = mybir.AxisListType

P = 128
B, L, D, H = 4, 1024, 256, 512
E, F, FS, K = 8, 1024, 256, 2
T = B * L
DC, HC, FC, SC = D // P, H // P, F // P, FS // P
HALF = 512
HT = HALF // P
LT = L // P
TT = T // P
EPS = 1e-5
CLIP = 10.0
EXP_CAP = 1e9

W1_AT, DL_AT, A_AT, B_AT = 0, DC * D, DC * (D + H), DC * (D + 2 * H)
C_AT = DC * (D + 3 * H)
DD_AT = C_AT + HC * D
W2_AT, W3_AT = DD_AT + DC * D, DD_AT + 2 * DC * D
RT_AT = W3_AT + DC * D
W_COLS = RT_AT + DC * E
SGU_AT, SDN_AT = 0, DC * 2 * FS
S_COLS = SDN_AT + SC * D
V_CW, V_CB = 0, 3 * DC
V_AB = V_CB + DC
V_BB, V_DLB = V_AB + HC, V_AB + 2 * HC
V_CDB = V_DLB + HC
V_G, V_BE = V_CDB + 2 * DC, V_CDB + 3 * DC
V_COLS = V_BE + DC


def split_weights(nc, weights, consts, w_hi, w_lo, vec, ident, ident_r, zeros, ones, neg_half, eps):
    with ExitStack() as ctx:
        raw = ctx.enter_context(nc.sbuf_tensor("raw_w", [P, W_COLS], F32))
        loaded = [ctx.enter_context(nc.semaphore(f"prep_loaded{i}")) for i in range(len(weights))]
        vec_loaded = ctx.enter_context(nc.semaphore("vec_loaded"))
        hi_ready = ctx.enter_context(nc.semaphore("prep_hi"))
        lo_ready = ctx.enter_context(nc.semaphore("prep_lo"))
        made = ctx.enter_context(nc.semaphore("consts_made"))
        block = ctx.enter_context(nc.Block())
        parts = []
        for at, src, chunks in weights:
            parts.append((raw, w_hi, w_lo, at, src, chunks))

        @block.sync
        def _(sp):
            for n, (r, hi, lo, at, src, chunks) in enumerate(parts):
                width = src.shape[1]
                sp.dma_start(r[:, at:at + chunks * width].rearrange("p (c n) -> p c n", c=chunks),
                             src.rearrange("(c p) n -> p c n", p=P)).then_inc(loaded[n], 16)
            sp.dma_start(vec[:, :], consts).then_inc(vec_loaded, 16)
            sp.wait_ge(vec_loaded, 16)

        @block.scalar
        def _(act):
            for n, (r, hi, lo, at, src, chunks) in enumerate(parts):
                cols = chunks * src.shape[1]
                act.wait_ge(loaded[n], 16)
                nc.scalar.activation(hi[:, at:at + cols], r[:, at:at + cols], ACT.Copy).then_inc(hi_ready, 1)
            act.wait_ge(made, 3)
            nc.scalar.activation(ident_r[:, :], ident[:, :], ACT.Copy)

        @block.vector
        def _(dve):
            nc.vector.memset(zeros[:, :], 0.0)
            nc.vector.memset(ones[:, :], 1.0)
            nc.vector.memset(neg_half[:, :], -0.5)
            nc.vector.memset(eps[:, :], EPS)
            for n, (r, hi, lo, at, src, chunks) in enumerate(parts):
                cols = chunks * src.shape[1]
                dve.wait_ge(hi_ready, n + 1)
                nc.vector.tensor_tensor(lo[:, at:at + cols], r[:, at:at + cols], hi[:, at:at + cols],
                                        ALU.subtract).then_inc(lo_ready, 1)
            dve.wait_ge(lo_ready, len(parts))

        @block.gpsimd
        def _(pool):
            nc.gpsimd.memset(ident[:, :], 0.0).then_inc(made, 1)
            pool.wait_ge(made, 1)
            nc.gpsimd.affine_select(out=ident[:, :], in_=ident[:, :], compare_op=ALU.not_equal, fill=1.0,
                                    base=0, pattern=[[-1, P]], channel_multiplier=1).then_inc(made, 2)


def mixer(nc, x, xs_dram, x1_dram, n_dram, pick, val, slot_f, fill, w_hi, w_lo, vec, ident, ident_r, zeros, ones, neg_half, eps):
    with ExitStack() as ctx:
        def sb(name, shape, dt=F32):
            return ctx.enter_context(nc.sbuf_tensor(name, shape, dt))

        def sem(name):
            return ctx.enter_context(nc.semaphore(name))

        x_in = sb("x_in", [P, LT, D])
        xt_hi = sb("xt_hi", [P, DC, L], F32R)
        xt_lo = sb("xt_lo", [P, DC, L], F32R)
        u = sb("u", [P, DC, L + 2])
        cv = sb("cv", [P, DC, L])
        xs_hi = sb("xs_hi", [P, DC, L], F32R)
        xs_lo = sb("xs_lo", [P, DC, L], F32R)
        delta = sb("delta", [P, 2, HALF])
        decay = sb("decay", [P, 2, HALF])
        a_cum = sb("a_cum", [P, HALF])
        bx = sb("bx", [P, HALF])
        h = sb("h", [P, 2, HALF])
        carry_a = sb("carry_a", [P, HC])
        carry_h = sb("carry_h", [P, HC])
        h_hi = sb("h_hi", [P, HC, HALF], F32R)
        h_lo = sb("h_lo", [P, HC, HALF], F32R)
        s = sb("s", [P, DC, HALF])
        s_out_hi = sb("s_out_hi", [P, DC, HALF], F32R)
        s_out_lo = sb("s_out_lo", [P, DC, HALF], F32R)
        g = sb("g", [P, DC, HALF])
        z_hi = sb("z_hi", [P, DC, HALF], F32R)
        z_lo = sb("z_lo", [P, DC, HALF], F32R)
        xr = sb("xr", [P, HT, D])
        xnt_hi = sb("xnt_hi", [P, DC, HALF], F32R)
        xnt_lo = sb("xnt_lo", [P, DC, HALF], F32R)
        y_n = sb("y_n", [P, HT, D])
        n2 = sb("n2", [P, HT, D])
        cdb = sb("cdb", [P, DC])
        st = sb("st", [P, LT, 6])
        mv = sb("mv", [P, LT, 2])
        ve = sb("ve", [P, LT])
        rs = sb("rs", [P, LT])
        st2 = sb("st2", [P, 2 * HT, 6])
        mv2 = sb("mv2", [P, 2 * HT, 2])
        ve2 = sb("ve2", [P, HT])
        rs2 = sb("rs2", [P, HT])
        ve3 = sb("ve3", [P, HT])
        rs3 = sb("rs3", [P, HT])
        ve4 = sb("ve4", [P, HT])
        rs4 = sb("rs4", [P, HT])
        lt = sb("lt", [P, HALF])
        top = sb("top", [P, HT])
        prob = sb("prob", [P, HT, E])
        total = sb("total", [P, HT])
        desc = sb("desc", [P, HT, E])
        score = sb("score", [P, HT, E])
        best = sb("best", [P, HT])
        both = sb("both", [P, E, HT])
        run_sum = sb("run_sum", [P, E, HT])
        count = sb("count", [P, E])
        offset = sb("offset", [P, E])
        before = sb("before", [P, P])
        slot_half = sb("slot_half", [P, HT, K])
        slot_now = sb("slot_now", [P, HT, K], I32)
        banks = [ctx.enter_context(nc.psum_tensor(f"bank{i}", [P, HALF], F32)) for i in range(8)]

        x_loaded = sem("x_loaded")
        xr_loaded = sem("xr_loaded")
        x1_stored, n_stored, scattered = sem("x1_stored"), sem("n_stored"), sem("scattered")
        stats_seen, sp_seen = sem("stats_seen"), sem("sp_seen")
        a_order, d_order, start_made = sem("a_order"), sem("d_order"), sem("start_made")
        pool_a, pool_d = sem("pool_a"), sem("pool_d")
        mv_ready, rs_ready, xn_ready = sem("mv_ready"), sem("rs_ready"), sem("xn_ready")
        t1_done, xt_hi_ready, xt_lo_ready = sem("t1_done"), sem("xt_hi_ready"), sem("xt_lo_ready")
        u_done, u_copied, cv0_ready, cv_ready = sem("u_done"), sem("u_copied"), sem("cv0_ready"), sem("cv_ready")
        silu_ready, xs_hi_ready, xs_lo_ready = sem("silu_ready"), sem("xs_hi_ready"), sem("xs_lo_ready")
        dl_done, a_done, b_done = sem("dl_done"), sem("a_done"), sem("b_done")
        exp_ready, capped, ln_ready = sem("exp_ready"), sem("capped"), sem("ln_ready")
        delta_ready, da_ready, abar_ready = sem("delta_ready"), sem("da_ready"), sem("abar_ready")
        acum_ready, bx_ready, h_ready = sem("acum_ready"), sem("bx_ready"), sem("h_ready")
        carried, h_hi_ready, h_lo_ready = sem("carried"), sem("h_hi_ready"), sem("h_lo_ready")
        s_done, s_ready, s_hi_ready, s_lo_ready = sem("s_done"), sem("s_ready"), sem("s_hi_ready"), sem("s_lo_ready")
        g_done, g_ready, z_ready = sem("g_done"), sem("g_ready"), sem("z_ready")
        z_hi_ready, z_lo_ready, w3_done = sem("z_hi_ready"), sem("z_lo_ready"), sem("w3_done")
        mv2_ready, rs2_ready, yn_ready = sem("mv2_ready"), sem("rs2_ready"), sem("yn_ready")
        x1_ready, mv3_ready, rs4_ready, n2_ready = sem("x1_ready"), sem("mv3_ready"), sem("rs4_ready"), sem("n2_ready")
        t2_done, xn_hi_ready, xn_f_ready, xn_lo_ready = sem("t2_done"), sem("xn_hi_ready"), sem("xn_f_ready"), sem("xn_lo_ready")
        lt_done, lt_ready, logits_done = sem("lt_done"), sem("lt_ready"), sem("logits_done")
        shifted, probs_exp, counted = sem("shifted"), sem("probs_exp"), sem("counted")
        counts_done, route_steps, slots_ready = sem("counts_done"), sem("route_steps"), sem("slots_ready")
        pool_seen, before_set, before_made = sem("pool_seen"), sem("before_set"), sem("before_made")
        block = ctx.enter_context(nc.Block())

        LINKS = 20 + 2 * K
        UNITS = [(half, j) for half in range(2) for j in range(HC)]
        NU = len(UNITS)
        HH = ((h_hi, h_lo), (xt_hi[:, :, :].rearrange("p c (a l) -> p (c a) l", l=HALF),
                             xt_lo[:, :, :].rearrange("p c (a l) -> p (c a) l", l=HALF)))
        S_BANKS = ((6, 7), (4, 5))
        U_BANKS = (0, 1, 2, 3)

        BESIDE_A = [([(1, 1)], []), ([], [(0, 9)]), ([], [(0, 10)]), ([], [(0, 11)]),
                    ([], [(1, 2), (1, 3)]), ([], [(1, 4), (1, 5)])]
        BESIDE_C = [[(1, 6)], [(1, 7)], [(1, 8)], [(1, 9)], [(1, 10)], [(1, 11)],
                    [(0, 1), (0, 2)], [(0, 3), (0, 4)], [(0, 5), (0, 6)], [(0, 7), (0, 8)]]

        def run(eng, a_stage, c_step, d_stage):
            def turn(b, first):
                for a in range(6):
                    if not first:
                        for half, d in BESIDE_A[a][0]:
                            d_stage(b * 2 - 2 + half, half, d)
                    a_stage(b, a)
                    if not first:
                        for half, d in BESIDE_A[a][1]:
                            d_stage(b * 2 - 2 + half, half, d)
                for n in range(NU + 2):
                    c_step(b, n)
                    for half, d in BESIDE_C[n]:
                        if half == 0:
                            d_stage(b * 2, 0, d)
                        elif not first:
                            d_stage(b * 2 - 1, 1, d)

            turn(0, True)
            with eng.Fori(1, B) as b:
                turn(b, False)
            for half, d in [(1, 1)] + [(0, i) for i in range(9, 12)] + [(1, i) for i in range(2, 12)]:
                d_stage(2 * B - 2 + half, half, d)

        def W(hi_lo, at, c, width, lo=0, n=P):
            return hi_lo[:, at + c * width + lo:at + c * width + lo + n]

        @block.sync
        def _(sp):
            def load_x(b):
                sp.dma_start(x_in[:, :, :], x[b, :, :].rearrange("(t p) d -> p t d", p=P)).then_inc(x_loaded, 16)

            def passed(semaphore, value):
                sp.wait_ge(semaphore, value)
                sp.sem_inc(sp_seen, 1)

            def half_dmas(b, half):
                k = b * 2 + half
                rows = slice(half * HALF, (half + 1) * HALF)
                passed(x1_stored, k * 16 + 16)
                passed(n2_ready, k + 1)
                sp.dma_start(xr[:, :, :], x[b, rows, :].rearrange("(t p) d -> p t d", p=P)).then_inc(xr_loaded, 16)
                passed(x1_ready, k + 1)
                sp.dma_start(x1_dram[b, rows, :].rearrange("(t p) d -> p t d", p=P), xr[:, :, :]).then_inc(x1_stored, 16)
                passed(n2_ready, k + 2)
                sp.dma_start(n_dram[b, rows, :].rearrange("(t p) d -> p t d", p=P), n2[:, :, :]).then_inc(n_stored, 16)

            load_x(0)
            with sp.Fori(1, B) as b:
                passed(t1_done, b * 4)
                load_x(b)
                for half in range(2):
                    half_dmas(b - 1, half)
            for half in range(2):
                half_dmas(B - 1, half)
            sp.wait_ge(x1_stored, 16 + 32 * B)
            sp.wait_ge(n_stored, 16 + 32 * B)

        @block.tensor
        def _(pe):
            def product(out, hi, lo, x_hi, x_lo, first, last):
                nc.tensor.matmul(out, hi, x_hi, start=first, stop=False)
                nc.tensor.matmul(out, hi, x_lo, start=False, stop=False)
                return nc.tensor.matmul(out, lo, x_hi, start=False, stop=last)

            def product_t(out, x_hi, x_lo, hi, lo, first, last):
                nc.tensor.matmul(out, x_hi, hi, start=first, stop=False)
                nc.tensor.matmul(out, x_hi, lo, start=False, stop=False)
                return nc.tensor.matmul(out, x_lo, hi, start=False, stop=last)

            def a_stage(b, a):
                if a == 1:
                    pe.wait_ge(xn_ready, b + 1)
                    pe.wait_ge(bx_ready, b * NU + 2)
                    for n in range(4):
                        half, c = n // 2, n % 2
                        for t in range(HT):
                            i = nc.tensor.transpose(banks[n][:, t * P:(t + 1) * P],
                                                    x_in[:, half * HT + t, c * P:(c + 1) * P], ident[:, :])
                        i.then_inc(t1_done, 1)
                if a == 2:
                    for n in range(4):
                        half, o = n // 2, n % 2
                        cols = slice(half * HALF, (half + 1) * HALF)
                        pe.wait_ge(xt_lo_ready, b * 4 + 2 * half + 2)
                        for c in range(DC):
                            i = product(banks[U_BANKS[n]][:, :], W(w_hi, W1_AT, c, D, o * P), W(w_lo, W1_AT, c, D, o * P),
                                        xt_hi[:, c, cols], xt_lo[:, c, cols], c == 0, c == DC - 1)
                        i.then_inc(u_done, 1)

            def dl_a(b, n):
                half, j = UNITS[n]
                cols = slice(half * HALF, (half + 1) * HALF)
                for at, bank, done, free in ((DL_AT, n % 2, dl_done, delta_ready), (A_AT, 2 + n % 2, a_done, da_ready)):
                    pe.wait_ge(free, b * NU + n + 1)
                    for c in range(DC):
                        i = product(banks[bank][:, :], W(w_hi, at, c, H, j * P), W(w_lo, at, c, H, j * P),
                                    xs_hi[:, c, cols], xs_lo[:, c, cols], c == 0, c == DC - 1)
                    i.then_inc(done, 1)

            def b_unit(b, n):
                half, j = UNITS[n]
                cols = slice(half * HALF, (half + 1) * HALF)
                pe.wait_ge(bx_ready, b * NU + n + 1)
                if n == 0 and not (isinstance(b, int) and b == 0):
                    pe.wait_ge(s_hi_ready, b * 4)
                for c in range(DC):
                    i = product(banks[4 + n % 2][:, :], W(w_hi, B_AT, c, H, j * P), W(w_lo, B_AT, c, H, j * P),
                                xs_hi[:, c, cols], xs_lo[:, c, cols], c == 0, c == DC - 1)
                i.then_inc(b_done, 1)

            def c_step(b, n):
                if n == 0:
                    pe.wait_ge(u_copied, b * 4 + 4)
                    pe.wait_ge(xs_lo_ready, b + 1)
                if n < NU:
                    dl_a(b, n)
                if 1 <= n <= NU:
                    b_unit(b, n - 1)

            def d_stage(k, half, d):
                if d == 1:
                    cols = slice(half * HALF, (half + 1) * HALF)
                    if half == 0:
                        pe.wait_ge(slots_ready, k + 1)
                    else:
                        pe.wait_ge(bx_ready, (k - 1) * (NU // 2) + NU + 2)
                    for o in range(DC):
                        out = banks[S_BANKS[half][o]][:, :]
                        for c in range(DC):
                            product(out, W(w_hi, DD_AT, c, D, o * P), W(w_lo, DD_AT, c, D, o * P),
                                    xs_hi[:, c, cols], xs_lo[:, c, cols], c == 0, False)
                        if o == 0:
                            pe.wait_ge(h_lo_ready, k * HC + HC + 2)
                        for c in range(HC):
                            i = product(out, W(w_hi, C_AT, c, D, o * P), W(w_lo, C_AT, c, D, o * P),
                                        HH[half][0][:, c, :], HH[half][1][:, c, :], False, c == HC - 1)
                        i.then_inc(s_done, 1)
                if d == 2:
                    pe.wait_ge(s_lo_ready, k + 1)
                    pe.wait_ge(s_hi_ready, 2 * k + 2)
                    pe.wait_ge(slots_ready, k + 1)
                    for o in range(DC):
                        for c in range(DC):
                            i = product(banks[6 + o][:, :], W(w_hi, W2_AT, c, D, o * P), W(w_lo, W2_AT, c, D, o * P),
                                        s_out_hi[:, c, :], s_out_lo[:, c, :], c == 0, c == DC - 1)
                        i.then_inc(g_done, 1)
                if d == 4:
                    pe.wait_ge(g_ready, 2 * k + 2)
                    pe.wait_ge(z_lo_ready, k + 1)
                    for t in range(HT):
                        at = (t % 2) * D
                        out = banks[6 + t // 2][:, at:at + D]
                        toks = slice(t * P, (t + 1) * P)
                        for c in range(DC):
                            w3 = slice(W3_AT + c * D, W3_AT + (c + 1) * D)
                            product_t(out, z_hi[:, c, toks], z_lo[:, c, toks], w_hi[:, w3], w_lo[:, w3], c == 0, False)
                        for c in range(DC):
                            part = banks[6 + t // 2][:, at + c * P:at + (c + 1) * P]
                            nc.tensor.matmul(part, s_out_hi[:, c, toks], ident_r[:, :], start=False, stop=False)
                            i = nc.tensor.matmul(part, s_out_lo[:, c, toks], ident_r[:, :], start=False, stop=c == DC - 1)
                        i.then_inc(w3_done, 1)
                if d == 7:
                    pe.wait_ge(n2_ready, k + 2)
                    for c in range(DC):
                        for t in range(HT):
                            i = nc.tensor.transpose(banks[6 + c][:, t * P:(t + 1) * P], n2[:, t, c * P:(c + 1) * P],
                                                    ident[:, :])
                        i.then_inc(t2_done, 1)
                if d == 8:
                    pe.wait_ge(xn_lo_ready, 2 * k + 2)
                    for c in range(DC):
                        rt = slice(RT_AT + c * E, RT_AT + (c + 1) * E)
                        i = product(banks[6][0:E, :], w_hi[:, rt], w_lo[:, rt], xnt_hi[:, c, :], xnt_lo[:, c, :],
                                    c == 0, c == DC - 1)
                    i.then_inc(lt_done, 1)
                if d == 9:
                    pe.wait_ge(lt_ready, k + 1)
                    for t in range(HT):
                        i = nc.tensor.transpose(banks[7][:, t * P:(t + 1) * P], lt[:, t * P:(t + 1) * P], ident[:, :])
                    i.then_inc(logits_done, 1)
                if d == 10:
                    pe.wait_ge(counted, k + 1)
                    if isinstance(k, int) and k == 0:
                        pe.wait_ge(before_made, 1)
                    nc.tensor.matmul(banks[6][:, 0:E], before[:, :], count[:, :], start=True, stop=True)
                    nc.tensor.matmul(banks[6][:, E:2 * E], ones[:, 0:P], count[:, :], start=True, stop=True).then_inc(counts_done, 1)

            run(pe, a_stage, c_step, d_stage)

        @block.scalar
        def _(act):
            def a_stage(b, a):
                if a == 1:
                    act.wait_ge(s_done, b * 4 + 2)
                    for n in range(4):
                        half, c = n // 2, n % 2
                        act.wait_ge(t1_done, b * 4 + n + 1)
                        nc.scalar.activation(xt_hi[:, c, half * HALF:(half + 1) * HALF], banks[n][:, :],
                                             ACT.Copy).then_inc(xt_hi_ready, 1)
                if a == 2:
                    act.wait_ge(cv_ready, b * 2 + 2)
                    for n in range(4):
                        half, o = n // 2, n % 2
                        act.wait_ge(u_done, b * 4 + n + 1)
                        nc.scalar.activation(u[:, o, 1 + half * HALF:1 + (half + 1) * HALF],
                                             banks[U_BANKS[n]][:, :], ACT.Copy).then_inc(u_copied, 1)
                if a == 3:
                    for o in range(DC):
                        act.wait_ge(u_copied, b * 4 + 3 + o)
                        nc.scalar.activation(cv[:, o, :], u[:, o, 1:L + 1], ACT.Identity,
                                             bias=vec[:, V_CB + o:V_CB + o + 1],
                                             scale=vec[:, V_CW + 3 * o + 1:V_CW + 3 * o + 2]).then_inc(cv0_ready, 1)
                if a == 4:
                    for o in range(DC):
                        act.wait_ge(cv_ready, b * 2 + o + 3)
                        nc.scalar.activation(cv[:, o, :], cv[:, o, :], ACT.Silu).then_inc(silu_ready, 1)
                    for o in range(DC):
                        act.wait_ge(silu_ready, b * 2 + o + 1)
                        nc.scalar.activation(xs_hi[:, o, :], cv[:, o, :], ACT.Copy).then_inc(xs_hi_ready, 1)

            def c_step(b, n):
                if n == 0 or any(d in (2, 9, 11) for _, d in BESIDE_C[n - 1]):
                    act.preload_act_table_set("natural_log_exp_and_others")
                if n < NU:
                    half, j = UNITS[n]
                    act.wait_ge(dl_done, b * NU + n + 1)
                    act.wait_ge(da_ready, b * NU + n + 1)
                    nc.scalar.activation(delta[:, n % 2, :], banks[n % 2][:, :], ACT.Exp,
                                         bias=vec[:, V_DLB + j:V_DLB + j + 1]).then_inc(exp_ready, 1)
                if 1 <= n <= NU:
                    act.wait_ge(da_ready, b * NU + n - 1 + 3)
                    nc.scalar.activation(decay[:, (n - 1) % 2, :], decay[:, (n - 1) % 2, :], ACT.Exp,
                                         scale=-1.0).then_inc(abar_ready, 1)
                if n < NU:
                    act.wait_ge(capped, b * NU + n + 1)
                    nc.scalar.activation(delta[:, n % 2, :], delta[:, n % 2, :], ACT.Ln, bias=1.0).then_inc(ln_ready, 1)
                if n >= 2:
                    half, j = UNITS[n - 2]
                    act.wait_ge(h_ready, b * NU + n - 2 + 1)
                    nc.scalar.activation(HH[half][0][:, j, :], h[:, n % 2, :], ACT.Copy).then_inc(h_hi_ready, 1)

            def d_stage(k, half, d):
                if d == 1:
                    act.wait_ge(w3_done, k * 4 + 4)
                    for o in range(DC):
                        act.wait_ge(s_done, 2 * k + o + 3)
                        bank = banks[S_BANKS[half][o]]
                        nc.scalar.activation(s[:, o, :], bank[:, :], ACT.Identity, bias=cdb[:, o:o + 1]).then_inc(s_ready, 1)
                        nc.scalar.activation(s_out_hi[:, o, :], bank[:, :], ACT.Identity,
                                             bias=cdb[:, o:o + 1]).then_inc(s_hi_ready, 1)
                if d == 2:
                    for o in range(DC):
                        act.wait_ge(g_done, 2 * k + o + 1)
                        nc.scalar.activation(g[:, o, :], banks[6 + o][:, :], ACT.Silu).then_inc(g_ready, 1)
                if d == 3:
                    act.wait_ge(z_ready, k + 1)
                    nc.scalar.activation(z_hi[:, :, :], g[:, :, :], ACT.Copy).then_inc(z_hi_ready, 1)
                if d == 7:
                    for c in range(DC):
                        act.wait_ge(t2_done, 2 * k + c + 1)
                        nc.scalar.activation(xnt_hi[:, c, :], banks[6 + c][:, :], ACT.Identity,
                                             bias=vec[:, V_BE + c:V_BE + c + 1],
                                             scale=vec[:, V_G + c:V_G + c + 1]).then_inc(xn_hi_ready, 1)
                if d == 8:
                    act.wait_ge(lt_done, k + 1)
                    nc.scalar.activation(lt[0:E, :], banks[6][0:E, :], ACT.Copy).then_inc(lt_ready, 1)
                if d == 9:
                    act.wait_ge(shifted, k + 1)
                    nc.scalar.activation(prob[:, :, :], prob[:, :, :], ACT.Exp).then_inc(probs_exp, 1)

            run(act, a_stage, c_step, d_stage)

        @block.vector
        def _(dve):
            def moments(source, stats, out, n, order, count, ready):
                for t in range(n):
                    i = nc.vector.bn_stats(stats[:, t, :], source(t))
                i.then_inc(order, 1)
                dve.wait_ge(order, count)
                dve.sem_inc(stats_seen, 1)
                for t in range(n):
                    i = nc.vector.bn_aggr(out[:, t, :], stats[:, t, :])
                i.then_inc(ready, 1)

            def a_stage(b, a):
                if a == 0:
                    dve.wait_ge(x_loaded, b * 16 + 16)
                    moments(lambda t: x_in[:, t, :], st, mv, LT, a_order, b * 3 + 1, mv_ready)
                    dve.wait_ge(mv_ready, b + 1)
                    dve.wait_ge(rs_ready, b + 1)
                    for t in range(LT):
                        i = nc.vector.tensor_scalar(x_in[:, t, :], x_in[:, t, :], mv[:, t, 0:1], rs[:, t:t + 1],
                                                    ALU.subtract, ALU.mult)
                    i.then_inc(xn_ready, 1)
                if a == 1:
                    for n in range(4):
                        half, c = n // 2, n % 2
                        dve.wait_ge(xt_hi_ready, b * 4 + n + 1)
                        cols = slice(half * HALF, (half + 1) * HALF)
                        nc.vector.tensor_tensor(xt_lo[:, c, cols], banks[n][:, :], xt_hi[:, c, cols],
                                                ALU.subtract).then_inc(xt_lo_ready, 1)
                if a == 3:
                    for o in range(DC):
                        dve.wait_ge(cv0_ready, b * 2 + o + 1)
                        nc.vector.scalar_tensor_tensor(out=cv[:, o, :], in0=u[:, o, 0:L],
                                                       scalar=vec[:, V_CW + 3 * o:V_CW + 3 * o + 1],
                                                       in1=cv[:, o, :], op0=ALU.mult, op1=ALU.add).then_inc(a_order, 1)
                        dve.wait_ge(a_order, b * 3 + 2 + o)
                        nc.vector.scalar_tensor_tensor(out=cv[:, o, :], in0=u[:, o, 2:L + 2],
                                                       scalar=vec[:, V_CW + 3 * o + 2:V_CW + 3 * o + 3],
                                                       in1=cv[:, o, :], op0=ALU.mult, op1=ALU.add).then_inc(cv_ready, 1)
                if a == 5:
                    dve.wait_ge(xs_hi_ready, b * 2 + 2)
                    nc.vector.tensor_tensor(xs_lo[:, :, :], cv[:, :, :], xs_hi[:, :, :], ALU.subtract).then_inc(xs_lo_ready, 1)

            def c_step(b, n):
                if n < NU:
                    dve.wait_ge(exp_ready, b * NU + n + 1)
                    nc.vector.tensor_scalar(delta[:, n % 2, :], delta[:, n % 2, :], EXP_CAP, None, ALU.min).then_inc(capped, 1)
                if 1 <= n <= NU:
                    m = n - 1
                    half, j = UNITS[m]
                    dve.wait_ge(ln_ready, b * NU + m + 1)
                    nc.vector.scalar_tensor_tensor(out=delta[:, m % 2, :], in0=banks[m % 2][:, :],
                                                   scalar=vec[:, V_DLB + j:V_DLB + j + 1], in1=delta[:, m % 2, :],
                                                   op0=ALU.add, op1=ALU.max).then_inc(delta_ready, 1)
                    dve.wait_ge(delta_ready, b * NU + m + 3)
                    dve.wait_ge(a_done, b * NU + m + 1)
                    nc.vector.scalar_tensor_tensor(out=decay[:, m % 2, :], in0=banks[2 + m % 2][:, :],
                                                   scalar=vec[:, V_AB + j:V_AB + j + 1], in1=delta[:, m % 2, :],
                                                   op0=ALU.add, op1=ALU.mult).then_inc(da_ready, 1)
                if n >= 2:
                    m = n - 2
                    half, j = UNITS[m]
                    dve.wait_ge(abar_ready, b * NU + m + 1)
                    first = half == 0
                    if 1 <= m < HC:
                        dve.wait_ge(carried, b * 2 * HC + 2 * m - 1)
                    if m == HC:
                        dve.wait_ge(carried, b * 2 * HC + 2 * HC)
                    nc.vector.tensor_tensor_scan(a_cum[:, :], decay[:, m % 2, :], zeros[:, 0:HALF],
                                                 1.0 if first else carry_a[:, j:j + 1], ALU.mult, ALU.add).then_inc(acum_ready, 1)
                    dve.wait_ge(acum_ready, b * NU + m + 1)
                    dve.wait_ge(b_done, b * NU + m + 1)
                    nc.vector.scalar_tensor_tensor(out=bx[:, :], in0=banks[4 + m % 2][:, :],
                                                   scalar=vec[:, V_BB + j:V_BB + j + 1], in1=a_cum[:, :],
                                                   op0=ALU.add, op1=ALU.mult).then_inc(bx_ready, 1)
                    dve.wait_ge(bx_ready, b * NU + m + 3)
                    dve.wait_ge(h_lo_ready, b * NU + m + 1)
                    nc.vector.tensor_tensor_scan(h[:, m % 2, :], ones[:, 0:HALF], bx[:, :],
                                                 0.0 if first else carry_h[:, j:j + 1], ALU.mult, ALU.add).then_inc(h_ready, 1)

            def d_stage(k, half, d):
                if d == 2:
                    dve.wait_ge(s_hi_ready, 2 * k + 2)
                    nc.vector.tensor_tensor(s_out_lo[:, :, :], s[:, :, :], s_out_hi[:, :, :], ALU.subtract).then_inc(s_lo_ready, 1)
                if d == 3:
                    dve.wait_ge(g_ready, 2 * k + 2)
                    nc.vector.tensor_tensor(g[:, :, :], s[:, :, :], g[:, :, :], ALU.mult).then_inc(z_ready, 1)
                if d == 4:
                    dve.wait_ge(z_hi_ready, k + 1)
                    nc.vector.tensor_tensor(z_lo[:, :, :], g[:, :, :], z_hi[:, :, :], ALU.subtract).then_inc(z_lo_ready, 1)
                out = lambda t: banks[6 + t // 2][:, (t % 2) * D:(t % 2 + 1) * D]
                if d == 5:
                    dve.wait_ge(w3_done, k * 4 + 8)
                    moments(out, st2, mv2, HT, d_order, k * 2 + 1, mv2_ready)
                if d == 6:
                    dve.wait_ge(rs2_ready, k + 1)
                    for t in range(HT):
                        i = nc.vector.tensor_scalar(y_n[:, t, :], out(t), mv2[:, t, 0:1], rs2[:, t:t + 1],
                                                    ALU.subtract, ALU.mult)
                    i.then_inc(yn_ready, 1)
                    dve.wait_ge(yn_ready, k + 1)
                    dve.wait_ge(xr_loaded, k * 16 + 16)
                    nc.vector.tensor_tensor(xr[:, :, :], xr[:, :, :], y_n[:, :, :], ALU.add).then_inc(x1_ready, 1)
                    dve.wait_ge(x1_ready, k + 1)
                    moments(lambda t: xr[:, t, :], st2[:, HT:, :], mv2[:, HT:, :], HT, d_order, k * 2 + 2, mv3_ready)
                if d == 7:
                    dve.wait_ge(rs4_ready, k + 1)
                    dve.wait_ge(n_stored, k * 16 + 16)
                    if not (isinstance(k, int) and k == 0):
                        dve.wait_ge(scattered, k * 16 * HT * K)
                    for t in range(HT):
                        i = nc.vector.tensor_scalar(n2[:, t, :], xr[:, t, :], mv2[:, HT + t, 0:1], rs4[:, t:t + 1],
                                                    ALU.subtract, ALU.mult)
                    i.then_inc(n2_ready, 1)
                if d == 8:
                    for c in range(DC):
                        dve.wait_ge(xn_hi_ready, 2 * k + c + 1)
                        nc.vector.tensor_scalar(g[:, c, :], banks[6 + c][:, :], vec[:, V_G + c:V_G + c + 1],
                                                vec[:, V_BE + c:V_BE + c + 1], ALU.mult, ALU.add).then_inc(xn_f_ready, 1)
                        dve.wait_ge(xn_f_ready, 2 * k + c + 1)
                        nc.vector.tensor_tensor(xnt_lo[:, c, :], g[:, c, :], xnt_hi[:, c, :],
                                                ALU.subtract).then_inc(xn_lo_ready, 1)
                tiles = bass.ds(k * HT, HT)
                def link(i, n):
                    i.then_inc(route_steps, 1)
                    dve.wait_ge(route_steps, k * LINKS + n + 2)
                def wide(v):
                    return v.unsqueeze(2).to_broadcast([P, HT, E])
                if d == 9:
                    l = banks[7][:, :].rearrange("p (t e) -> p t e", e=P)[:, :, 0:E]
                    dve.wait_ge(logits_done, k + 1)
                    link(nc.vector.tensor_reduce(top[:, :], l, AX.X, ALU.max), 0)
                    nc.vector.tensor_tensor(prob[:, :, :], l, wide(top[:, :]), ALU.subtract).then_inc(shifted, 1)
                if d == 10:
                    dve.wait_ge(probs_exp, k + 1)
                    link(nc.vector.tensor_reduce(total[:, :], prob[:, :, :], AX.X, ALU.add), 1)
                    link(nc.vector.reciprocal(total[:, :], total[:, :]), 2)
                    link(nc.vector.tensor_tensor(prob[:, :, :], prob[:, :, :], wide(total[:, :]), ALU.mult), 3)
                    for m in range(K):
                        v, pk = val[m][:, tiles], pick[m][:, tiles, :]
                        n = 4 + m * 6
                        link(nc.vector.tensor_reduce(v, prob[:, :, :], AX.X, ALU.max), n)
                        link(nc.vector.tensor_tensor(score[:, :, :], prob[:, :, :], wide(v), ALU.is_equal), n + 1)
                        link(nc.vector.tensor_tensor(score[:, :, :], score[:, :, :], desc[:, :, :], ALU.mult), n + 2)
                        link(nc.vector.tensor_reduce(best[:, :], score[:, :, :], AX.X, ALU.max), n + 3)
                        link(nc.vector.tensor_tensor(pk, score[:, :, :], wide(best[:, :]), ALU.is_equal), n + 4)
                        if m == 0:
                            link(nc.vector.scalar_tensor_tensor(out=prob[:, :, :], in0=pk, scalar=-2.0,
                                                                in1=prob[:, :, :], op0=ALU.mult, op1=ALU.add), n + 5)
                    link(nc.vector.tensor_tensor(both[:, :, :].rearrange("p e t -> p t e"), pick[0][:, tiles, :],
                                                 pick[1][:, tiles, :], ALU.add), 15)
                    nc.vector.tensor_tensor_scan(run_sum[:, :, :].rearrange("p e t -> p (e t)"), ones[:, 0:E * HT],
                                                 both[:, :, :].rearrange("p e t -> p (e t)"), 0.0, ALU.mult, ALU.add)
                    nc.vector.tensor_reduce(count[:, :], both[:, :, :], AX.X, ALU.add).then_inc(counted, 1)
                if d == 11:
                    dve.wait_ge(counts_done, k + 1)
                    link(nc.vector.tensor_tensor(offset[:, :], fill[:, :], banks[6][:, 0:E], ALU.add), 16)
                    nc.vector.tensor_tensor(fill[:, :], fill[:, :], banks[6][:, E:2 * E], ALU.add)
                    link(nc.vector.tensor_tensor(offset[:, :], offset[:, :], count[:, :], ALU.add), 17)
                    link(nc.vector.tensor_tensor(offset[:, :], offset[:, :], run_sum[:, :, HT - 1], ALU.subtract), 18)
                    link(nc.vector.tensor_tensor(run_sum[:, :, :], run_sum[:, :, :],
                                                 offset[:, :].unsqueeze(2).to_broadcast([P, E, HT]), ALU.add), 19)
                    for m in range(K):
                        link(nc.vector.tensor_tensor(score[:, :, :], pick[m][:, tiles, :],
                                                     run_sum[:, :, :].rearrange("p e t -> p t e"), ALU.mult), 20 + 2 * m)
                        link(nc.vector.tensor_reduce(slot_half[:, :, m:m + 1], score[:, :, :], AX.X, ALU.add), 21 + 2 * m)
                    nc.vector.tensor_copy(slot_now[:, :, :], slot_half[:, :, :]).then_inc(slots_ready, 1)
                    nc.vector.tensor_copy(slot_f[:, tiles, :], slot_half[:, :, :])

            for pad in (0, L + 1):
                nc.vector.memset(u[:, :, pad:pad + 1], 0.0)
            nc.vector.tensor_tensor(cdb[:, :], vec[:, V_CDB:V_CDB + DC], vec[:, V_CDB + DC:V_CDB + 2 * DC],
                                    ALU.add).then_inc(start_made, 1)
            for e in range(E):
                nc.vector.memset(desc[:, :, e:e + 1], float(E - e))
                i = nc.vector.memset(fill[:, e:e + 1], float(e * CAP - 1))
            i = nc.vector.memset(lt[:, :], 0.0)
            i.then_inc(start_made, 1)
            dve.wait_ge(start_made, 2)
            dve.sem_inc(slots_ready, 1)
            dve.sem_inc(route_steps, 1)
            dve.sem_inc(delta_ready, 2)
            dve.sem_inc(da_ready, 2)
            dve.sem_inc(bx_ready, 2)
            dve.sem_inc(cv_ready, 2)
            dve.sem_inc(n2_ready, 1)
            run(dve, a_stage, c_step, d_stage)

        @block.gpsimd
        def _(pool):
            def chain(order, first, steps):
                for n, (out, x0, x1, op) in enumerate(steps):
                    i = nc.gpsimd.tensor_tensor(out, x0, x1, op)
                    if n < len(steps) - 1:
                        i.then_inc(order, 1)
                        pool.wait_ge(order, first + n + 1)
                return i

            def a_stage(b, a):
                if a == 0:
                    pool.wait_ge(mv_ready, b + 1)
                    chain(pool_a, b, [(ve[:, :], mv[:, :, 1], eps[:, 0:LT], ALU.add),
                                      (rs[:, :], ve[:, :], neg_half[:, 0:LT], ALU.pow)]).then_inc(rs_ready, 1)

            def c_step(b, n):
                if n >= 2:
                    m = n - 2
                    half, j = UNITS[m]
                    if half == 0:
                        pool.wait_ge(acum_ready, b * NU + m + 1)
                        nc.gpsimd.tensor_tensor(carry_a[:, j:j + 1], a_cum[:, HALF - 1:HALF], ones[:, 0:1],
                                                ALU.mult).then_inc(carried, 1)
                        pool.wait_ge(h_ready, b * NU + m + 1)
                        nc.gpsimd.tensor_tensor(carry_h[:, j:j + 1], h[:, m % 2, HALF - 1:HALF], ones[:, 0:1],
                                                ALU.mult).then_inc(carried, 1)
                    pool.wait_ge(h_hi_ready, b * NU + m + 1)
                    nc.gpsimd.tensor_tensor(HH[half][1][:, j, :], h[:, m % 2, :], HH[half][0][:, j, :],
                                            ALU.subtract).then_inc(h_lo_ready, 1)

            def d_stage(k, half, d):
                if d == 5:
                    pool.wait_ge(mv2_ready, k + 1)
                    chain(pool_d, k * 7, [(ve2[:, :], mv2[:, 0:HT, 1], eps[:, 0:HT], ALU.add),
                                          (rs2[:, :], ve2[:, :], neg_half[:, 0:HT], ALU.pow)]).then_inc(rs2_ready, 1)
                if d == 6:
                    var = mv2[:, HT:2 * HT, 1]
                    pool.wait_ge(mv3_ready, k + 1)
                    chain(pool_d, k * 7 + 1, [(ve3[:, :], var, eps[:, 0:HT], ALU.add),
                                              (rs3[:, :], ve3[:, :], neg_half[:, 0:HT], ALU.pow),
                                              (ve4[:, :], var, rs3[:, :], ALU.mult),
                                              (ve4[:, :], ve4[:, :], rs3[:, :], ALU.mult),
                                              (ve4[:, :], ve4[:, :], eps[:, 0:HT], ALU.add),
                                              (ve4[:, :], ve4[:, :], neg_half[:, 0:HT], ALU.pow),
                                              (rs4[:, :], ve4[:, :], rs3[:, :], ALU.mult)]).then_inc(rs4_ready, 1)

                if d == 11:
                    pool.wait_ge(slots_ready, k + 2)
                    pool.sem_inc(pool_seen, 1)
                    for t in range(HT):
                        for m in range(K):
                            nc.gpsimd.indirect_dma_start(
                                out=xs_dram, out_offset=bass.IndirectOffsetOnAxis(ap=slot_now[:, t, m:m + 1], axis=0),
                                in_=n2[:, t, :], in_offset=None).then_inc(scattered, 16)

            nc.gpsimd.memset(before[:, :], 1.0).then_inc(before_set, 1)
            pool.wait_ge(before_set, 1)
            nc.gpsimd.affine_select(out=before[:, :], in_=before[:, :], compare_op=ALU.is_gt, fill=0.0,
                                    base=0, pattern=[[1, P]], channel_multiplier=-1).then_inc(before_made, 1)
            pool.sem_inc(h_lo_ready, 2)
            pool.sem_inc(s_done, 2)
            pool.sem_inc(w3_done, 4)
            pool.sem_inc(x1_stored, 16)
            pool.sem_inc(n_stored, 16)
            run(pool, a_stage, c_step, d_stage)
            pool.wait_ge(scattered, 2 * B * 16 * HT * K)



G = 384
GT = G // P
NG = (T * K + E * (G - 1)) // G
CW = 4 * P + D
MAXG = T // G + 1
CAP = T + G
TC = 4
NC = TT // TC


def token_rows(dram):
    return dram.rearrange("b l d -> (b l) d").rearrange("(c t p) d -> c p t d", t=TC, p=P)


def plan(nc, shared, s_hi, s_lo, xs_dram, pick, val, slot_f, fill, slot, weight, group_expert, group_row, zeros):
    with ExitStack() as ctx:
        def sb(name, shape, dt=F32):
            return ctx.enter_context(nc.sbuf_tensor(name, shape, dt))
        def sem(name):
            return ctx.enter_context(nc.semaphore(name))
        raw_s = sb("raw_s", [P, S_COLS])
        start_row = sb("start_row", [P, E])
        end_row = sb("end_row", [P, E], I32)
        n_all = sb("n_all", [P, E])
        limits = sb("limits", [P, E, MAXG])
        over = sb("over", [P, E, MAXG])
        groups = sb("groups", [P, E])
        group_end = sb("group_end", [P, E])
        shift = sb("shift", [P, E])
        n_one = sb("n_one", [P, E])
        total = sb("w_total", [P, TT])
        moved = sb("moved", [P, TT, E])
        step_f = sb("step_f", [P, TT])
        group_no = sb("group_no", [P, NG + 1, E])
        past = sb("past", [P, NG + 1, E])
        number = sb("number", [P, NG + 1])
        expert_f = sb("expert_f", [P, NG + 1])
        passed = sb("passed", [P, NG + 1])
        row_f = sb("row_f", [P, NG + 1])
        steps, ends_ready, ends_cleared = sem("plan_steps"), sem("ends_ready"), sem("ends_cleared")
        loaded = [sem(f"shared_loaded{i}") for i in range(len(shared))]
        s_hi_ready = sem("shared_hi")
        block = ctx.enter_context(nc.Block())

        @block.sync
        def _(sp):
            for n, (at, src, chunks) in enumerate(shared):
                sp.dma_start(raw_s[:, at:at + chunks * src.shape[1]].rearrange("p (c n) -> p c n", c=chunks),
                             src.rearrange("(c p) n -> p c n", p=P)).then_inc(loaded[n], 16)
            sp.wait_ge(ends_ready, 1)
            for e in range(E):
                row = sp.value_load(end_row[0:1, e:e + 1], min_val=e * CAP, max_val=e * CAP + T)
                sp.dma_start(xs_dram[bass.ds(row, G), :].rearrange("(p m) d -> p (m d)", p=P),
                             zeros[:, 0:GT * D]).then_inc(ends_cleared, 16)
            sp.wait_ge(ends_cleared, 16 * E)

        @block.scalar
        def _(act):
            for n, (at, src, chunks) in enumerate(shared):
                cols = slice(at, at + chunks * src.shape[1])
                act.wait_ge(loaded[n], 16)
                nc.scalar.activation(s_hi[:, cols], raw_s[:, cols], ACT.Copy).then_inc(s_hi_ready, 1)

        @block.gpsimd
        def _(pool):
            for n, (at, src, chunks) in enumerate(shared):
                cols = slice(at, at + chunks * src.shape[1])
                pool.wait_ge(s_hi_ready, n + 1)
                nc.gpsimd.tensor_tensor(s_lo[:, cols], raw_s[:, cols], s_hi[:, cols], ALU.subtract)

        @block.vector
        def _(dve):
            n = [0]
            def link(i):
                n[0] += 1
                i.then_inc(steps, 1)
                dve.wait_ge(steps, n[0])
            nc.vector.memset(n_one[:, :], 1.0)
            for e in range(E):
                i = nc.vector.memset(start_row[:, e:e + 1], float(e * CAP))
            link(i)
            nc.vector.tensor_scalar(end_row[:, :], fill[:, :], 1.0, None, ALU.add).then_inc(ends_ready, 1)
            nc.vector.tensor_tensor(n_all[:, :], fill[:, :], start_row[:, :], ALU.subtract)
            for j in range(MAXG):
                nc.vector.memset(limits[:, :, j:j + 1], float(j * G - 1))
            for g in range(NG + 1):
                i = nc.vector.memset(group_no[:, g:g + 1, :], float(g))
            for g in range(NG + 1):
                i = nc.vector.memset(number[:, g:g + 1], float(g))
            link(i)
            link(nc.vector.tensor_tensor(over[:, :, :], n_all[:, :].unsqueeze(2).to_broadcast([P, E, MAXG]),
                                         limits[:, :, :], ALU.is_gt))
            link(nc.vector.tensor_reduce(groups[:, :], over[:, :, :], AX.X, ALU.add))
            link(nc.vector.tensor_tensor_scan(group_end[:, :], n_one[:, :], groups[:, :], 0.0, ALU.mult, ALU.add))
            link(nc.vector.tensor_tensor(past[:, :, :], group_no[:, :, :],
                                         group_end[:, :].unsqueeze(1).to_broadcast([P, NG + 1, E]), ALU.is_ge))
            link(nc.vector.tensor_reduce(expert_f[:, :], past[:, :, 0:E - 1], AX.X, ALU.add))
            nc.vector.tensor_copy(group_expert[:, :], expert_f[:, :])
            link(nc.vector.tensor_tensor(group_no[:, :, 0:E - 1], past[:, :, 0:E - 1],
                                         groups[:, 0:E - 1].unsqueeze(1).to_broadcast([P, NG + 1, E - 1]), ALU.mult))
            link(nc.vector.tensor_reduce(passed[:, :], group_no[:, :, 0:E - 1], AX.X, ALU.add))
            link(nc.vector.tensor_tensor(row_f[:, :], number[:, :], passed[:, :], ALU.subtract))
            link(nc.vector.tensor_tensor(number[:, :], row_f[:, :], past[:, :, E - 1], ALU.mult))
            link(nc.vector.tensor_tensor(row_f[:, :], row_f[:, :], number[:, :], ALU.subtract))
            link(nc.vector.tensor_scalar(row_f[:, :], row_f[:, :], float(G), None, ALU.mult))
            link(nc.vector.scalar_tensor_tensor(out=row_f[:, :], in0=expert_f[:, :], scalar=float(CAP), in1=row_f[:, :],
                                                op0=ALU.mult, op1=ALU.add))
            nc.vector.tensor_copy(group_row[:, :], row_f[:, :])
            link(nc.vector.tensor_tensor(shift[:, :], group_end[:, :], groups[:, :], ALU.subtract))
            link(nc.vector.scalar_tensor_tensor(out=shift[:, :], in0=shift[:, :], scalar=float(G), in1=start_row[:, :],
                                                op0=ALU.mult, op1=ALU.subtract))
            for k in range(K):
                link(nc.vector.tensor_tensor(moved[:, :, :], pick[k][:, :, :],
                                             shift[:, :].unsqueeze(1).to_broadcast([P, TT, E]), ALU.mult))
                link(nc.vector.tensor_reduce(step_f[:, :], moved[:, :, :], AX.X, ALU.add))
                link(nc.vector.tensor_tensor(slot_f[:, :, k], slot_f[:, :, k], step_f[:, :], ALU.add))
            nc.vector.tensor_copy(slot[:, :, :], slot_f[:, :, :])
            link(nc.vector.tensor_tensor(total[:, :], val[0][:, :], val[1][:, :], ALU.add))
            link(nc.vector.reciprocal(total[:, :], total[:, :]))
            for k in range(K):
                nc.vector.tensor_tensor(weight[:, :, k], val[k][:, :], total[:, :], ALU.mult)


def experts(nc, w_e, xs_dram, y_dram, group_expert, group_row, vec, ident):
    with ExitStack() as ctx:
        def sb(name, shape, dt=F32):
            return ctx.enter_context(nc.sbuf_tensor(name, shape, dt))

        def sem(name):
            return ctx.enter_context(nc.semaphore(name))

        RAW, RING, AHEAD, LAG = 4, FC, 5, 2
        raw = sb("raw", [P, RAW, CW])
        e_hi = sb("e_hi", [P, RING, CW], F32R)
        e_lo = sb("e_lo", [P, RING, CW], F32R)
        rows = sb("x_rows", [P, 2, GT, D])
        xg_hi = sb("xg_hi", [P, 2, DC, G], F32R)
        xg_lo = sb("xg_lo", [P, 2, DC, G], F32R)
        xg_f = sb("xg_f", [P, DC, G])
        gate = sb("gate", [P, 2, G])
        hg_hi = sb("hg_hi", [P, 4, G], F32R)
        hg_lo = sb("hg_lo", [P, 4, G], F32R)
        y = sb("y", [P, 2, GT, D])
        gate_ps = [ctx.enter_context(nc.psum_tensor(f"gate_ps{i}", [P, 512], F32)) for i in range(2)]
        up_ps = [ctx.enter_context(nc.psum_tensor(f"up_ps{i}", [P, 512], F32)) for i in range(2)]
        x_ps = ctx.enter_context(nc.psum_tensor("x_ps", [P, 512], F32))
        down_ps = [ctx.enter_context(nc.psum_tensor(f"down_ps{i}", [P, 512], F32)) for i in range(GT)]
        loaded = [sem(f"chunk_loaded{i}") for i in range(RAW)]
        hi_ready, lo_ready = sem("chunk_hi"), sem("chunk_lo")
        rows_loaded = [sem(f"x_rows_loaded{i}") for i in range(2)]
        x_turned, x_hi_ready, x_f_ready, x_lo_ready = sem("x_turned"), sem("x_hi_ready"), sem("x_f_ready"), sem("x_lo_ready")
        gate_done, up_done, down_done = sem("e_gate_done"), sem("e_up_done"), sem("e_down_done")
        clipped, silu_ready, h_ready = sem("e_clipped"), sem("e_silu"), sem("e_h_ready")
        h_hi_ready, h_lo_ready, y_ready = sem("e_h_hi"), sem("e_h_lo"), sem("e_y_ready")
        y_stored = [sem(f"y_stored{i}") for i in range(2)]
        block = ctx.enter_context(nc.Block())

        def groups(eng, turn):
            turn(0, 0)
            with eng.Fori(0, (NG - 1) // 2) as i:
                for k in range(2):
                    turn(i * 2 + 1 + k, 1 - k)

        assert NG % 2 == 1

        @block.sync
        def _(sp):
            def load_rows(g, par):
                row = sp.value_load(group_row[0:1, bass.ds(g, 1)], min_val=0, max_val=E * CAP - G)
                sp.dma_start(rows[:, par, :, :], xs_dram[bass.ds(row, G), :].rearrange("(t p) d -> p t d", p=P)
                             ).then_inc(rows_loaded[par], 16)

            def load_chunk(g, f, e):
                sp.wait_ge(lo_ready, g * FC + f + 1)
                sp.dma_start(raw[:, f % RAW, :], w_e[e, f, :, :]).then_inc(loaded[f % RAW], 16)

            def store_y(g, par):
                sp.wait_ge(y_ready, g + 2 + 1)
                sp.dma_start(y_dram.rearrange("(g t p) d -> g p t d", t=GT, p=P)[g, :, :, :], y[:, par, :, :]
                             ).then_inc(y_stored[par], 16)

            def expert_of(g):
                return sp.value_load(group_expert[0:1, bass.ds(g, 1)], min_val=0, max_val=E - 1)

            def turn(g, par):
                e = expert_of(g)
                for f in range(FC):
                    load_chunk(g, f, e)
                    if f == 0:
                        if not (isinstance(g, int) and g == 0):
                            sp.wait_ge(x_turned, g * DC)
                        load_rows(g + 1, 1 - par)

            load_rows(0, 0)
            turn(0, 0)
            turn(1, 1)
            turn(2, 0)
            with sp.Fori(0, (NG - 3) // 2) as i:
                for k in range(2):
                    g = i * 2 + 3 + k
                    store_y(g - 3, 0 if k == 0 else 1)
                    turn(g, 1 - k)
            e = expert_of(NG)
            for f in range(AHEAD):
                load_chunk(NG, f, e)
            for g in range(NG - 3, NG):
                store_y(g, g % 2)
            sp.wait_ge(y_stored[0], 16 + 16 * ((NG + 1) // 2))
            sp.wait_ge(y_stored[1], 16 + 16 * (NG // 2))

        @block.tensor
        def _(pe):
            def turn_rows(g, par, c):
                if c == 0:
                    pe.wait_ge(rows_loaded[par], (g_half(g, par)) * 16 + 16)
                pe.wait_ge(x_f_ready, g * DC + c + 1)
                for t in range(GT):
                    i = nc.tensor.transpose(x_ps[:, t * P:(t + 1) * P], rows[:, par, t, c * P:(c + 1) * P], ident[:, :])
                i.then_inc(x_turned, 1)

            def gate_up(g, par, f):
                pe.wait_ge(lo_ready, g * FC + f + 1 + RAW)
                if f == 0:
                    pe.wait_ge(x_lo_ready, g * DC + DC)
                pe.wait_ge(h_ready, g * FC + f + 1)
                for ps, at, done in ((gate_ps, 0, gate_done), (up_ps, 2 * P, up_done)):
                    out = ps[f % 2][:, 0:G]
                    for c in range(DC):
                        cols = slice(at + c * P, at + (c + 1) * P)
                        nc.tensor.matmul(out, e_hi[:, f, cols], xg_hi[:, par, c, :], start=c == 0, stop=False)
                        nc.tensor.matmul(out, e_hi[:, f, cols], xg_lo[:, par, c, :], start=False, stop=False)
                        i = nc.tensor.matmul(out, e_lo[:, f, cols], xg_hi[:, par, c, :], start=False, stop=c == DC - 1)
                    i.then_inc(done, 1)

            def down(g, f):
                pe.wait_ge(h_lo_ready, g * FC + f + 1)
                if f == 0:
                    pe.wait_ge(y_ready, g + 2)
                for t in range(GT):
                    toks = slice(t * P, (t + 1) * P)
                    out = down_ps[t][:, 0:D]
                    nc.tensor.matmul(out, hg_hi[:, f % 4, toks], e_hi[:, f, 4 * P:CW], start=f == 0, stop=False)
                    nc.tensor.matmul(out, hg_hi[:, f % 4, toks], e_lo[:, f, 4 * P:CW], start=False, stop=False)
                    i = nc.tensor.matmul(out, hg_lo[:, f % 4, toks], e_hi[:, f, 4 * P:CW], start=False, stop=f == FC - 1)
                i.then_inc(down_done, 1)

            def turn(g, par):
                for f in range(FC):
                    gate_up(g, par, f)
                    if f >= LAG:
                        down(g, f - LAG)
                    elif not (isinstance(g, int) and g == 0):
                        down(g - 1, FC + f - LAG)
                    if f in (2, 4):
                        turn_rows(g + 1, 1 - par, (f - 2) // 2)

            for c in range(DC):
                turn_rows(0, 0, c)
            groups(pe, turn)
            for f in range(FC - LAG, FC):
                down(NG - 1, f)

        @block.scalar
        def _(act):
            def split(g, f):
                act.wait_ge(loaded[f % RAW], (g * (FC // RAW) + f // RAW) * 16 + 16)
                act.wait_ge(down_done, g * FC + f + 1)
                nc.scalar.activation(e_hi[:, f, :], raw[:, f % RAW, :], ACT.Copy).then_inc(hi_ready, 1)

            def rows_hi(g, par, c):
                act.wait_ge(x_turned, g * DC + c + 1)
                nc.scalar.activation(xg_hi[:, par, c, :], x_ps[:, 0:G], ACT.Identity,
                                     bias=vec[:, V_BE + c:V_BE + c + 1],
                                     scale=vec[:, V_G + c:V_G + c + 1]).then_inc(x_hi_ready, 1)

            def turn(g, par):
                for f in range(FC):
                    act.wait_ge(clipped, g * FC + f + 1)
                    nc.scalar.activation(gate[:, f % 2, :], gate[:, f % 2, :], ACT.Silu).then_inc(silu_ready, 1)
                    ahead = f + AHEAD
                    split(g + ahead // FC, ahead % FC)
                    if f in (3, 5):
                        rows_hi(g + 1, 1 - par, (f - 3) // 2)
                    act.wait_ge(h_ready, g * FC + f + 1 + 2)
                    nc.scalar.activation(hg_hi[:, f % 4, :], gate[:, f % 2, :], ACT.Copy).then_inc(h_hi_ready, 1)

            act.sem_inc(down_done, FC)
            for c in range(DC):
                rows_hi(0, 0, c)
            for f in range(AHEAD):
                split(0, f)
            groups(act, turn)

        @block.vector
        def _(dve):
            def rows_lo(g, par, c):
                dve.wait_ge(x_hi_ready, g * DC + c + 1)
                nc.vector.tensor_scalar(xg_f[:, c, :], x_ps[:, 0:G], vec[:, V_G + c:V_G + c + 1],
                                        vec[:, V_BE + c:V_BE + c + 1], ALU.mult, ALU.add).then_inc(x_f_ready, 1)
                dve.wait_ge(x_f_ready, g * DC + c + 2)
                nc.vector.tensor_tensor(xg_lo[:, par, c, :], xg_f[:, c, :], xg_hi[:, par, c, :],
                                        ALU.subtract).then_inc(x_lo_ready, 1)

            def copy_y(g, par):
                dve.wait_ge(down_done, (g + 1) * FC + FC)
                dve.wait_ge(y_stored[par], (g_half(g, par)) * 16 + 16)
                for t in range(GT):
                    i = nc.vector.tensor_copy(y[:, par, t, :], down_ps[t][:, 0:D])
                i.then_inc(y_ready, 1)

            def turn(g, par):
                for f in range(FC):
                    if f == LAG and not (isinstance(g, int) and g == 0):
                        copy_y(g - 1, 1 - par)
                    dve.wait_ge(gate_done, g * FC + f + 1)
                    nc.vector.tensor_scalar(gate[:, f % 2, :], gate_ps[f % 2][:, 0:G], CLIP, -CLIP,
                                            ALU.min, ALU.max).then_inc(clipped, 1)
                    dve.wait_ge(silu_ready, g * FC + f + 1)
                    dve.wait_ge(up_done, g * FC + f + 1)
                    nc.vector.tensor_tensor(gate[:, f % 2, :], up_ps[f % 2][:, 0:G], gate[:, f % 2, :],
                                            ALU.mult).then_inc(h_ready, 1)
                    if f in (3, 5):
                        rows_lo(g + 1, 1 - par, (f - 3) // 2)
                    dve.wait_ge(h_hi_ready, g * FC + f + 1)
                    nc.vector.tensor_tensor(hg_lo[:, f % 4, :], gate[:, f % 2, :], hg_hi[:, f % 4, :],
                                            ALU.subtract).then_inc(h_lo_ready, 1)

            dve.sem_inc(x_f_ready, 1)
            dve.sem_inc(h_ready, 2)
            dve.sem_inc(y_ready, 2)
            for par in range(2):
                dve.sem_inc(y_stored[par], 16)
            for c in range(DC):
                rows_lo(0, 0, c)
            groups(dve, turn)
            copy_y(NG - 1, 0)

        @block.gpsimd
        def _(pool):
            def split(g, f):
                pool.wait_ge(hi_ready, g * FC + f + 1)
                nc.gpsimd.tensor_tensor(e_lo[:, f, :], raw[:, f % RAW, :], e_hi[:, f, :], ALU.subtract).then_inc(lo_ready, 1)

            pool.sem_inc(lo_ready, RAW)
            for f in range(AHEAD):
                split(0, f)

            def turn(g, par):
                for f in range(FC):
                    ahead = f + AHEAD
                    split(g + ahead // FC, ahead % FC)

            groups(pool, turn)


def g_half(g, par):
    if isinstance(g, int):
        return g // 2
    return (g - par) // 2


def combine(nc, y_dram, n_dram, x1_dram, out, slot, weight, s_hi, s_lo, vec, ident, neg_half, eps):
    with ExitStack() as ctx:
        def sb(name, shape, dt=F32):
            return ctx.enter_context(nc.sbuf_tensor(name, shape, dt))
        def sem(name):
            return ctx.enter_context(nc.semaphore(name))
        x1 = sb("c_x1", [P, 2, TC, D])
        n_rows = sb("c_n", [P, 2, TC, D])
        ye = sb("c_ye", [P, 2, TC, K, D])
        acc = sb("c_acc", [P, 2, TC, D])
        nt_hi = sb("nt_hi", [P, DC, HALF], F32R)
        nt_lo = sb("nt_lo", [P, DC, HALF], F32R)
        nt_f = sb("nt_f", [P, DC, HALF])
        gate = sb("c_gate", [P, SC, HALF])
        hid_hi = sb("hid_hi", [P, SC, HALF], F32R)
        hid_lo = sb("hid_lo", [P, SC, HALF], F32R)
        st = sb("c_st", [P, TC, 6])
        mv = sb("c_mv", [P, 2, TC, 2])
        ve = sb("c_ve", [P, 2, TC])
        rs = sb("c_rs", [P, 2, TC])
        nt_ps, gate_ps, up_ps, down_ps = ([ctx.enter_context(nc.psum_tensor(f"{name}{i}", [P, HALF], F32)) for i in range(2)]
                                          for name in ("nt_ps", "c_gate_ps", "c_up_ps", "c_down_ps"))
        x1_loaded = [sem(f"c_x1_loaded{i}") for i in range(2)]
        n_loaded = [sem(f"c_n_loaded{i}") for i in range(2)]
        gathered = [sem(f"gathered{i}") for i in range(2)]
        stored = [sem(f"out_stored{i}") for i in range(2)]
        nt_done, nt_hi_ready, nt_f_ready, nt_lo_ready = sem("nt_done"), sem("nt_hi_ready"), sem("nt_f_ready"), sem("nt_lo_ready")
        gate_done, up_done, down_done = sem("c_gate_done"), sem("c_up_done"), sem("c_down_done")
        clipped, silu_ready, hid_ready = sem("c_clipped"), sem("c_silu"), sem("c_hid_ready")
        hid_hi_ready, hid_lo_ready = sem("c_hid_hi"), sem("c_hid_lo")
        mixed, mixed_one, order, seen = sem("c_mixed"), sem("c_mixed_one"), sem("c_order"), sem("c_seen")
        moments_ready, rs_ready, ve_ready = sem("c_moments"), sem("c_rs_ready"), sem("c_ve_ready")
        normed, out_ready = sem("c_normed"), sem("c_out_ready")
        block = ctx.enter_context(nc.Block())

        def steps(eng, turn):
            for c in range(2):
                turn(c, c, 2)
            with eng.Fori(1, NC // 2 - 1) as i:
                for par in range(2):
                    turn(i * 2 + par, par, 2)
            for par in range(2):
                turn(NC - 2 + par, par, 1 - par)
        assert NC % 2 == 0

        @block.sync
        def _(sp):
            def load_n(c, par):
                sp.dma_start(n_rows[:, par, :, :], token_rows(n_dram)[c, :, :, :]).then_inc(n_loaded[par], 16)
            def load_x1(c, par):
                sp.dma_start(x1[:, par, :, :], token_rows(x1_dram)[c, :, :, :]).then_inc(x1_loaded[par], 16)
            def store(c, par):
                sp.wait_ge(out_ready, c + 3)
                sp.dma_start(token_rows(out)[c, :, :, :], x1[:, par, :, :]).then_inc(stored[par], 16)
            for par in range(2):
                load_n(par, par)
                load_x1(par, par)
            def n_next(c, par):
                sp.wait_ge(nt_done, c * DC + DC)
                load_n(c + 2, par)
            def x1_next(c, par):
                store(c, par)
                sp.wait_ge(stored[par], g_half(c, par) * 16 + 16)
                load_x1(c + 2, par)
            n_next(0, 0)
            with sp.Fori(0, (NC - 4) // 2) as i:
                for par in range(2):
                    n_next(i * 2 + par + 1, 1 - par)
                    x1_next(i * 2 + par, par)
            n_next(NC - 3, 1)
            for par in range(2):
                x1_next(NC - 4 + par, par)
            for par in range(2):
                store(NC - 2 + par, par)
            for par in range(2):
                sp.wait_ge(stored[par], 16 * (NC // 2))

        @block.gpsimd
        def _(pool):
            def roots(c):
                pool.wait_ge(moments_ready, c + 1)
                if c >= 2:
                    pool.wait_ge(normed, c - 1)
                nc.gpsimd.tensor_tensor(ve[:, c % 2, :], mv[:, c % 2, :, 1], eps[:, 0:TC], ALU.add).then_inc(ve_ready, 1)
                pool.wait_ge(ve_ready, c + 1)
                nc.gpsimd.tensor_tensor(rs[:, c % 2, :], ve[:, c % 2, :], neg_half[:, 0:TC], ALU.pow).then_inc(rs_ready, 1)
            for c in range(NC):
                if c >= 2:
                    pool.wait_ge(mixed, c - 1)
                for t in range(TC):
                    for k in range(K):
                        nc.gpsimd.indirect_dma_start(
                            out=ye[:, c % 2, t, k, :], out_offset=None, in_=y_dram,
                            in_offset=bass.IndirectOffsetOnAxis(ap=slot[:, c * TC + t, k:k + 1], axis=0)
                        ).then_inc(gathered[c % 2], 16)
                if c >= 1:
                    roots(c - 1)
            roots(NC - 1)

        @block.tensor
        def _(pe):
            def turned(c, par):
                pe.wait_ge(n_loaded[par], g_half(c, par) * 16 + 16)
                pe.wait_ge(nt_hi_ready, c * DC + DC)
                pe.wait_ge(nt_f_ready, c * DC + DC)
                for f in range(DC):
                    for t in range(TC):
                        i = nc.tensor.transpose(nt_ps[f][:, t * P:(t + 1) * P], n_rows[:, par, t, f * P:(f + 1) * P],
                                                ident[:, :])
                    i.then_inc(nt_done, 1)
            def gate_up(c):
                pe.wait_ge(nt_lo_ready, c + 1)
                pe.wait_ge(hid_ready, c * SC + SC)
                for f in range(SC):
                    for ps, at, done in ((gate_ps, 0, gate_done), (up_ps, FS, up_done)):
                        for m in range(DC):
                            cols = slice(SGU_AT + m * 2 * FS + at + f * P, SGU_AT + m * 2 * FS + at + (f + 1) * P)
                            nc.tensor.matmul(ps[f][:, :], s_hi[:, cols], nt_hi[:, m, :], start=m == 0, stop=False)
                            nc.tensor.matmul(ps[f][:, :], s_hi[:, cols], nt_lo[:, m, :], start=False, stop=False)
                            i = nc.tensor.matmul(ps[f][:, :], s_lo[:, cols], nt_hi[:, m, :], start=False, stop=m == DC - 1)
                        i.then_inc(done, 1)
            def down(c):
                pe.wait_ge(mixed_one, c + 1)
                pe.wait_ge(hid_lo_ready, c + 1)
                for t in range(TC):
                    toks = slice(t * P, (t + 1) * P)
                    out_ps = down_ps[t // 2][:, (t % 2) * D:(t % 2 + 1) * D]
                    for f in range(SC):
                        cols = slice(SDN_AT + f * D, SDN_AT + (f + 1) * D)
                        nc.tensor.matmul(out_ps, hid_hi[:, f, toks], s_hi[:, cols], start=f == 0, stop=False)
                        nc.tensor.matmul(out_ps, hid_hi[:, f, toks], s_lo[:, cols], start=False, stop=False)
                        i = nc.tensor.matmul(out_ps, hid_lo[:, f, toks], s_hi[:, cols], start=False, stop=f == SC - 1)
                i.then_inc(down_done, 1)
            def turn(c, par, later):
                if later >= 1:
                    gate_up(c + 1)
                if later >= 2:
                    turned(c + 2, par)
                if later >= 1:
                    down(c + 1)
            turned(0, 0)
            gate_up(0)
            turned(1, 1)
            down(0)
            steps(pe, turn)

        @block.scalar
        def _(act):
            def turned(c):
                for f in range(DC):
                    act.wait_ge(nt_done, c * DC + f + 1)
                    if f == 0:
                        act.wait_ge(up_done, c * SC + SC)
                    b, g = vec[:, V_BE + f:V_BE + f + 1], vec[:, V_G + f:V_G + f + 1]
                    nc.scalar.activation(nt_hi[:, f, :], nt_ps[f][:, :], ACT.Identity, bias=b, scale=g).then_inc(nt_hi_ready, 1)
                    nc.scalar.activation(nt_f[:, f, :], nt_ps[f][:, :], ACT.Identity, bias=b, scale=g).then_inc(nt_f_ready, 1)
            def hidden(c):
                for f in range(SC):
                    act.wait_ge(clipped, c * SC + f + 1)
                    nc.scalar.activation(gate[:, f, :], gate[:, f, :], ACT.Silu).then_inc(silu_ready, 1)
                act.wait_ge(down_done, c + 1)
                act.wait_ge(hid_ready, c * SC + SC + SC)
                nc.scalar.activation(hid_hi[:, :, :], gate[:, :, :], ACT.Copy).then_inc(hid_hi_ready, 1)
            def turn(c, par, later):
                if later >= 1:
                    hidden(c + 1)
                if later >= 2:
                    turned(c + 2)
            act.sem_inc(nt_hi_ready, DC)
            act.sem_inc(nt_f_ready, DC)
            turned(0)
            hidden(0)
            turned(1)
            steps(act, turn)

        @block.vector
        def _(dve):
            def nt_low(c):
                dve.wait_ge(nt_f_ready, c * DC + 2 * DC)
                nc.vector.tensor_tensor(nt_lo[:, :, :], nt_f[:, :, :], nt_hi[:, :, :], ALU.subtract).then_inc(nt_lo_ready, 1)
            def clip(c, f):
                dve.wait_ge(gate_done, c * SC + f + 1)
                nc.vector.tensor_scalar(gate[:, f, :], gate_ps[f][:, :], CLIP, -CLIP, ALU.min, ALU.max).then_inc(clipped, 1)
            def times_up(c, f):
                dve.wait_ge(silu_ready, c * SC + f + 1)
                dve.wait_ge(up_done, c * SC + f + 1 + SC)
                nc.vector.tensor_tensor(gate[:, f, :], up_ps[f][:, :], gate[:, f, :], ALU.mult).then_inc(hid_ready, 1)
            def hid_low(c):
                dve.wait_ge(hid_hi_ready, c + 1)
                nc.vector.tensor_tensor(hid_lo[:, :, :], gate[:, :, :], hid_hi[:, :, :], ALU.subtract).then_inc(hid_lo_ready, 1)
            def mix(c, par, m):
                if m == 0:
                    dve.wait_ge(out_ready, c + 1)
                    dve.wait_ge(down_done, c + 2)
                    dve.wait_ge(gathered[par], g_half(c, par) * 16 * TC * K + 16 * TC * K)
                for t in range(TC):
                    before = down_ps[t // 2][:, (t % 2) * D:(t % 2 + 1) * D] if m == 0 else acc[:, par, t, :]
                    j = nc.vector.scalar_tensor_tensor(out=acc[:, par, t, :], in0=ye[:, par, t, m, :],
                                                       scalar=weight[:, bass.ds(c * TC + t, 1), m:m + 1].rearrange("p t k -> p (t k)"),
                                                       in1=before, op0=ALU.mult, op1=ALU.add)
                j.then_inc(mixed_one if m == 0 else mixed, 1)
            def stats(c, par):
                dve.wait_ge(mixed, c + 1)
                for t in range(TC):
                    j = nc.vector.bn_stats(st[:, t, :], acc[:, par, t, :])
                j.then_inc(order, 1)
                dve.wait_ge(order, c + 1)
                dve.sem_inc(seen, 1)
                for t in range(TC):
                    j = nc.vector.bn_aggr(mv[:, par, t, :], st[:, t, :])
                j.then_inc(moments_ready, 1)
            def norm(c, par):
                dve.wait_ge(rs_ready, c + 1)
                for t in range(TC):
                    j = nc.vector.tensor_scalar(acc[:, par, t, :], acc[:, par, t, :], mv[:, par, t, 0:1], rs[:, par, t:t + 1],
                                                ALU.subtract, ALU.mult)
                j.then_inc(normed, 1)
            def finish(c, par):
                dve.wait_ge(normed, c + 1)
                dve.wait_ge(x1_loaded[par], g_half(c, par) * 16 + 16)
                nc.vector.tensor_tensor(x1[:, par, :, :], x1[:, par, :, :], acc[:, par, :, :], ALU.add).then_inc(out_ready, 1)
            def turn(c, par, later):
                first = isinstance(c, int) and c == 0
                mix(c, par, 0)
                if later >= 1:
                    clip(c + 1, 0)
                    clip(c + 1, 1)
                dve.wait_ge(mixed_one, c + 2)
                mix(c, par, 1)
                if later >= 1:
                    times_up(c + 1, 0)
                    times_up(c + 1, 1)
                stats(c, par)
                if later >= 1:
                    hid_low(c + 1)
                if later >= 2:
                    nt_low(c + 2)
                if not first:
                    norm(c - 1, 1 - par)
                    finish(c - 1, 1 - par)
            dve.sem_inc(mixed_one, 1)
            dve.sem_inc(out_ready, 2)
            dve.sem_inc(hid_ready, SC)
            dve.sem_inc(up_done, SC)
            dve.sem_inc(down_done, 1)
            nt_low(0)
            clip(0, 0)
            clip(0, 1)
            times_up(0, 0)
            times_up(0, 1)
            hid_low(0)
            nt_low(1)
            steps(dve, turn)
            norm(NC - 1, 1)
            finish(NC - 1, 1)


def program(nc, d, out):
    scratch = lambda name, shape: nc.dram_tensor(name, shape, F32, kind="Internal").ap()
    x1_dram = scratch("x1_scratch", (B, L, D))
    n_dram = scratch("n_scratch", (B, L, D))
    xs_dram = scratch("xs_scratch", (E * CAP, D))
    y_dram = scratch("y_scratch", (NG * G, D))
    with ExitStack() as ctx:
        def sb(name, shape, dt=F32):
            return ctx.enter_context(nc.sbuf_tensor(name, shape, dt))

        vec = sb("vec", [P, V_COLS])
        slot = sb("slot", [P, TT, K], I32)
        weight = sb("weight", [P, TT, K])
        group_expert = sb("group_expert", [P, NG + 1], I32)
        group_row = sb("group_row", [P, NG + 1], I32)
        s_hi, s_lo = sb("s_hi", [P, S_COLS], F32R), sb("s_lo", [P, S_COLS], F32R)
        ident = sb("ident", [P, P])
        neg_half = sb("neg_half", [P, LT])
        eps = sb("eps", [P, LT])
        with ExitStack() as first:
            def sb1(name, shape, dt=F32):
                return first.enter_context(nc.sbuf_tensor(name, shape, dt))

            w_hi, w_lo = sb1("w_hi", [P, W_COLS], F32R), sb1("w_lo", [P, W_COLS], F32R)
            ident_r = sb1("ident_r", [P, P], F32R)
            zeros, ones = sb1("zeros", [P, GT * D]), sb1("ones", [P, HALF])
            pick = [sb1(f"pick{k}", [P, TT, E]) for k in range(K)]
            val = [sb1(f"val{k}", [P, TT]) for k in range(K)]
            slot_f, fill = sb1("slot_f", [P, TT, K]), sb1("fill", [P, E])
            split_weights(nc, [(W1_AT, d["w1_t"], DC), (DL_AT, d["dl_w_t"], DC), (A_AT, d["A_w_t"], DC),
                               (B_AT, d["B_w_t"], DC), (C_AT, d["C_w_t"], HC), (DD_AT, d["D_w_t"], DC),
                               (W2_AT, d["w2_t"], DC), (W3_AT, d["w3_t"], DC), (RT_AT, d["router"], DC)],
                          d["vecs"], w_hi, w_lo, vec, ident, ident_r, zeros, ones, neg_half, eps)
            mixer(nc, d["x"], xs_dram, x1_dram, n_dram, pick, val, slot_f, fill, w_hi, w_lo, vec, ident, ident_r,
                  zeros, ones, neg_half, eps)
            plan(nc, [(SGU_AT, d["sgu"], DC), (SDN_AT, d["sdn"], SC)], s_hi, s_lo, xs_dram, pick, val, slot_f, fill,
                 slot, weight, group_expert, group_row, zeros)
        experts(nc, d["w_e"], xs_dram, y_dram, group_expert, group_row, vec, ident)
        combine(nc, y_dram, n_dram, x1_dram, out, slot, weight, s_hi, s_lo, vec, ident, neg_half, eps)

def kernel(**inputs):
    import numpy as np
    import concourse.bacc as bacc
    from concourse.bass_utils import run_bass_kernel_spmd as run

    a = {k.replace("L0_attn_", "").replace("L0_ffn_", "f_"): np.asarray(v) for k, v in inputs.items()}
    cols = lambda v: v.reshape(-1, P).T
    vecs = np.concatenate([a["conv_w"].reshape(DC, P, 3).transpose(1, 0, 2).reshape(P, DC * 3)] +
                          [cols(a[k]) for k in ("conv_b", "A_b", "B_b", "dl_b", "C_b", "D_b", "f_ln_gamma", "f_ln_beta")], axis=1)
    arrays = {"x": a["x"], "vecs": vecs, "sgu": a["f_shared_gate_up_w"], "sdn": a["f_shared_down_w"],
              "router": a["f_router_w"]}
    gu = a["f_gate_up_w"].reshape(E, DC, P, 2, FC, P).transpose(0, 4, 2, 3, 1, 5).reshape(E, FC, P, 4 * P)
    arrays["w_e"] = np.concatenate([gu, a["f_down_w"].reshape(E, FC, P, D)], axis=3)
    for k in ("w1", "w2", "w3", "A_w", "B_w", "C_w", "D_w", "dl_w"):
        arrays[k + "_t"] = a[k].T
    arrays = {k: np.ascontiguousarray(v) for k, v in arrays.items()}
    nc = bacc.Bacc("TRN2", target_bir_lowering=False, num_devices=1)
    d = {k: nc.dram_tensor(k, v.shape, mybir.dt.from_np(v.dtype), kind="ExternalInput").ap() for k, v in arrays.items()}
    out = nc.dram_tensor("out", (B, L, D), F32, kind="ExternalOutput").ap()
    program(nc, d, out)
    return run(nc, [arrays], core_ids=[0]).results[0]["out"]
```

```python
import concourse.bass as bass
from concourse import mybir
from contextlib import ExitStack

F32 = mybir.dt.float32
F32R = mybir.dt.float32r
I32 = mybir.dt.int32
ALU = mybir.AluOpType
ACT = mybir.ActivationFunctionType
AX = mybir.AxisListType

P = 128
B, L, D, H = 4, 1024, 256, 512
E, F, FS, K = 8, 1024, 256, 2
T = B * L
DC, HC, FC, SC = D // P, H // P, F // P, FS // P
HALF = 512
HT = HALF // P
LT = L // P
TT = T // P
EPS = 1e-5
CLIP = 10.0
EXP_CAP = 1e9

W1_AT, DL_AT, A_AT, B_AT = 0, DC * D, DC * (D + H), DC * (D + 2 * H)
C_AT = DC * (D + 3 * H)
DD_AT = C_AT + HC * D
W2_AT, W3_AT = DD_AT + DC * D, DD_AT + 2 * DC * D
RT_AT = W3_AT + DC * D
W_COLS = RT_AT + DC * E
SGU_AT, SDN_AT = 0, DC * 2 * FS
S_COLS = SDN_AT + SC * D
V_CW, V_CB = 0, 3 * DC
V_AB = V_CB + DC
V_BB, V_DLB = V_AB + HC, V_AB + 2 * HC
V_CDB = V_DLB + HC
V_G, V_BE = V_CDB + 2 * DC, V_CDB + 3 * DC
V_COLS = V_BE + DC


def split_weights(nc, weights, consts, w_hi, w_lo, vec, ident, ident_r, zeros, ones, neg_half, eps, tables):
    with ExitStack() as ctx:
        raw = ctx.enter_context(nc.sbuf_tensor("raw_w", [P, W_COLS], F32))
        loaded = [ctx.enter_context(nc.semaphore(f"prep_loaded{i}")) for i in range(len(weights))]
        vec_loaded = ctx.enter_context(nc.semaphore("vec_loaded"))
        hi_ready = ctx.enter_context(nc.semaphore("prep_hi"))
        lo_ready = ctx.enter_context(nc.semaphore("prep_lo"))
        made = ctx.enter_context(nc.semaphore("consts_made"))
        block = ctx.enter_context(nc.Block())
        parts = []
        for at, src, chunks in weights:
            parts.append((raw, w_hi, w_lo, at, src, chunks))

        @block.sync
        def _(sp):
            for n, (r, hi, lo, at, src, chunks) in enumerate(parts):
                width = src.shape[1]
                sp.dma_start(r[:, at:at + chunks * width].rearrange("p (c n) -> p c n", c=chunks),
                             src.rearrange("(c p) n -> p c n", p=P)).then_inc(loaded[n], 16)
            sp.dma_start(vec[:, :], consts).then_inc(vec_loaded, 16)
            sp.wait_ge(vec_loaded, 16)

        @block.scalar
        def _(act):
            for n, (r, hi, lo, at, src, chunks) in enumerate(parts):
                cols = chunks * src.shape[1]
                act.wait_ge(loaded[n], 16)
                nc.scalar.activation(hi[:, at:at + cols], r[:, at:at + cols], ACT.Copy).then_inc(hi_ready, 1)
            act.wait_ge(made, 3)
            nc.scalar.activation(ident_r[:, :], ident[:, :], ACT.Copy)

        @block.vector
        def _(dve):
            nc.vector.memset(zeros[:, :], 0.0)
            nc.vector.memset(ones[:, :], 1.0)
            nc.vector.memset(neg_half[:, :], -0.5)
            nc.vector.memset(eps[:, :], EPS)
            for n, (r, hi, lo, at, src, chunks) in enumerate(parts):
                cols = chunks * src.shape[1]
                dve.wait_ge(hi_ready, n + 1)
                nc.vector.tensor_tensor(lo[:, at:at + cols], r[:, at:at + cols], hi[:, at:at + cols],
                                        ALU.subtract).then_inc(lo_ready, 1)
            dve.wait_ge(lo_ready, len(parts))

        @block.gpsimd
        def _(pool):
            nc.gpsimd.memset(ident[:, :], 0.0).then_inc(made, 1)
            pool.wait_ge(made, 1)
            nc.gpsimd.affine_select(out=ident[:, :], in_=ident[:, :], compare_op=ALU.not_equal, fill=1.0,
                                    base=0, pattern=[[-1, P]], channel_multiplier=1).then_inc(made, 2)
            start_row, limits, group_no, number = tables
            for e in range(E):
                nc.gpsimd.memset(start_row[:, e:e + 1], float(e * CAP))
            for j in range(MAXG):
                nc.gpsimd.memset(limits[:, :, j:j + 1], float(j * G - 1))
            for g in range(NG + 1):
                nc.gpsimd.memset(group_no[:, g:g + 1, :], float(g))
                nc.gpsimd.memset(number[:, g:g + 1], float(g))


def mixer(nc, x, xs_dram, x1_dram, n_dram, pick, val, slot_f, fill, w_hi, w_lo, vec, ident, ident_r, zeros, ones, neg_half, eps):
    with ExitStack() as ctx:
        def sb(name, shape, dt=F32):
            return ctx.enter_context(nc.sbuf_tensor(name, shape, dt))

        def sem(name):
            return ctx.enter_context(nc.semaphore(name))

        x_in = sb("x_in", [P, LT, D])
        xt_hi = sb("xt_hi", [P, DC, L], F32R)
        xt_lo = sb("xt_lo", [P, DC, L], F32R)
        u = sb("u", [P, DC, L + 2])
        cv = sb("cv", [P, DC, L])
        xs_hi = sb("xs_hi", [P, DC, L], F32R)
        xs_lo = sb("xs_lo", [P, DC, L], F32R)
        delta = sb("delta", [P, 2, HALF])
        decay = sb("decay", [P, 2, HALF])
        a_cum = sb("a_cum", [P, HALF])
        bx = sb("bx", [P, HALF])
        h = sb("h", [P, 2, HALF])
        carry_a = sb("carry_a", [P, HC])
        carry_h = sb("carry_h", [P, HC])
        h_hi = sb("h_hi", [P, HC, HALF], F32R)
        h_lo = sb("h_lo", [P, HC, HALF], F32R)
        s = sb("s", [P, DC, HALF])
        s_out_hi = sb("s_out_hi", [P, DC, HALF], F32R)
        s_out_lo = sb("s_out_lo", [P, DC, HALF], F32R)
        g = sb("g", [P, DC, HALF])
        z_hi = sb("z_hi", [P, DC, HALF], F32R)
        z_lo = sb("z_lo", [P, DC, HALF], F32R)
        xr = sb("xr", [P, HT, D])
        xnt_hi = sb("xnt_hi", [P, DC, HALF], F32R)
        xnt_lo = sb("xnt_lo", [P, DC, HALF], F32R)
        xn_f = sb("xn_f", [P, DC, HALF])
        y_n = sb("y_n", [P, HT, D])
        n2 = sb("n2", [P, HT, D])
        cdb = sb("cdb", [P, DC])
        st = sb("st", [P, LT, 6])
        mv = sb("mv", [P, LT, 2])
        ve = sb("ve", [P, LT])
        rs = sb("rs", [P, LT])
        st2 = sb("st2", [P, 2 * HT, 6])
        mv2 = sb("mv2", [P, 2 * HT, 2])
        ve2 = sb("ve2", [P, HT])
        rs2 = sb("rs2", [P, HT])
        ve3 = sb("ve3", [P, HT])
        rs3 = sb("rs3", [P, HT])
        ve4 = sb("ve4", [P, HT])
        rs4 = sb("rs4", [P, HT])
        lt = sb("lt", [P, HALF])
        top = sb("top", [P, HT])
        prob = sb("prob", [P, HT, E])
        total = sb("total", [P, HT])
        desc = sb("desc", [P, HT, E])
        score = sb("score", [P, HT, E])
        best = sb("best", [P, HT])
        both = sb("both", [P, E, HT])
        run_sum = sb("run_sum", [P, E, HT])
        count = sb("count", [P, E])
        offset = sb("offset", [P, E])
        before = sb("before", [P, P])
        slot_half = sb("slot_half", [P, HT, K])
        slot_now = sb("slot_now", [P, HT, K], I32)
        banks = [ctx.enter_context(nc.psum_tensor(f"bank{i}", [P, HALF], F32)) for i in range(8)]

        x_loaded = sem("x_loaded")
        xr_loaded = sem("xr_loaded")
        x1_stored, n_stored, scattered = sem("x1_stored"), sem("n_stored"), sem("scattered")
        stats_seen, sp_seen = sem("stats_seen"), sem("sp_seen")
        a_order, d_order, start_made = sem("a_order"), sem("d_order"), sem("start_made")
        pool_a, pool_d = sem("pool_a"), sem("pool_d")
        mv_ready, rs_ready, xn_ready = sem("mv_ready"), sem("rs_ready"), sem("xn_ready")
        t1_done, xt_hi_ready, xt_lo_ready = sem("t1_done"), sem("xt_hi_ready"), sem("xt_lo_ready")
        u_done, u_copied, cv0_ready, cv_ready = sem("u_done"), sem("u_copied"), sem("cv0_ready"), sem("cv_ready")
        silu_ready, xs_hi_ready, xs_lo_ready = sem("silu_ready"), sem("xs_hi_ready"), sem("xs_lo_ready")
        dl_done, a_done, b_done = sem("dl_done"), sem("a_done"), sem("b_done")
        exp_ready, capped, ln_ready = sem("exp_ready"), sem("capped"), sem("ln_ready")
        delta_ready, da_ready, abar_ready = sem("delta_ready"), sem("da_ready"), sem("abar_ready")
        acum_ready, bx_ready, h_ready = sem("acum_ready"), sem("bx_ready"), sem("h_ready")
        carried, h_hi_ready, h_lo_ready = sem("carried"), sem("h_hi_ready"), sem("h_lo_ready")
        s_done, s_ready, s_hi_ready, s_lo_ready = sem("s_done"), sem("s_ready"), sem("s_hi_ready"), sem("s_lo_ready")
        g_done, g_ready, z_ready = sem("g_done"), sem("g_ready"), sem("z_ready")
        z_hi_ready, z_lo_ready, w3_done = sem("z_hi_ready"), sem("z_lo_ready"), sem("w3_done")
        mv2_ready, rs2_ready, yn_ready = sem("mv2_ready"), sem("rs2_ready"), sem("yn_ready")
        x1_ready, mv3_ready, rs4_ready, n2_ready = sem("x1_ready"), sem("mv3_ready"), sem("rs4_ready"), sem("n2_ready")
        t2_done, xn_hi_ready, xn_f_ready, xn_lo_ready = sem("t2_done"), sem("xn_hi_ready"), sem("xn_f_ready"), sem("xn_lo_ready")
        lt_done, lt_ready, logits_done = sem("lt_done"), sem("lt_ready"), sem("logits_done")
        shifted, probs_exp, counted = sem("shifted"), sem("probs_exp"), sem("counted")
        counts_done, route_steps, slots_ready = sem("counts_done"), sem("route_steps"), sem("slots_ready")
        pool_seen, before_set, before_made = sem("pool_seen"), sem("before_set"), sem("before_made")
        block = ctx.enter_context(nc.Block())

        LINKS = 20 + 2 * K
        UNITS = [(half, j) for half in range(2) for j in range(HC)]
        NU = len(UNITS)
        HH = ((h_hi, h_lo), (xt_hi[:, :, :].rearrange("p c (a l) -> p (c a) l", l=HALF),
                             xt_lo[:, :, :].rearrange("p c (a l) -> p (c a) l", l=HALF)))
        U_BANKS = (0, 1, 2, 3)

        ORDER = {
            "tensor":
                "a2 d0.4' d1.11'' d1.0' d1.1' d1.2' d0.7' a3 d0.8' d0.9' d0.10' d1.4' dl0 dl1 d0.11' dl2 dl3 "
                "b0 b1 dl4 b2 dl5 d1.7' b3 dl6 b4 d1.8' d0.0 b5 d0.1 dl7 b6 d0.2 b7 d1.9' d1.10'",
            "scalar":
                "a2 d1.2' d0.7' d1.3' a3 d0.8' a4 d0.9' a5 d0.10' exp0 ln0 exp1 ln1 exp2 exp3 abar0 ln2 abar1 "
                "hi0 ln3 exp4 abar2 hi1 abar3 ln4 exp5 hi2 d1.7' exp6 hi3 ln5 ln6 abar4 abar5 d1.8' d0.1 exp7 "
                "hi4 abar6 hi5 ln7 d0.2 abar7 d1.9' d0.3 hi6 hi7 d1.10' d1.1",
            "vector":
                "a0 d0.2' cap7' scan6' da7' a1 d0.3' scan7' d0.4' d1.10'' d1.11'' d0.5' d1.12'' d0.6' d1.2' "
                "d0.7' a2 d1.3' d0.8' d0.9' a4 d1.4' d0.10' a6 d0.11' cap0 d1.5' da0 cap1 d0.12' da1 cap2 "
                "d1.6' cap3 scan0 da2 scan1 cap4 da3 d1.7' scan2 da4 scan3 cap5 cap6 d1.8' da5 scan4 da6 "
                "scan5 d1.9'",
            "gpsimd":
                "a0 lo5' lo6' lo7' d0.5' d1.12'' d1.13'' d1.14'' d1.15'' d0.6' d1.5' d0.12' d0.13' d0.14' "
                "d0.15' lo0 d1.6' lo1 lo2 lo3 lo4",
        }

        def run(eng, name, a_stage, c_stage, d_stage):
            order = []
            for word in ORDER[name].split():
                stage = word.rstrip("'")
                kind = stage.rstrip("0123456789.")
                order.append((kind, stage[len(kind):], len(word) - len(stage)))
            lags = max(lag for _, _, lag in order)
            def turn(b, least, most):
                for kind, number, lag in order:
                    if not least <= lag <= most:
                        continue
                    if kind == "a":
                        a_stage(b - lag, int(number))
                    elif kind == "d":
                        half, d = (int(i) for i in number.split("."))
                        d_stage((b - lag) * 2 + half, half, d)
                    else:
                        c_stage(b - lag, kind, int(number))
            for b in range(lags):
                turn(b, 0, b)
            with eng.Fori(lags, B) as b:
                turn(b, 0, lags)
            for b in range(B, B + lags):
                turn(b, b - B + 1, lags)

        def W(hi_lo, at, c, width, lo=0, n=P):
            return hi_lo[:, at + c * width + lo:at + c * width + lo + n]

        @block.sync
        def _(sp):
            def load_x(b):
                sp.dma_start(x_in[:, :, :], x[b, :, :].rearrange("(t p) d -> p t d", p=P)).then_inc(x_loaded, 16)

            def passed(semaphore, value):
                sp.wait_ge(semaphore, value)
                sp.sem_inc(sp_seen, 1)

            def half_dmas(b, half):
                k = b * 2 + half
                rows = slice(half * HALF, (half + 1) * HALF)
                passed(x1_stored, k * 16 + 16)
                passed(n2_ready, k + 1)
                sp.dma_start(xr[:, :, :], x[b, rows, :].rearrange("(t p) d -> p t d", p=P)).then_inc(xr_loaded, 16)
                passed(x1_ready, k + 1)
                sp.dma_start(x1_dram[b, rows, :].rearrange("(t p) d -> p t d", p=P), xr[:, :, :]).then_inc(x1_stored, 16)
                passed(n2_ready, k + 2)
                sp.dma_start(n_dram[b, rows, :].rearrange("(t p) d -> p t d", p=P), n2[:, :, :]).then_inc(n_stored, 16)

            load_x(0)
            with sp.Fori(1, B) as b:
                passed(t1_done, b * 4)
                load_x(b)
                for half in range(2):
                    half_dmas(b - 1, half)
            for half in range(2):
                half_dmas(B - 1, half)
            sp.wait_ge(x1_stored, 16 + 32 * B)
            sp.wait_ge(n_stored, 16 + 32 * B)

        @block.tensor
        def _(pe):
            def product(out, hi, lo, x_hi, x_lo, first, last):
                nc.tensor.matmul(out, hi, x_hi, start=first, stop=False)
                nc.tensor.matmul(out, hi, x_lo, start=False, stop=False)
                return nc.tensor.matmul(out, lo, x_hi, start=False, stop=last)

            def product_t(out, x_hi, x_lo, hi, lo, first, last):
                nc.tensor.matmul(out, x_hi, hi, start=first, stop=False)
                nc.tensor.matmul(out, x_hi, lo, start=False, stop=False)
                return nc.tensor.matmul(out, x_lo, hi, start=False, stop=last)

            def a_stage(b, a):
                if a == 2:
                    pe.wait_ge(xn_ready, b + 1)
                    pe.wait_ge(bx_ready, b * NU + 2)
                    for n in range(4):
                        half, c = n // 2, n % 2
                        for t in range(HT):
                            i = nc.tensor.transpose(banks[n][:, t * P:(t + 1) * P],
                                                    x_in[:, half * HT + t, c * P:(c + 1) * P], ident[:, :])
                        i.then_inc(t1_done, 1)
                if a == 3:
                    for n in range(4):
                        half, o = n // 2, n % 2
                        cols = slice(half * HALF, (half + 1) * HALF)
                        pe.wait_ge(xt_lo_ready, b * 4 + 2 * half + 2)
                        for c in range(DC):
                            i = product(banks[U_BANKS[n]][:, :], W(w_hi, W1_AT, c, D, o * P), W(w_lo, W1_AT, c, D, o * P),
                                        xt_hi[:, c, cols], xt_lo[:, c, cols], c == 0, c == DC - 1)
                        i.then_inc(u_done, 1)

            def dl_a(b, n):
                if n == 0:
                    pe.wait_ge(u_copied, b * 4 + 4)
                    pe.wait_ge(xs_lo_ready, b + 1)
                half, j = UNITS[n]
                cols = slice(half * HALF, (half + 1) * HALF)
                for at, bank, done, free in ((DL_AT, n % 2, dl_done, delta_ready), (A_AT, 2 + n % 2, a_done, da_ready)):
                    pe.wait_ge(free, b * NU + n + 1)
                    for c in range(DC):
                        i = product(banks[bank][:, :], W(w_hi, at, c, H, j * P), W(w_lo, at, c, H, j * P),
                                    xs_hi[:, c, cols], xs_lo[:, c, cols], c == 0, c == DC - 1)
                    i.then_inc(done, 1)

            def b_unit(b, n):
                half, j = UNITS[n]
                cols = slice(half * HALF, (half + 1) * HALF)
                pe.wait_ge(bx_ready, b * NU + n + 2)
                for c in range(DC):
                    i = product(banks[4][:, :], W(w_hi, B_AT, c, H, j * P), W(w_lo, B_AT, c, H, j * P),
                                xs_hi[:, c, cols], xs_lo[:, c, cols], c == 0, c == DC - 1)
                i.then_inc(b_done, 1)

            def c_stage(b, kind, n):
                if kind == "dl":
                    dl_a(b, n)
                if kind == "b":
                    b_unit(b, n)

            def d_stage(k, half, d):
                if d in (0, 1):
                    cols = slice(half * HALF, (half + 1) * HALF)
                    o = d
                    if o == 0:
                        pe.wait_ge(yn_ready, k + 1)
                    out = banks[6 + o][:, :]
                    for c in range(DC):
                        product(out, W(w_hi, DD_AT, c, D, o * P), W(w_lo, DD_AT, c, D, o * P),
                                xs_hi[:, c, cols], xs_lo[:, c, cols], c == 0, False)
                    if o == 0:
                        pe.wait_ge(h_lo_ready, k * HC + HC + 2)
                    for c in range(HC):
                        i = product(out, W(w_hi, C_AT, c, D, o * P), W(w_lo, C_AT, c, D, o * P),
                                    HH[half][0][:, c, :], HH[half][1][:, c, :], False, c == HC - 1)
                    i.then_inc(s_done, 1)
                if d == 2:
                    pe.wait_ge(s_lo_ready, k + 1)
                    pe.wait_ge(s_hi_ready, 2 * k + 2)
                    for o in range(DC):
                        for c in range(DC):
                            i = product(banks[6 + o][:, :], W(w_hi, W2_AT, c, D, o * P), W(w_lo, W2_AT, c, D, o * P),
                                        s_out_hi[:, c, :], s_out_lo[:, c, :], c == 0, c == DC - 1)
                        i.then_inc(g_done, 1)
                if d == 4:
                    pe.wait_ge(g_ready, 2 * k + 2)
                    pe.wait_ge(z_lo_ready, k + 1)
                    for t in range(HT):
                        at = (t % 2) * D
                        out = banks[6 + t // 2][:, at:at + D]
                        toks = slice(t * P, (t + 1) * P)
                        for c in range(DC):
                            w3 = slice(W3_AT + c * D, W3_AT + (c + 1) * D)
                            product_t(out, z_hi[:, c, toks], z_lo[:, c, toks], w_hi[:, w3], w_lo[:, w3], c == 0, False)
                        for c in range(DC):
                            part = banks[6 + t // 2][:, at + c * P:at + (c + 1) * P]
                            nc.tensor.matmul(part, s_out_hi[:, c, toks], ident_r[:, :], start=False, stop=False)
                            i = nc.tensor.matmul(part, s_out_lo[:, c, toks], ident_r[:, :], start=False, stop=c == DC - 1)
                        i.then_inc(w3_done, 1)
                if d in (7, 8):
                    c = d - 7
                    if c == 0:
                        pe.wait_ge(n2_ready, k + 2)
                        pe.wait_ge(slots_ready, k + 1)
                    else:
                        pe.wait_ge(xn_hi_ready, 2 * k + 1)
                        pe.wait_ge(xn_f_ready, 2 * k + 1)
                    for t in range(HT):
                        i = nc.tensor.transpose(banks[5][:, t * P:(t + 1) * P], n2[:, t, c * P:(c + 1) * P], ident[:, :])
                    i.then_inc(t2_done, 1)
                if d == 9:
                    pe.wait_ge(xn_lo_ready, 2 * k + 2)
                    for c in range(DC):
                        rt = slice(RT_AT + c * E, RT_AT + (c + 1) * E)
                        i = product(banks[5][0:E, :], w_hi[:, rt], w_lo[:, rt], xnt_hi[:, c, :], xnt_lo[:, c, :],
                                    c == 0, c == DC - 1)
                    i.then_inc(lt_done, 1)
                if d == 10:
                    pe.wait_ge(lt_ready, k + 1)
                    for t in range(HT):
                        i = nc.tensor.transpose(banks[5][:, t * P:(t + 1) * P], lt[:, t * P:(t + 1) * P], ident[:, :])
                    i.then_inc(logits_done, 1)
                if d == 11:
                    pe.wait_ge(counted, k + 1)
                    if isinstance(k, int) and k == 0:
                        pe.wait_ge(before_made, 1)
                    nc.tensor.matmul(banks[5][:, 0:E], before[:, :], count[:, :], start=True, stop=True)
                    nc.tensor.matmul(banks[5][:, E:2 * E], ones[:, 0:P], count[:, :], start=True, stop=True).then_inc(counts_done, 1)

            run(pe, "tensor", a_stage, c_stage, d_stage)

        @block.scalar
        def _(act):
            table = [None]
            def take_table(wanted):
                if wanted == "exp_ln" and table[0] != wanted:
                    act.preload_act_table_set("natural_log_exp_and_others")
                table[0] = wanted
            def a_stage(b, a):
                if a == 2:
                    act.wait_ge(s_done, b * 4 + 2)
                    for n in range(4):
                        half, c = n // 2, n % 2
                        act.wait_ge(t1_done, b * 4 + n + 1)
                        nc.scalar.activation(xt_hi[:, c, half * HALF:(half + 1) * HALF], banks[n][:, :],
                                             ACT.Copy).then_inc(xt_hi_ready, 1)
                if a == 3:
                    act.wait_ge(cv_ready, b * 2 + 2)
                    for n in range(4):
                        half, o = n // 2, n % 2
                        act.wait_ge(u_done, b * 4 + n + 1)
                        nc.scalar.activation(u[:, o, 1 + half * HALF:1 + (half + 1) * HALF],
                                             banks[U_BANKS[n]][:, :], ACT.Copy).then_inc(u_copied, 1)
                if a == 4:
                    for o in range(DC):
                        act.wait_ge(u_copied, b * 4 + 3 + o)
                        nc.scalar.activation(cv[:, o, :], u[:, o, 1:L + 1], ACT.Identity,
                                             bias=vec[:, V_CB + o:V_CB + o + 1],
                                             scale=vec[:, V_CW + 3 * o + 1:V_CW + 3 * o + 2]).then_inc(cv0_ready, 1)
                if a == 5:
                    take_table("silu")
                    for o in range(DC):
                        act.wait_ge(cv_ready, b * 2 + o + 3)
                        nc.scalar.activation(cv[:, o, :], cv[:, o, :], ACT.Silu).then_inc(silu_ready, 1)
                    for o in range(DC):
                        act.wait_ge(silu_ready, b * 2 + o + 1)
                        nc.scalar.activation(xs_hi[:, o, :], cv[:, o, :], ACT.Copy).then_inc(xs_hi_ready, 1)

            def c_stage(b, kind, n):
                if kind != "hi":
                    take_table("exp_ln")
                if kind == "exp":
                    half, j = UNITS[n]
                    act.wait_ge(dl_done, b * NU + n + 1)
                    act.wait_ge(da_ready, b * NU + n + 1)
                    nc.scalar.activation(delta[:, n % 2, :], banks[n % 2][:, :], ACT.Exp,
                                         bias=vec[:, V_DLB + j:V_DLB + j + 1]).then_inc(exp_ready, 1)
                if kind == "ln":
                    act.wait_ge(capped, b * NU + n + 1)
                    nc.scalar.activation(delta[:, n % 2, :], delta[:, n % 2, :], ACT.Ln, bias=1.0).then_inc(ln_ready, 1)
                if kind == "abar":
                    act.wait_ge(da_ready, b * NU + n + 3)
                    nc.scalar.activation(decay[:, n % 2, :], decay[:, n % 2, :], ACT.Exp,
                                         scale=-1.0).then_inc(abar_ready, 1)
                if kind == "hi":
                    half, j = UNITS[n]
                    act.wait_ge(h_ready, b * NU + n + 1)
                    nc.scalar.activation(HH[half][0][:, j, :], h[:, n % 2, :], ACT.Copy).then_inc(h_hi_ready, 1)

            def d_stage(k, half, d):
                if d == 1:
                    act.wait_ge(w3_done, k * 4 + 4)
                    for o in range(DC):
                        act.wait_ge(s_done, 2 * k + o + 3)
                        bank = banks[6 + o]
                        nc.scalar.activation(s[:, o, :], bank[:, :], ACT.Identity, bias=cdb[:, o:o + 1]).then_inc(s_ready, 1)
                        nc.scalar.activation(s_out_hi[:, o, :], bank[:, :], ACT.Identity,
                                             bias=cdb[:, o:o + 1]).then_inc(s_hi_ready, 1)
                if d == 2:
                    take_table("silu")
                    for o in range(DC):
                        act.wait_ge(g_done, 2 * k + o + 1)
                        nc.scalar.activation(g[:, o, :], banks[6 + o][:, :], ACT.Silu).then_inc(g_ready, 1)
                if d == 3:
                    act.wait_ge(z_ready, k + 1)
                    nc.scalar.activation(z_hi[:, :, :], g[:, :, :], ACT.Copy).then_inc(z_hi_ready, 1)
                if d in (7, 8):
                    c = d - 7
                    act.wait_ge(t2_done, 2 * k + c + 1)
                    nc.scalar.activation(xnt_hi[:, c, :], banks[5][:, :], ACT.Identity,
                                         bias=vec[:, V_BE + c:V_BE + c + 1],
                                         scale=vec[:, V_G + c:V_G + c + 1]).then_inc(xn_hi_ready, 1)
                if d == 9:
                    act.wait_ge(lt_done, k + 1)
                    nc.scalar.activation(lt[0:E, :], banks[5][0:E, :], ACT.Copy).then_inc(lt_ready, 1)
                if d == 10:
                    take_table("exp_ln")
                    act.wait_ge(shifted, k + 1)
                    nc.scalar.activation(prob[:, :, :], prob[:, :, :], ACT.Exp).then_inc(probs_exp, 1)

            run(act, "scalar", a_stage, c_stage, d_stage)

        @block.vector
        def _(dve):
            def moments(source, stats, out, n, order, count, ready):
                for t in range(n):
                    i = nc.vector.bn_stats(stats[:, t, :], source(t))
                i.then_inc(order, 1)
                dve.wait_ge(order, count)
                dve.sem_inc(stats_seen, 1)
                for t in range(n):
                    i = nc.vector.bn_aggr(out[:, t, :], stats[:, t, :])
                i.then_inc(ready, 1)

            def a_stage(b, a):
                if a == 0:
                    dve.wait_ge(x_loaded, b * 16 + 16)
                    moments(lambda t: x_in[:, t, :], st, mv, LT, a_order, b * 3 + 1, mv_ready)
                if a == 1:
                    dve.wait_ge(mv_ready, b + 1)
                    dve.wait_ge(rs_ready, b + 1)
                    for t in range(LT):
                        i = nc.vector.tensor_scalar(x_in[:, t, :], x_in[:, t, :], mv[:, t, 0:1], rs[:, t:t + 1],
                                                    ALU.subtract, ALU.mult)
                    i.then_inc(xn_ready, 1)
                if a == 2:
                    for n in range(4):
                        half, c = n // 2, n % 2
                        dve.wait_ge(xt_hi_ready, b * 4 + n + 1)
                        cols = slice(half * HALF, (half + 1) * HALF)
                        nc.vector.tensor_tensor(xt_lo[:, c, cols], banks[n][:, :], xt_hi[:, c, cols],
                                                ALU.subtract).then_inc(xt_lo_ready, 1)
                if a == 4:
                    for o in range(DC):
                        dve.wait_ge(cv0_ready, b * 2 + o + 1)
                        nc.vector.scalar_tensor_tensor(out=cv[:, o, :], in0=u[:, o, 0:L],
                                                       scalar=vec[:, V_CW + 3 * o:V_CW + 3 * o + 1],
                                                       in1=cv[:, o, :], op0=ALU.mult, op1=ALU.add).then_inc(a_order, 1)
                        dve.wait_ge(a_order, b * 3 + 2 + o)
                        nc.vector.scalar_tensor_tensor(out=cv[:, o, :], in0=u[:, o, 2:L + 2],
                                                       scalar=vec[:, V_CW + 3 * o + 2:V_CW + 3 * o + 3],
                                                       in1=cv[:, o, :], op0=ALU.mult, op1=ALU.add).then_inc(cv_ready, 1)
                if a == 6:
                    dve.wait_ge(xs_hi_ready, b * 2 + 2)
                    nc.vector.tensor_tensor(xs_lo[:, :, :], cv[:, :, :], xs_hi[:, :, :], ALU.subtract).then_inc(xs_lo_ready, 1)

            def c_stage(b, kind, n):
                half, j = UNITS[n]
                if kind == "cap":
                    dve.wait_ge(exp_ready, b * NU + n + 1)
                    nc.vector.tensor_scalar(delta[:, n % 2, :], delta[:, n % 2, :], EXP_CAP, None, ALU.min).then_inc(capped, 1)
                if kind == "da":
                    dve.wait_ge(ln_ready, b * NU + n + 1)
                    nc.vector.scalar_tensor_tensor(out=delta[:, n % 2, :], in0=banks[n % 2][:, :],
                                                   scalar=vec[:, V_DLB + j:V_DLB + j + 1], in1=delta[:, n % 2, :],
                                                   op0=ALU.add, op1=ALU.max).then_inc(delta_ready, 1)
                    dve.wait_ge(delta_ready, b * NU + n + 3)
                    dve.wait_ge(a_done, b * NU + n + 1)
                    nc.vector.scalar_tensor_tensor(out=decay[:, n % 2, :], in0=banks[2 + n % 2][:, :],
                                                   scalar=vec[:, V_AB + j:V_AB + j + 1], in1=delta[:, n % 2, :],
                                                   op0=ALU.add, op1=ALU.mult).then_inc(da_ready, 1)
                if kind == "scan":
                    dve.wait_ge(abar_ready, b * NU + n + 1)
                    first = half == 0
                    if 1 <= n < HC:
                        dve.wait_ge(carried, b * 2 * HC + 2 * n - 1)
                    if n == HC:
                        dve.wait_ge(carried, b * 2 * HC + 2 * HC)
                    nc.vector.tensor_tensor_scan(a_cum[:, :], decay[:, n % 2, :], zeros[:, 0:HALF],
                                                 1.0 if first else carry_a[:, j:j + 1], ALU.mult, ALU.add).then_inc(acum_ready, 1)
                    dve.wait_ge(acum_ready, b * NU + n + 1)
                    dve.wait_ge(b_done, b * NU + n + 1)
                    nc.vector.scalar_tensor_tensor(out=bx[:, :], in0=banks[4][:, :],
                                                   scalar=vec[:, V_BB + j:V_BB + j + 1], in1=a_cum[:, :],
                                                   op0=ALU.add, op1=ALU.mult).then_inc(bx_ready, 1)
                    dve.wait_ge(bx_ready, b * NU + n + 3)
                    dve.wait_ge(h_lo_ready, b * NU + n + 1)
                    nc.vector.tensor_tensor_scan(h[:, n % 2, :], ones[:, 0:HALF], bx[:, :],
                                                 0.0 if first else carry_h[:, j:j + 1], ALU.mult, ALU.add).then_inc(h_ready, 1)

            def d_stage(k, half, d):
                if d == 2:
                    dve.wait_ge(s_hi_ready, 2 * k + 2)
                    nc.vector.tensor_tensor(s_out_lo[:, :, :], s[:, :, :], s_out_hi[:, :, :], ALU.subtract).then_inc(s_lo_ready, 1)
                if d == 3:
                    dve.wait_ge(g_ready, 2 * k + 2)
                    nc.vector.tensor_tensor(g[:, :, :], s[:, :, :], g[:, :, :], ALU.mult).then_inc(z_ready, 1)
                if d == 4:
                    dve.wait_ge(z_hi_ready, k + 1)
                    nc.vector.tensor_tensor(z_lo[:, :, :], g[:, :, :], z_hi[:, :, :], ALU.subtract).then_inc(z_lo_ready, 1)
                out = lambda t: banks[6 + t // 2][:, (t % 2) * D:(t % 2 + 1) * D]
                if d == 5:
                    dve.wait_ge(w3_done, k * 4 + 8)
                    moments(out, st2, mv2, HT, d_order, k * 2 + 1, mv2_ready)
                if d == 6:
                    dve.wait_ge(rs2_ready, k + 1)
                    for t in range(HT):
                        i = nc.vector.tensor_scalar(y_n[:, t, :], out(t), mv2[:, t, 0:1], rs2[:, t:t + 1],
                                                    ALU.subtract, ALU.mult)
                    i.then_inc(yn_ready, 1)
                    dve.wait_ge(yn_ready, k + 2)
                    dve.wait_ge(xr_loaded, k * 16 + 16)
                    nc.vector.tensor_tensor(xr[:, :, :], xr[:, :, :], y_n[:, :, :], ALU.add).then_inc(x1_ready, 1)
                    dve.wait_ge(x1_ready, k + 1)
                    moments(lambda t: xr[:, t, :], st2[:, HT:, :], mv2[:, HT:, :], HT, d_order, k * 2 + 2, mv3_ready)
                if d == 7:
                    dve.wait_ge(rs4_ready, k + 1)
                    dve.wait_ge(n_stored, k * 16 + 16)
                    if not (isinstance(k, int) and k == 0):
                        dve.wait_ge(scattered, k * 16 * HT * K)
                    for t in range(HT):
                        i = nc.vector.tensor_scalar(n2[:, t, :], xr[:, t, :], mv2[:, HT + t, 0:1], rs4[:, t:t + 1],
                                                    ALU.subtract, ALU.mult)
                    i.then_inc(n2_ready, 1)
                if d in (8, 9):
                    c = d - 8
                    dve.wait_ge(xn_hi_ready, 2 * k + c + 1)
                    nc.vector.tensor_scalar(xn_f[:, c, :], banks[5][:, :], vec[:, V_G + c:V_G + c + 1],
                                            vec[:, V_BE + c:V_BE + c + 1], ALU.mult, ALU.add).then_inc(xn_f_ready, 1)
                    dve.wait_ge(xn_f_ready, 2 * k + c + 1)
                    nc.vector.tensor_tensor(xnt_lo[:, c, :], xn_f[:, c, :], xnt_hi[:, c, :],
                                            ALU.subtract).then_inc(xn_lo_ready, 1)
                tiles = bass.ds(k * HT, HT)
                def link(i, n):
                    i.then_inc(route_steps, 1)
                    dve.wait_ge(route_steps, k * LINKS + n + 2)
                def wide(v):
                    return v.unsqueeze(2).to_broadcast([P, HT, E])
                if d == 10:
                    l = banks[5][:, :].rearrange("p (t e) -> p t e", e=P)[:, :, 0:E]
                    dve.wait_ge(logits_done, k + 1)
                    link(nc.vector.tensor_reduce(top[:, :], l, AX.X, ALU.max), 0)
                    nc.vector.tensor_tensor(prob[:, :, :], l, wide(top[:, :]), ALU.subtract).then_inc(shifted, 1)
                if d == 11:
                    dve.wait_ge(probs_exp, k + 1)
                    link(nc.vector.tensor_reduce(total[:, :], prob[:, :, :], AX.X, ALU.add), 1)
                    link(nc.vector.reciprocal(total[:, :], total[:, :]), 2)
                    link(nc.vector.tensor_tensor(prob[:, :, :], prob[:, :, :], wide(total[:, :]), ALU.mult), 3)
                    for m in range(K):
                        v, pk = val[m][:, tiles], pick[m][:, tiles, :]
                        n = 4 + m * 6
                        link(nc.vector.tensor_reduce(v, prob[:, :, :], AX.X, ALU.max), n)
                        link(nc.vector.tensor_tensor(score[:, :, :], prob[:, :, :], wide(v), ALU.is_equal), n + 1)
                        link(nc.vector.tensor_tensor(score[:, :, :], score[:, :, :], desc[:, :, :], ALU.mult), n + 2)
                        link(nc.vector.tensor_reduce(best[:, :], score[:, :, :], AX.X, ALU.max), n + 3)
                        link(nc.vector.tensor_tensor(pk, score[:, :, :], wide(best[:, :]), ALU.is_equal), n + 4)
                        if m == 0:
                            link(nc.vector.scalar_tensor_tensor(out=prob[:, :, :], in0=pk, scalar=-2.0,
                                                                in1=prob[:, :, :], op0=ALU.mult, op1=ALU.add), n + 5)
                    link(nc.vector.tensor_tensor(both[:, :, :].rearrange("p e t -> p t e"), pick[0][:, tiles, :],
                                                 pick[1][:, tiles, :], ALU.add), 15)
                    nc.vector.tensor_tensor_scan(run_sum[:, :, :].rearrange("p e t -> p (e t)"), ones[:, 0:E * HT],
                                                 both[:, :, :].rearrange("p e t -> p (e t)"), 0.0, ALU.mult, ALU.add)
                    nc.vector.tensor_reduce(count[:, :], both[:, :, :], AX.X, ALU.add).then_inc(counted, 1)
                if d == 12:
                    dve.wait_ge(counts_done, k + 1)
                    link(nc.vector.tensor_tensor(offset[:, :], fill[:, :], banks[5][:, 0:E], ALU.add), 16)
                    nc.vector.tensor_tensor(fill[:, :], fill[:, :], banks[5][:, E:2 * E], ALU.add)
                    link(nc.vector.tensor_tensor(offset[:, :], offset[:, :], count[:, :], ALU.add), 17)
                    link(nc.vector.tensor_tensor(offset[:, :], offset[:, :], run_sum[:, :, HT - 1], ALU.subtract), 18)
                    link(nc.vector.tensor_tensor(run_sum[:, :, :], run_sum[:, :, :],
                                                 offset[:, :].unsqueeze(2).to_broadcast([P, E, HT]), ALU.add), 19)
                    for m in range(K):
                        link(nc.vector.tensor_tensor(score[:, :, :], pick[m][:, tiles, :],
                                                     run_sum[:, :, :].rearrange("p e t -> p t e"), ALU.mult), 20 + 2 * m)
                        link(nc.vector.tensor_reduce(slot_half[:, :, m:m + 1], score[:, :, :], AX.X, ALU.add), 21 + 2 * m)
                    nc.vector.tensor_copy(slot_now[:, :, :], slot_half[:, :, :]).then_inc(slots_ready, 1)
                    nc.vector.tensor_copy(slot_f[:, tiles, :], slot_half[:, :, :])

            for pad in (0, L + 1):
                nc.vector.memset(u[:, :, pad:pad + 1], 0.0)
            nc.vector.tensor_tensor(cdb[:, :], vec[:, V_CDB:V_CDB + DC], vec[:, V_CDB + DC:V_CDB + 2 * DC],
                                    ALU.add).then_inc(start_made, 1)
            for e in range(E):
                nc.vector.memset(desc[:, :, e:e + 1], float(E - e))
                i = nc.vector.memset(fill[:, e:e + 1], float(e * CAP - 1))
            i = nc.vector.memset(lt[:, :], 0.0)
            i.then_inc(start_made, 1)
            dve.wait_ge(start_made, 2)
            dve.sem_inc(slots_ready, 1)
            dve.sem_inc(yn_ready, 1)
            dve.sem_inc(route_steps, 1)
            dve.sem_inc(delta_ready, 2)
            dve.sem_inc(da_ready, 2)
            dve.sem_inc(bx_ready, 2)
            dve.sem_inc(cv_ready, 2)
            dve.sem_inc(n2_ready, 1)
            run(dve, "vector", a_stage, c_stage, d_stage)

        @block.gpsimd
        def _(pool):
            def chain(order, first, steps):
                for n, (out, x0, x1, op) in enumerate(steps):
                    i = nc.gpsimd.tensor_tensor(out, x0, x1, op)
                    if n < len(steps) - 1:
                        i.then_inc(order, 1)
                        pool.wait_ge(order, first + n + 1)
                return i

            def a_stage(b, a):
                if a == 0:
                    pool.wait_ge(mv_ready, b + 1)
                    chain(pool_a, b, [(ve[:, :], mv[:, :, 1], eps[:, 0:LT], ALU.add),
                                      (rs[:, :], ve[:, :], neg_half[:, 0:LT], ALU.pow)]).then_inc(rs_ready, 1)

            def c_stage(b, kind, n):
                if kind == "lo":
                    half, j = UNITS[n]
                    if half == 0:
                        pool.wait_ge(acum_ready, b * NU + n + 1)
                        nc.gpsimd.tensor_tensor(carry_a[:, j:j + 1], a_cum[:, HALF - 1:HALF], ones[:, 0:1],
                                                ALU.mult).then_inc(carried, 1)
                        pool.wait_ge(h_ready, b * NU + n + 1)
                        nc.gpsimd.tensor_tensor(carry_h[:, j:j + 1], h[:, n % 2, HALF - 1:HALF], ones[:, 0:1],
                                                ALU.mult).then_inc(carried, 1)
                    pool.wait_ge(h_hi_ready, b * NU + n + 1)
                    nc.gpsimd.tensor_tensor(HH[half][1][:, j, :], h[:, n % 2, :], HH[half][0][:, j, :],
                                            ALU.subtract).then_inc(h_lo_ready, 1)

            def d_stage(k, half, d):
                if d == 5:
                    pool.wait_ge(mv2_ready, k + 1)
                    chain(pool_d, k * 7, [(ve2[:, :], mv2[:, 0:HT, 1], eps[:, 0:HT], ALU.add),
                                          (rs2[:, :], ve2[:, :], neg_half[:, 0:HT], ALU.pow)]).then_inc(rs2_ready, 1)
                if d == 6:
                    var = mv2[:, HT:2 * HT, 1]
                    pool.wait_ge(mv3_ready, k + 1)
                    chain(pool_d, k * 7 + 1, [(ve3[:, :], var, eps[:, 0:HT], ALU.add),
                                              (rs3[:, :], ve3[:, :], neg_half[:, 0:HT], ALU.pow),
                                              (ve4[:, :], var, rs3[:, :], ALU.mult),
                                              (ve4[:, :], ve4[:, :], rs3[:, :], ALU.mult),
                                              (ve4[:, :], ve4[:, :], eps[:, 0:HT], ALU.add),
                                              (ve4[:, :], ve4[:, :], neg_half[:, 0:HT], ALU.pow),
                                              (rs4[:, :], ve4[:, :], rs3[:, :], ALU.mult)]).then_inc(rs4_ready, 1)

                if d >= 12:
                    t = d - 12
                    if t == 0:
                        pool.wait_ge(slots_ready, k + 2)
                        pool.sem_inc(pool_seen, 1)
                    for m in range(K):
                        nc.gpsimd.indirect_dma_start(
                            out=xs_dram, out_offset=bass.IndirectOffsetOnAxis(ap=slot_now[:, t, m:m + 1], axis=0),
                            in_=n2[:, t, :], in_offset=None).then_inc(scattered, 16)

            nc.gpsimd.memset(before[:, :], 1.0).then_inc(before_set, 1)
            pool.wait_ge(before_set, 1)
            nc.gpsimd.affine_select(out=before[:, :], in_=before[:, :], compare_op=ALU.is_gt, fill=0.0,
                                    base=0, pattern=[[1, P]], channel_multiplier=-1).then_inc(before_made, 1)
            pool.sem_inc(h_lo_ready, 2)
            pool.sem_inc(s_done, 2)
            pool.sem_inc(w3_done, 4)
            pool.sem_inc(x1_stored, 16)
            pool.sem_inc(n_stored, 16)
            run(pool, "gpsimd", a_stage, c_stage, d_stage)
            pool.wait_ge(scattered, 2 * B * 16 * HT * K)



G = 256
GT = G // P
NG = (T * K + E * (G - 1)) // G
CW = 4 * P + D
MAXG = T // G + 1
CAP = T + G
TC = 4
NC = TT // TC


def token_rows(dram):
    return dram.rearrange("b l d -> (b l) d").rearrange("(c t p) d -> c p t d", t=TC, p=P)


def plan(nc, shared, s_hi, s_lo, xs_dram, pick, val, slot_f, fill, slot, weight, group_expert, group_row, zeros, tables):
    with ExitStack() as ctx:
        def sb(name, shape, dt=F32):
            return ctx.enter_context(nc.sbuf_tensor(name, shape, dt))
        def sem(name):
            return ctx.enter_context(nc.semaphore(name))
        raw_s = sb("raw_s", [P, S_COLS])
        start_row, limits, group_no, number = tables
        end_row = sb("end_row", [P, E], I32)
        n_all = sb("n_all", [P, E])
        over = sb("over", [P, E, MAXG])
        groups = sb("groups", [P, E])
        group_end = sb("group_end", [P, E])
        shift = sb("shift", [P, E])
        n_one = sb("n_one", [P, E])
        total = sb("w_total", [P, TT])
        moved = sb("moved", [P, TT, E])
        step_f = sb("step_f", [P, TT])
        past = sb("past", [P, NG + 1, E])
        unused = sb("unused", [P, NG + 1])
        expert_f = sb("expert_f", [P, NG + 1])
        passed = sb("passed", [P, NG + 1])
        row_f = sb("row_f", [P, NG + 1])
        steps, ends_ready, ends_cleared = sem("plan_steps"), sem("ends_ready"), sem("ends_cleared")
        loaded = [sem(f"shared_loaded{i}") for i in range(len(shared))]
        s_hi_ready = sem("shared_hi")
        block = ctx.enter_context(nc.Block())

        @block.sync
        def _(sp):
            for n, (at, src, chunks) in enumerate(shared):
                sp.dma_start(raw_s[:, at:at + chunks * src.shape[1]].rearrange("p (c n) -> p c n", c=chunks),
                             src.rearrange("(c p) n -> p c n", p=P)).then_inc(loaded[n], 16)
            sp.wait_ge(ends_ready, 1)
            for e in range(E):
                row = sp.value_load(end_row[0:1, e:e + 1], min_val=e * CAP, max_val=e * CAP + T)
                sp.dma_start(xs_dram[bass.ds(row, G), :].rearrange("(p m) d -> p (m d)", p=P),
                             zeros[:, 0:GT * D]).then_inc(ends_cleared, 16)
            sp.wait_ge(ends_cleared, 16 * E)

        @block.scalar
        def _(act):
            for n, (at, src, chunks) in enumerate(shared):
                cols = slice(at, at + chunks * src.shape[1])
                act.wait_ge(loaded[n], 16)
                nc.scalar.activation(s_hi[:, cols], raw_s[:, cols], ACT.Copy).then_inc(s_hi_ready, 1)

        @block.gpsimd
        def _(pool):
            for n, (at, src, chunks) in enumerate(shared):
                cols = slice(at, at + chunks * src.shape[1])
                pool.wait_ge(s_hi_ready, n + 1)
                nc.gpsimd.tensor_tensor(s_lo[:, cols], raw_s[:, cols], s_hi[:, cols], ALU.subtract)

        @block.vector
        def _(dve):
            n = [0]
            def link(i):
                n[0] += 1
                i.then_inc(steps, 1)
                dve.wait_ge(steps, n[0])
            nc.vector.memset(n_one[:, :], 1.0)
            nc.vector.tensor_scalar(end_row[:, :], fill[:, :], 1.0, None, ALU.add).then_inc(ends_ready, 1)
            link(nc.vector.tensor_tensor(n_all[:, :], fill[:, :], start_row[:, :], ALU.subtract))
            link(nc.vector.tensor_tensor(over[:, :, :], n_all[:, :].unsqueeze(2).to_broadcast([P, E, MAXG]),
                                         limits[:, :, :], ALU.is_gt))
            link(nc.vector.tensor_reduce(groups[:, :], over[:, :, :], AX.X, ALU.add))
            link(nc.vector.tensor_tensor_scan(group_end[:, :], n_one[:, :], groups[:, :], 0.0, ALU.mult, ALU.add))
            link(nc.vector.tensor_tensor(past[:, :, :], group_no[:, :, :],
                                         group_end[:, :].unsqueeze(1).to_broadcast([P, NG + 1, E]), ALU.is_ge))
            link(nc.vector.tensor_reduce(expert_f[:, :], past[:, :, 0:E - 1], AX.X, ALU.add))
            nc.vector.tensor_copy(group_expert[:, :], expert_f[:, :])
            link(nc.vector.tensor_tensor(group_no[:, :, 0:E - 1], past[:, :, 0:E - 1],
                                         groups[:, 0:E - 1].unsqueeze(1).to_broadcast([P, NG + 1, E - 1]), ALU.mult))
            link(nc.vector.tensor_reduce(passed[:, :], group_no[:, :, 0:E - 1], AX.X, ALU.add))
            link(nc.vector.tensor_tensor(row_f[:, :], number[:, :], passed[:, :], ALU.subtract))
            link(nc.vector.tensor_tensor(unused[:, :], row_f[:, :], past[:, :, E - 1], ALU.mult))
            link(nc.vector.tensor_tensor(row_f[:, :], row_f[:, :], unused[:, :], ALU.subtract))
            link(nc.vector.tensor_scalar(row_f[:, :], row_f[:, :], float(G), None, ALU.mult))
            link(nc.vector.scalar_tensor_tensor(out=row_f[:, :], in0=expert_f[:, :], scalar=float(CAP), in1=row_f[:, :],
                                                op0=ALU.mult, op1=ALU.add))
            nc.vector.tensor_copy(group_row[:, :], row_f[:, :])
            link(nc.vector.tensor_tensor(shift[:, :], group_end[:, :], groups[:, :], ALU.subtract))
            link(nc.vector.scalar_tensor_tensor(out=shift[:, :], in0=shift[:, :], scalar=float(G), in1=start_row[:, :],
                                                op0=ALU.mult, op1=ALU.subtract))
            for k in range(K):
                link(nc.vector.tensor_tensor(moved[:, :, :], pick[k][:, :, :],
                                             shift[:, :].unsqueeze(1).to_broadcast([P, TT, E]), ALU.mult))
                link(nc.vector.tensor_reduce(step_f[:, :], moved[:, :, :], AX.X, ALU.add))
                link(nc.vector.tensor_tensor(slot_f[:, :, k], slot_f[:, :, k], step_f[:, :], ALU.add))
            nc.vector.tensor_copy(slot[:, :, :], slot_f[:, :, :])
            link(nc.vector.tensor_tensor(total[:, :], val[0][:, :], val[1][:, :], ALU.add))
            link(nc.vector.reciprocal(total[:, :], total[:, :]))
            for k in range(K):
                nc.vector.tensor_tensor(weight[:, :, k], val[k][:, :], total[:, :], ALU.mult)


def experts(nc, w_e, xs_dram, y_dram, group_expert, group_row, vec, ident):
    with ExitStack() as ctx:
        def sb(name, shape, dt=F32):
            return ctx.enter_context(nc.sbuf_tensor(name, shape, dt))

        def sem(name):
            return ctx.enter_context(nc.semaphore(name))

        RAW, RING, AHEAD, LAG = 4, FC, 4, 3
        raw = sb("raw", [P, RAW, CW])
        e_hi = sb("e_hi", [P, RING, CW], F32R)
        e_lo = sb("e_lo", [P, RING, CW], F32R)
        rows = sb("x_rows", [P, 2, GT, D])
        xg_hi = sb("xg_hi", [P, 2, DC, G], F32R)
        xg_lo = sb("xg_lo", [P, 2, DC, G], F32R)
        xg_f = sb("xg_f", [P, DC, G])
        gate = sb("gate", [P, 4, G])
        hg_hi = sb("hg_hi", [P, 4, G], F32R)
        hg_lo = sb("hg_lo", [P, 4, G], F32R)
        y = sb("y", [P, 2, GT, D])
        gu_ps = [ctx.enter_context(nc.psum_tensor(f"gu_ps{i}", [P, 2 * G], F32)) for i in range(2)]
        x_ps = ctx.enter_context(nc.psum_tensor("x_ps", [P, 512], F32))
        down_ps = [[ctx.enter_context(nc.psum_tensor(f"down_ps{par}{t}", [P, 512], F32)) for t in range(GT)]
                   for par in range(2)]
        loaded = [sem(f"chunk_loaded{i}") for i in range(RAW)]
        hi_ready, lo_ready, dn_lo_ready = sem("chunk_hi"), sem("chunk_lo"), sem("chunk_down_lo")
        rows_loaded = [sem(f"x_rows_loaded{i}") for i in range(2)]
        x_turned, x_hi_ready, x_f_ready, x_lo_ready = sem("x_turned"), sem("x_hi_ready"), sem("x_f_ready"), sem("x_lo_ready")
        gu_done, down_done = sem("e_gu_done"), sem("e_down_done")
        clipped, silu_ready, h_ready = sem("e_clipped"), sem("e_silu"), sem("e_h_ready")
        h_hi_ready, h_lo_ready, y_ready = sem("e_h_hi"), sem("e_h_lo"), sem("e_y_ready")
        y_stored = [sem(f"y_stored{i}") for i in range(2)]
        block = ctx.enter_context(nc.Block())

        def groups(eng, turn):
            turn(0, 0)
            with eng.Fori(0, (NG - 1) // 2) as i:
                for k in range(2):
                    turn(i * 2 + 1 + k, 1 - k)

        assert NG % 2 == 1

        @block.sync
        def _(sp):
            def load_rows(g, par):
                row = sp.value_load(group_row[0:1, bass.ds(g, 1)], min_val=0, max_val=E * CAP - G)
                sp.dma_start(rows[:, par, :, :], xs_dram[bass.ds(row, G), :].rearrange("(t p) d -> p t d", p=P)
                             ).then_inc(rows_loaded[par], 16)

            def load_chunk(g, f, e):
                sp.wait_ge(lo_ready, g * FC + f + 1)
                sp.wait_ge(dn_lo_ready, g * FC + f + 1)
                sp.dma_start(raw[:, f % RAW, :], w_e[e, f, :, :]).then_inc(loaded[f % RAW], 16)

            def store_y(g, par):
                sp.wait_ge(y_ready, g + 2 + 1)
                sp.dma_start(y_dram.rearrange("(g t p) d -> g p t d", t=GT, p=P)[g, :, :, :], y[:, par, :, :]
                             ).then_inc(y_stored[par], 16)

            def expert_of(g):
                return sp.value_load(group_expert[0:1, bass.ds(g, 1)], min_val=0, max_val=E - 1)

            def turn(g, par):
                e = expert_of(g)
                for f in range(FC):
                    load_chunk(g, f, e)
                    if f == 0:
                        if not (isinstance(g, int) and g == 0):
                            sp.wait_ge(x_turned, g * DC)
                        load_rows(g + 1, 1 - par)

            load_rows(0, 0)
            turn(0, 0)
            turn(1, 1)
            turn(2, 0)
            with sp.Fori(0, (NG - 3) // 2) as i:
                for k in range(2):
                    g = i * 2 + 3 + k
                    store_y(g - 3, 0 if k == 0 else 1)
                    turn(g, 1 - k)
            e = expert_of(NG)
            for f in range(AHEAD):
                load_chunk(NG, f, e)
            for g in range(NG - 3, NG):
                store_y(g, g % 2)
            sp.wait_ge(y_stored[0], 16 + 16 * ((NG + 1) // 2))
            sp.wait_ge(y_stored[1], 16 + 16 * (NG // 2))

        @block.tensor
        def _(pe):
            def turn_rows(g, par, c):
                if c == 0:
                    pe.wait_ge(rows_loaded[par], (g_half(g, par)) * 16 + 16)
                pe.wait_ge(x_f_ready, g * DC + c + 1)
                for t in range(GT):
                    i = nc.tensor.transpose(x_ps[:, t * P:(t + 1) * P], rows[:, par, t, c * P:(c + 1) * P], ident[:, :])
                i.then_inc(x_turned, 1)

            def gate_up(g, par, f):
                pe.wait_ge(lo_ready, g * FC + f + 1 + RAW)
                if f == 0:
                    pe.wait_ge(x_lo_ready, g * DC + DC)
                pe.wait_ge(h_ready, g * FC + f + 1)
                for m, at in enumerate((0, 2 * P)):
                    out = gu_ps[f % 2][:, m * G:(m + 1) * G]
                    for c in range(DC):
                        cols = slice(at + c * P, at + (c + 1) * P)
                        nc.tensor.matmul(out, e_hi[:, f, cols], xg_hi[:, par, c, :], start=c == 0, stop=False)
                        nc.tensor.matmul(out, e_hi[:, f, cols], xg_lo[:, par, c, :], start=False, stop=False)
                        i = nc.tensor.matmul(out, e_lo[:, f, cols], xg_hi[:, par, c, :], start=False, stop=c == DC - 1)
                i.then_inc(gu_done, 1)
            def down(g, par, f):
                pe.wait_ge(h_lo_ready, g * FC + f + 1)
                pe.wait_ge(dn_lo_ready, g * FC + f + 1 + RAW)
                if f == 0:
                    pe.wait_ge(y_ready, g + 1)
                for t in range(GT):
                    toks = slice(t * P, (t + 1) * P)
                    out = down_ps[par][t][:, 0:D]
                    nc.tensor.matmul(out, hg_hi[:, f % 4, toks], e_hi[:, f, 4 * P:CW], start=f == 0, stop=False)
                    nc.tensor.matmul(out, hg_hi[:, f % 4, toks], e_lo[:, f, 4 * P:CW], start=False, stop=False)
                    i = nc.tensor.matmul(out, hg_lo[:, f % 4, toks], e_hi[:, f, 4 * P:CW], start=False, stop=f == FC - 1)
                i.then_inc(down_done, 1)

            def turn(g, par):
                for f in range(FC):
                    gate_up(g, par, f)
                    if f >= LAG:
                        down(g, par, f - LAG)
                    elif not (isinstance(g, int) and g == 0):
                        down(g - 1, 1 - par, FC + f - LAG)
                    if f in (1, 4):
                        turn_rows(g + 1, 1 - par, (f - 1) // 3)

            for c in range(DC):
                turn_rows(0, 0, c)
            groups(pe, turn)
            for f in range(FC - LAG, FC):
                down(NG - 1, (NG - 1) % 2, f)

        @block.scalar
        def _(act):
            def split(g, f):
                act.wait_ge(loaded[f % RAW], (g * (FC // RAW) + f // RAW) * 16 + 16)
                act.wait_ge(down_done, g * FC + f + 1)
                nc.scalar.activation(e_hi[:, f, :], raw[:, f % RAW, :], ACT.Copy).then_inc(hi_ready, 1)

            def rows_hi(g, par, c):
                act.wait_ge(x_turned, g * DC + c + 1)
                nc.scalar.activation(xg_hi[:, par, c, :], x_ps[:, 0:G], ACT.Identity,
                                     bias=vec[:, V_BE + c:V_BE + c + 1],
                                     scale=vec[:, V_G + c:V_G + c + 1]).then_inc(x_hi_ready, 1)
                nc.scalar.activation(xg_f[:, c, :], x_ps[:, 0:G], ACT.Identity,
                                     bias=vec[:, V_BE + c:V_BE + c + 1],
                                     scale=vec[:, V_G + c:V_G + c + 1]).then_inc(x_f_ready, 1)

            def h_high(g, f):
                act.wait_ge(h_ready, g * FC + f + 1 + 2)
                nc.scalar.activation(hg_hi[:, f % 4, :], gate[:, f % 4, :], ACT.Copy).then_inc(h_hi_ready, 1)
            def turn(g, par):
                for f in range(FC):
                    if f >= 1:
                        h_high(g, f - 1)
                    elif not (isinstance(g, int) and g == 0):
                        h_high(g - 1, FC - 1)
                    act.wait_ge(clipped, g * FC + f + 1)
                    nc.scalar.activation(gate[:, f % 4, :], gate[:, f % 4, :], ACT.Silu).then_inc(silu_ready, 1)
                    ahead = f + AHEAD
                    split(g + ahead // FC, ahead % FC)
                    if f in (2, 5):
                        rows_hi(g + 1, 1 - par, (f - 2) // 3)
            act.sem_inc(down_done, FC)
            for c in range(DC):
                rows_hi(0, 0, c)
            for f in range(AHEAD):
                split(0, f)
            groups(act, turn)
            h_high(NG - 1, FC - 1)

        @block.vector
        def _(dve):
            def rows_lo(g, par, c):
                dve.wait_ge(x_f_ready, g * DC + c + 2)
                nc.vector.tensor_tensor(xg_lo[:, par, c, :], xg_f[:, c, :], xg_hi[:, par, c, :],
                                        ALU.subtract).then_inc(x_lo_ready, 1)

            def copy_y(g, par):
                dve.wait_ge(down_done, (g + 1) * FC + FC)
                dve.wait_ge(y_stored[par], (g_half(g, par)) * 16 + 16)
                for t in range(GT):
                    i = nc.vector.tensor_copy(y[:, par, t, :], down_ps[par][t][:, 0:D])
                i.then_inc(y_ready, 1)

            def split_down(g, f):
                dve.wait_ge(hi_ready, g * FC + f + 1)
                nc.vector.tensor_tensor(e_lo[:, f, 4 * P:CW], raw[:, f % RAW, 4 * P:CW], e_hi[:, f, 4 * P:CW],
                                        ALU.subtract).then_inc(dn_lo_ready, 1)
            def h_low(g, f):
                dve.wait_ge(h_hi_ready, g * FC + f + 1)
                nc.vector.tensor_tensor(hg_lo[:, f % 4, :], gate[:, f % 4, :], hg_hi[:, f % 4, :],
                                        ALU.subtract).then_inc(h_lo_ready, 1)
            def turn(g, par):
                for f in range(FC):
                    dve.wait_ge(gu_done, g * FC + f + 1)
                    nc.vector.tensor_scalar(gate[:, f % 4, :], gu_ps[f % 2][:, 0:G], CLIP, -CLIP,
                                            ALU.min, ALU.max).then_inc(clipped, 1)
                    if f >= 1:
                        h_low(g, f - 1)
                    elif not (isinstance(g, int) and g == 0):
                        h_low(g - 1, FC - 1)
                    dve.wait_ge(silu_ready, g * FC + f + 1)
                    nc.vector.tensor_tensor(gate[:, f % 4, :], gu_ps[f % 2][:, G:2 * G], gate[:, f % 4, :],
                                            ALU.mult).then_inc(h_ready, 1)
                    ahead = f + AHEAD
                    split_down(g + ahead // FC, ahead % FC)
                    if f == LAG and not (isinstance(g, int) and g == 0):
                        copy_y(g - 1, 1 - par)
                    if f in (3, 6):
                        rows_lo(g + 1, 1 - par, (f - 3) // 3)
            dve.sem_inc(x_f_ready, 1)
            dve.sem_inc(h_ready, 2)
            dve.sem_inc(y_ready, 2)
            for par in range(2):
                dve.sem_inc(y_stored[par], 16)
            for c in range(DC):
                rows_lo(0, 0, c)
            dve.sem_inc(dn_lo_ready, RAW)
            for f in range(AHEAD):
                split_down(0, f)
            groups(dve, turn)
            h_low(NG - 1, FC - 1)
            copy_y(NG - 1, 0)

        @block.gpsimd
        def _(pool):
            def split(g, f):
                pool.wait_ge(hi_ready, g * FC + f + 1)
                nc.gpsimd.tensor_tensor(e_lo[:, f, 0:4 * P], raw[:, f % RAW, 0:4 * P], e_hi[:, f, 0:4 * P],
                                        ALU.subtract).then_inc(lo_ready, 1)

            pool.sem_inc(lo_ready, RAW)
            for f in range(AHEAD):
                split(0, f)

            def turn(g, par):
                for f in range(FC):
                    ahead = f + AHEAD
                    split(g + ahead // FC, ahead % FC)

            groups(pool, turn)


def g_half(g, par):
    if isinstance(g, int):
        return g // 2
    return (g - par) // 2


def combine(nc, y_dram, n_dram, x1_dram, out, slot, weight, s_hi, s_lo, vec, ident, neg_half, eps):
    with ExitStack() as ctx:
        def sb(name, shape, dt=F32):
            return ctx.enter_context(nc.sbuf_tensor(name, shape, dt))
        def sem(name):
            return ctx.enter_context(nc.semaphore(name))
        x1 = sb("c_x1", [P, 2, TC, D])
        n_rows = sb("c_n", [P, 2, TC, D])
        ye = sb("c_ye", [P, 2, TC, K, D])
        acc = sb("c_acc", [P, 2, TC, D])
        nt_hi = sb("nt_hi", [P, DC, HALF], F32R)
        nt_lo = sb("nt_lo", [P, DC, HALF], F32R)
        nt_f = sb("nt_f", [P, DC, HALF])
        gate = sb("c_gate", [P, SC, HALF])
        hid_hi = sb("hid_hi", [P, SC, HALF], F32R)
        hid_lo = sb("hid_lo", [P, SC, HALF], F32R)
        st = sb("c_st", [P, TC, 6])
        mv = sb("c_mv", [P, 2, TC, 2])
        ve = sb("c_ve", [P, 2, TC])
        rs = sb("c_rs", [P, 2, TC])
        nt_ps, gate_ps, up_ps, down_ps = ([ctx.enter_context(nc.psum_tensor(f"{name}{i}", [P, HALF], F32)) for i in range(2)]
                                          for name in ("nt_ps", "c_gate_ps", "c_up_ps", "c_down_ps"))
        x1_loaded = [sem(f"c_x1_loaded{i}") for i in range(2)]
        n_loaded = [sem(f"c_n_loaded{i}") for i in range(2)]
        gathered = [sem(f"gathered{i}") for i in range(2)]
        stored = [sem(f"out_stored{i}") for i in range(2)]
        nt_done, nt_hi_ready, nt_f_ready, nt_lo_ready = sem("nt_done"), sem("nt_hi_ready"), sem("nt_f_ready"), sem("nt_lo_ready")
        gate_done, up_done, down_done = sem("c_gate_done"), sem("c_up_done"), sem("c_down_done")
        clipped, silu_ready, hid_ready = sem("c_clipped"), sem("c_silu"), sem("c_hid_ready")
        hid_hi_ready, hid_lo_ready = sem("c_hid_hi"), sem("c_hid_lo")
        mixed, mixed_one, order, seen = sem("c_mixed"), sem("c_mixed_one"), sem("c_order"), sem("c_seen")
        moments_ready, rs_ready, ve_ready = sem("c_moments"), sem("c_rs_ready"), sem("c_ve_ready")
        normed, out_ready = sem("c_normed"), sem("c_out_ready")
        block = ctx.enter_context(nc.Block())

        def steps(eng, turn):
            for c in range(2):
                turn(c, c, 2)
            with eng.Fori(1, NC // 2 - 1) as i:
                for par in range(2):
                    turn(i * 2 + par, par, 2)
            for par in range(2):
                turn(NC - 2 + par, par, 1 - par)
        assert NC % 2 == 0

        @block.sync
        def _(sp):
            def load_n(c, par):
                sp.dma_start(n_rows[:, par, :, :], token_rows(n_dram)[c, :, :, :]).then_inc(n_loaded[par], 16)
            def load_x1(c, par):
                sp.dma_start(x1[:, par, :, :], token_rows(x1_dram)[c, :, :, :]).then_inc(x1_loaded[par], 16)
            def store(c, par):
                sp.wait_ge(out_ready, c + 3)
                sp.dma_start(token_rows(out)[c, :, :, :], x1[:, par, :, :]).then_inc(stored[par], 16)
            for par in range(2):
                load_n(par, par)
                load_x1(par, par)
            def n_next(c, par):
                sp.wait_ge(nt_done, c * DC + DC)
                load_n(c + 2, par)
            def x1_next(c, par):
                sp.wait_ge(stored[par], g_half(c, par) * 16 + 16)
                load_x1(c + 2, par)
            n_next(0, 0)
            n_next(1, 1)
            store(0, 0)
            with sp.Fori(0, (NC - 4) // 2) as i:
                for k in range(2):
                    c = i * 2 + 1 + k
                    n_next(c + 1, k)
                    x1_next(c - 1, k)
                    store(c, 1 - k)
            for c in range(NC - 3, NC):
                if c < NC - 1:
                    x1_next(c - 1, (c - 1) % 2)
                store(c, c % 2)
            for par in range(2):
                sp.wait_ge(stored[par], 16 * (NC // 2))

        @block.gpsimd
        def _(pool):
            def roots(c):
                pool.wait_ge(moments_ready, c + 1)
                if c >= 2:
                    pool.wait_ge(normed, c - 1)
                nc.gpsimd.tensor_tensor(ve[:, c % 2, :], mv[:, c % 2, :, 1], eps[:, 0:TC], ALU.add).then_inc(ve_ready, 1)
                pool.wait_ge(ve_ready, c + 1)
                nc.gpsimd.tensor_tensor(rs[:, c % 2, :], ve[:, c % 2, :], neg_half[:, 0:TC], ALU.pow).then_inc(rs_ready, 1)
            for c in range(NC):
                if c >= 2:
                    pool.wait_ge(mixed, c - 1)
                for t in range(TC):
                    for k in range(K):
                        nc.gpsimd.indirect_dma_start(
                            out=ye[:, c % 2, t, k, :], out_offset=None, in_=y_dram,
                            in_offset=bass.IndirectOffsetOnAxis(ap=slot[:, c * TC + t, k:k + 1], axis=0)
                        ).then_inc(gathered[c % 2], 16)
                if c >= 1:
                    roots(c - 1)
            roots(NC - 1)

        @block.tensor
        def _(pe):
            def turned(c, par):
                pe.wait_ge(n_loaded[par], g_half(c, par) * 16 + 16)
                pe.wait_ge(nt_hi_ready, c * DC + DC)
                pe.wait_ge(nt_f_ready, c * DC + DC)
                for f in range(DC):
                    for t in range(TC):
                        i = nc.tensor.transpose(nt_ps[f][:, t * P:(t + 1) * P], n_rows[:, par, t, f * P:(f + 1) * P],
                                                ident[:, :])
                    i.then_inc(nt_done, 1)
            def gate_up(c):
                pe.wait_ge(nt_lo_ready, c + 1)
                pe.wait_ge(hid_ready, c * SC + SC)
                for f in range(SC):
                    for ps, at, done in ((gate_ps, 0, gate_done), (up_ps, FS, up_done)):
                        for m in range(DC):
                            cols = slice(SGU_AT + m * 2 * FS + at + f * P, SGU_AT + m * 2 * FS + at + (f + 1) * P)
                            nc.tensor.matmul(ps[f][:, :], s_hi[:, cols], nt_hi[:, m, :], start=m == 0, stop=False)
                            nc.tensor.matmul(ps[f][:, :], s_hi[:, cols], nt_lo[:, m, :], start=False, stop=False)
                            i = nc.tensor.matmul(ps[f][:, :], s_lo[:, cols], nt_hi[:, m, :], start=False, stop=m == DC - 1)
                        i.then_inc(done, 1)
            def down(c):
                pe.wait_ge(mixed_one, c + 1)
                pe.wait_ge(hid_lo_ready, c + 1)
                for t in range(TC):
                    toks = slice(t * P, (t + 1) * P)
                    out_ps = down_ps[t // 2][:, (t % 2) * D:(t % 2 + 1) * D]
                    for f in range(SC):
                        cols = slice(SDN_AT + f * D, SDN_AT + (f + 1) * D)
                        nc.tensor.matmul(out_ps, hid_hi[:, f, toks], s_hi[:, cols], start=f == 0, stop=False)
                        nc.tensor.matmul(out_ps, hid_hi[:, f, toks], s_lo[:, cols], start=False, stop=False)
                        i = nc.tensor.matmul(out_ps, hid_lo[:, f, toks], s_hi[:, cols], start=False, stop=f == SC - 1)
                i.then_inc(down_done, 1)
            def turn(c, par, later):
                if later >= 2:
                    turned(c + 2, par)
                    gate_up(c + 2)
                if later >= 1:
                    down(c + 1)
            for c in range(2):
                turned(c, c)
                gate_up(c)
            down(0)
            steps(pe, turn)

        @block.scalar
        def _(act):
            def turned(c):
                for f in range(DC):
                    act.wait_ge(nt_done, c * DC + f + 1)
                    if f == 0:
                        act.wait_ge(up_done, c * SC + SC)
                    b, g = vec[:, V_BE + f:V_BE + f + 1], vec[:, V_G + f:V_G + f + 1]
                    nc.scalar.activation(nt_hi[:, f, :], nt_ps[f][:, :], ACT.Identity, bias=b, scale=g).then_inc(nt_hi_ready, 1)
                    nc.scalar.activation(nt_f[:, f, :], nt_ps[f][:, :], ACT.Identity, bias=b, scale=g).then_inc(nt_f_ready, 1)
            def hidden(c):
                for f in range(SC):
                    act.wait_ge(clipped, c * SC + f + 1)
                    nc.scalar.activation(gate[:, f, :], gate[:, f, :], ACT.Silu).then_inc(silu_ready, 1)
            def hidden_high(c):
                act.wait_ge(down_done, c + 1)
                act.wait_ge(hid_ready, c * SC + SC + SC)
                nc.scalar.activation(hid_hi[:, :, :], gate[:, :, :], ACT.Copy).then_inc(hid_hi_ready, 1)
            def turn(c, par, later):
                if later >= 1:
                    hidden(c + 1)
                if later >= 2:
                    turned(c + 2)
                if later >= 1:
                    hidden_high(c + 1)
            act.sem_inc(nt_hi_ready, DC)
            act.sem_inc(nt_f_ready, DC)
            turned(0)
            hidden(0)
            turned(1)
            hidden_high(0)
            steps(act, turn)

        @block.vector
        def _(dve):
            def nt_low(c):
                dve.wait_ge(nt_f_ready, c * DC + 2 * DC)
                nc.vector.tensor_tensor(nt_lo[:, :, :], nt_f[:, :, :], nt_hi[:, :, :], ALU.subtract).then_inc(nt_lo_ready, 1)
            def clip(c, f):
                dve.wait_ge(gate_done, c * SC + f + 1)
                if f == 0 and not (isinstance(c, int) and c == 0):
                    dve.wait_ge(hid_lo_ready, c)
                nc.vector.tensor_scalar(gate[:, f, :], gate_ps[f][:, :], CLIP, -CLIP, ALU.min, ALU.max).then_inc(clipped, 1)
            def times_up(c, f):
                dve.wait_ge(silu_ready, c * SC + f + 1)
                dve.wait_ge(up_done, c * SC + f + 1 + SC)
                nc.vector.tensor_tensor(gate[:, f, :], up_ps[f][:, :], gate[:, f, :], ALU.mult).then_inc(hid_ready, 1)
            def hid_low(c):
                dve.wait_ge(hid_hi_ready, c + 1)
                nc.vector.tensor_tensor(hid_lo[:, :, :], gate[:, :, :], hid_hi[:, :, :], ALU.subtract).then_inc(hid_lo_ready, 1)
            def mix(c, par, m):
                if m == 0:
                    dve.wait_ge(out_ready, c + 1)
                    dve.wait_ge(down_done, c + 2)
                    dve.wait_ge(gathered[par], g_half(c, par) * 16 * TC * K + 16 * TC * K)
                for t in range(TC):
                    before = down_ps[t // 2][:, (t % 2) * D:(t % 2 + 1) * D] if m == 0 else acc[:, par, t, :]
                    j = nc.vector.scalar_tensor_tensor(out=acc[:, par, t, :], in0=ye[:, par, t, m, :],
                                                       scalar=weight[:, bass.ds(c * TC + t, 1), m:m + 1].rearrange("p t k -> p (t k)"),
                                                       in1=before, op0=ALU.mult, op1=ALU.add)
                j.then_inc(mixed_one if m == 0 else mixed, 1)
            def stats(c, par):
                dve.wait_ge(mixed, c + 1)
                for t in range(TC):
                    j = nc.vector.bn_stats(st[:, t, :], acc[:, par, t, :])
                j.then_inc(order, 1)
                dve.wait_ge(order, c + 1)
                dve.sem_inc(seen, 1)
                for t in range(TC):
                    j = nc.vector.bn_aggr(mv[:, par, t, :], st[:, t, :])
                j.then_inc(moments_ready, 1)
            def norm(c, par):
                dve.wait_ge(rs_ready, c + 1)
                for t in range(TC):
                    j = nc.vector.tensor_scalar(acc[:, par, t, :], acc[:, par, t, :], mv[:, par, t, 0:1], rs[:, par, t:t + 1],
                                                ALU.subtract, ALU.mult)
                j.then_inc(normed, 1)
            def finish(c, par):
                dve.wait_ge(normed, c + 1)
                dve.wait_ge(x1_loaded[par], g_half(c, par) * 16 + 16)
                nc.vector.tensor_tensor(x1[:, par, :, :], x1[:, par, :, :], acc[:, par, :, :], ALU.add).then_inc(out_ready, 1)
            def turn(c, par, later):
                first = isinstance(c, int) and c == 0
                if later >= 1:
                    clip(c + 1, 0)
                    clip(c + 1, 1)
                if not first:
                    norm(c - 1, 1 - par)
                    finish(c - 1, 1 - par)
                if later >= 1:
                    times_up(c + 1, 0)
                    times_up(c + 1, 1)
                if later >= 2:
                    nt_low(c + 2)
                if later >= 1:
                    hid_low(c + 1)
                mix(c, par, 0)
                dve.wait_ge(mixed_one, c + 2)
                mix(c, par, 1)
                stats(c, par)

            dve.sem_inc(mixed_one, 1)
            dve.sem_inc(out_ready, 2)
            dve.sem_inc(hid_ready, SC)
            dve.sem_inc(up_done, SC)
            dve.sem_inc(down_done, 1)
            nt_low(0)
            clip(0, 0)
            clip(0, 1)
            times_up(0, 0)
            times_up(0, 1)
            nt_low(1)
            hid_low(0)
            steps(dve, turn)
            norm(NC - 1, 1)
            finish(NC - 1, 1)


def program(nc, d, out):
    scratch = lambda name, shape: nc.dram_tensor(name, shape, F32, kind="Internal").ap()
    x1_dram = scratch("x1_scratch", (B, L, D))
    n_dram = scratch("n_scratch", (B, L, D))
    xs_dram = scratch("xs_scratch", (E * CAP, D))
    y_dram = scratch("y_scratch", (NG * G, D))
    with ExitStack() as ctx:
        def sb(name, shape, dt=F32):
            return ctx.enter_context(nc.sbuf_tensor(name, shape, dt))

        vec = sb("vec", [P, V_COLS])
        slot = sb("slot", [P, TT, K], I32)
        weight = sb("weight", [P, TT, K])
        group_expert = sb("group_expert", [P, NG + 1], I32)
        group_row = sb("group_row", [P, NG + 1], I32)
        zeros = sb("zeros", [P, GT * D])
        pick = [sb(f"pick{k}", [P, TT, E]) for k in range(K)]
        val = [sb(f"val{k}", [P, TT]) for k in range(K)]
        tables = [sb("start_row", [P, E]), sb("limits", [P, E, MAXG]), sb("group_no", [P, NG + 1, E]), sb("number", [P, NG + 1])]
        slot_f, fill = sb("slot_f", [P, TT, K]), sb("fill", [P, E])
        ident = sb("ident", [P, P])
        neg_half = sb("neg_half", [P, LT])
        eps = sb("eps", [P, LT])
        with ExitStack() as first:
            def sb1(name, shape, dt=F32):
                return first.enter_context(nc.sbuf_tensor(name, shape, dt))

            w_hi, w_lo = sb1("w_hi", [P, W_COLS], F32R), sb1("w_lo", [P, W_COLS], F32R)
            ident_r = sb1("ident_r", [P, P], F32R)
            ones = sb1("ones", [P, HALF])
            split_weights(nc, [(W1_AT, d["w1_t"], DC), (DL_AT, d["dl_w_t"], DC), (A_AT, d["A_w_t"], DC),
                               (B_AT, d["B_w_t"], DC), (C_AT, d["C_w_t"], HC), (DD_AT, d["D_w_t"], DC),
                               (W2_AT, d["w2_t"], DC), (W3_AT, d["w3_t"], DC), (RT_AT, d["router"], DC)],
                          d["vecs"], w_hi, w_lo, vec, ident, ident_r, zeros, ones, neg_half, eps, tables)
            mixer(nc, d["x"], xs_dram, x1_dram, n_dram, pick, val, slot_f, fill, w_hi, w_lo, vec, ident, ident_r,
                  zeros, ones, neg_half, eps)
        s_hi, s_lo = sb("s_hi", [P, S_COLS], F32R), sb("s_lo", [P, S_COLS], F32R)
        plan(nc, [(SGU_AT, d["sgu"], DC), (SDN_AT, d["sdn"], SC)], s_hi, s_lo, xs_dram, pick, val, slot_f, fill,
             slot, weight, group_expert, group_row, zeros, tables)
        experts(nc, d["w_e"], xs_dram, y_dram, group_expert, group_row, vec, ident)
        combine(nc, y_dram, n_dram, x1_dram, out, slot, weight, s_hi, s_lo, vec, ident, neg_half, eps)

def kernel(**inputs):
    import numpy as np
    import concourse.bacc as bacc
    from concourse.bass_utils import run_bass_kernel_spmd as run

    a = {k.replace("L0_attn_", "").replace("L0_ffn_", "f_"): np.asarray(v) for k, v in inputs.items()}
    cols = lambda v: v.reshape(-1, P).T
    vecs = np.concatenate([a["conv_w"].reshape(DC, P, 3).transpose(1, 0, 2).reshape(P, DC * 3)] +
                          [cols(a[k]) for k in ("conv_b", "A_b", "B_b", "dl_b", "C_b", "D_b", "f_ln_gamma", "f_ln_beta")], axis=1)
    arrays = {"x": a["x"], "vecs": vecs, "sgu": a["f_shared_gate_up_w"], "sdn": a["f_shared_down_w"],
              "router": a["f_router_w"]}
    gu = a["f_gate_up_w"].reshape(E, DC, P, 2, FC, P).transpose(0, 4, 2, 3, 1, 5).reshape(E, FC, P, 4 * P)
    arrays["w_e"] = np.concatenate([gu, a["f_down_w"].reshape(E, FC, P, D)], axis=3)
    for k in ("w1", "w2", "w3", "A_w", "B_w", "C_w", "D_w", "dl_w"):
        arrays[k + "_t"] = a[k].T
    arrays = {k: np.ascontiguousarray(v) for k, v in arrays.items()}
    nc = bacc.Bacc("TRN2", target_bir_lowering=False, num_devices=1)
    d = {k: nc.dram_tensor(k, v.shape, mybir.dt.from_np(v.dtype), kind="ExternalInput").ap() for k, v in arrays.items()}
    out = nc.dram_tensor("out", (B, L, D), F32, kind="ExternalOutput").ap()
    program(nc, d, out)
    return run(nc, [arrays], core_ids=[0]).results[0]["out"]
```
